# Optimizing a Trainium2 kernel written in Bass

```python
import numpy as np
import jax
import jax.numpy as jnp

def _softmax(x, axis=-1):
    return jax.nn.softmax(x, axis=axis)

def _gelu(x):
    return jax.nn.gelu(x, approximate=True)

def _silu(x):
    return jax.nn.silu(x)

def _sigmoid(x):
    return jax.nn.sigmoid(x)

def _layernorm(x, axis=-1, eps=1e-05):
    m = jnp.mean(x, axis=axis, keepdims=True)
    v = jnp.var(x, axis=axis, keepdims=True)
    return (x - m) / jnp.sqrt(v + eps)

def _scatter_add(tgt, idx, src, axis=0):
    return tgt.at[idx].add(src)

def _segment_sum(src, seg, n):
    return jax.ops.segment_sum(src, seg, n)
kernel_name = 'mk_macaron_d1_jaxref_r8_6a0c5b'

def setup_inputs(seed: int=0):
    np.random.seed(seed)
    _w = jnp.asarray

    def _L0_attn_setup():
        import jax, jax.numpy as jnp
        import numpy as np
        D_MODEL = 128
        NUM_HEADS = 16
        HEAD_DIM = D_MODEL // NUM_HEADS
        key = jax.random.key(seed)
        ks = jax.random.split(key, 9)
        B, S = (2, 256)
        s = 1.0 / np.sqrt(D_MODEL)
        return {'x': jax.random.normal(ks[0], (B, S, D_MODEL), dtype=jnp.float32), 'Wq': jax.random.normal(ks[1], (D_MODEL, D_MODEL), dtype=jnp.float32) * s, 'bq': jnp.zeros((D_MODEL,), dtype=jnp.float32), 'Wk': jax.random.normal(ks[2], (D_MODEL, D_MODEL), dtype=jnp.float32) * s, 'bk': jnp.zeros((D_MODEL,), dtype=jnp.float32), 'Wv': jax.random.normal(ks[3], (D_MODEL, D_MODEL), dtype=jnp.float32) * s, 'bv': jnp.zeros((D_MODEL,), dtype=jnp.float32), 'Wo': jax.random.normal(ks[4], (D_MODEL, D_MODEL), dtype=jnp.float32) * s, 'bo': jnp.zeros((D_MODEL,), dtype=jnp.float32)}
    _L0_attn_in = _L0_attn_setup()

    def _L0_ffn_setup():
        import jax, jax.numpy as jnp
        import numpy as np
        D_MODEL, D_FF, N_EXPERTS, TOP_K = (128, 512, 8, 2)
        BATCH, SEQ = (2, 256)
        key = jax.random.key(seed)
        ks = jax.random.split(key, 10)
        s = 0.02
        return {'x': jax.random.normal(ks[0], (BATCH, SEQ, D_MODEL), jnp.float32), 'Wg': jax.random.normal(ks[1], (D_MODEL, N_EXPERTS), jnp.float32) * s, 'W1': jax.random.normal(ks[2], (N_EXPERTS, D_MODEL, D_FF), jnp.float32) * s, 'b1': jnp.zeros((N_EXPERTS, D_FF), jnp.float32), 'W2': jax.random.normal(ks[3], (N_EXPERTS, D_FF, D_MODEL), jnp.float32) * s, 'b2': jnp.zeros((N_EXPERTS, D_MODEL), jnp.float32), 'Ws1': jax.random.normal(ks[4], (D_MODEL, D_FF), jnp.float32) * s, 'bs1': jnp.zeros((D_FF,), jnp.float32), 'Ws2': jax.random.normal(ks[5], (D_FF, D_MODEL), jnp.float32) * s, 'bs2': jnp.zeros((D_MODEL,), jnp.float32)}
    _L0_ffn_in = _L0_ffn_setup()
    _d = {'L0_attn_x': _L0_attn_in['x'], 'L0_attn_Wq': _L0_attn_in['Wq'], 'L0_attn_bq': _L0_attn_in['bq'], 'L0_attn_Wk': _L0_attn_in['Wk'], 'L0_attn_bk': _L0_attn_in['bk'], 'L0_attn_Wv': _L0_attn_in['Wv'], 'L0_attn_bv': _L0_attn_in['bv'], 'L0_attn_Wo': _L0_attn_in['Wo'], 'L0_attn_bo': _L0_attn_in['bo'], 'L0_ffn_Wg': _L0_ffn_in['Wg'], 'L0_ffn_W1': _L0_ffn_in['W1'], 'L0_ffn_b1': _L0_ffn_in['b1'], 'L0_ffn_W2': _L0_ffn_in['W2'], 'L0_ffn_b2': _L0_ffn_in['b2'], 'L0_ffn_Ws1': _L0_ffn_in['Ws1'], 'L0_ffn_bs1': _L0_ffn_in['bs1'], 'L0_ffn_Ws2': _L0_ffn_in['Ws2'], 'L0_ffn_bs2': _L0_ffn_in['bs2']}
    _x0 = _d['L0_attn_x']
    _d['L0_attn_x'] = jax.random.normal(jax.random.fold_in(jax.random.key(seed), 1), (8, 512, 128), dtype=_x0.dtype)
    del _x0
    return _d

def reference(L0_attn_x, L0_attn_Wq, L0_attn_bq, L0_attn_Wk, L0_attn_bk, L0_attn_Wv, L0_attn_bv, L0_attn_Wo, L0_attn_bo, L0_ffn_Wg, L0_ffn_W1, L0_ffn_b1, L0_ffn_W2, L0_ffn_b2, L0_ffn_Ws1, L0_ffn_bs1, L0_ffn_Ws2, L0_ffn_bs2):

    def _L0_attn_ref(x, Wq, bq, Wk, bk, Wv, bv, Wo, bo):
        import jax, jax.numpy as jnp
        import numpy as np
        D_MODEL = 128
        NUM_HEADS = 16
        HEAD_DIM = D_MODEL // NUM_HEADS
        B, S, _ = x.shape

        def heads(y):
            return y.reshape(B, S, NUM_HEADS, HEAD_DIM).transpose(0, 2, 1, 3)
        Q = heads(x @ Wq + bq)
        K = heads(x @ Wk + bk)
        V = heads(x @ Wv + bv)
        scale = 1.0 / np.sqrt(HEAD_DIM).astype(np.float32)
        scores = jnp.einsum('bhqd,bhkd->bhqk', Q, K) * scale
        attn = jax.nn.softmax(scores, axis=-1)
        ctx = jnp.einsum('bhqk,bhkd->bhqd', attn, V)
        ctx = ctx.transpose(0, 2, 1, 3).reshape(B, S, D_MODEL)
        return ctx @ Wo + bo

    def _L0_ffn_ref(x, Wg, W1, b1, W2, b2, Ws1, bs1, Ws2, bs2):
        import jax, jax.numpy as jnp
        import numpy as np
        D_MODEL, D_FF, N_EXPERTS, TOP_K = (128, 512, 8, 2)
        BATCH, SEQ = (2, 256)
        B, S, D = x.shape
        xf = x.reshape(B * S, D)
        T = B * S
        logits = xf @ Wg
        top_vals, top_idx = jax.lax.top_k(logits, TOP_K)
        top_w = jax.nn.softmax(top_vals, axis=-1)
        combine = jnp.zeros((T, N_EXPERTS), x.dtype).at[jnp.arange(T)[:, None], top_idx].add(top_w)
        h = jax.nn.relu(jnp.einsum('td,edf->tef', xf, W1) + b1)
        sparse = jnp.einsum('te,tef,efd->td', combine, h, W2)
        sparse = sparse + combine @ b2
        shared = jax.nn.relu(xf @ Ws1 + bs1) @ Ws2 + bs2
        out = sparse + shared
        return out.reshape(B, S, D)
    x = L0_attn_x
    x = x + 0.5 * _L0_ffn_ref(_layernorm(x, axis=-1), L0_ffn_Wg, L0_ffn_W1, L0_ffn_b1, L0_ffn_W2, L0_ffn_b2, L0_ffn_Ws1, L0_ffn_bs1, L0_ffn_Ws2, L0_ffn_bs2)
    x = x + _L0_attn_ref(_layernorm(x, axis=-1), L0_attn_Wq, L0_attn_bq, L0_attn_Wk, L0_attn_bk, L0_attn_Wv, L0_attn_bv, L0_attn_Wo, L0_attn_bo)
    x = x + 0.5 * _L0_ffn_ref(_layernorm(x, axis=-1), L0_ffn_Wg, L0_ffn_W1, L0_ffn_b1, L0_ffn_W2, L0_ffn_b2, L0_ffn_Ws1, L0_ffn_bs1, L0_ffn_Ws2, L0_ffn_bs2)
    return x

_drawn_inputs = setup_inputs


def setup_inputs(seed=0):
    import zlib

    import numpy as np

    out = dict(_drawn_inputs(seed))
    spreads = {'L0_attn_bq': (0.0, 0.724),
     'L0_attn_bk': (0.0, 0.8),
     'L0_attn_bv': (0.0, 0.1),
     'L0_attn_bo': (0.0, 0.1),
     'L0_ffn_b1': (0.0, 0.38),
     'L0_ffn_b2': (0.0, 0.1),
     'L0_ffn_bs1': (0.0, 0.281),
     'L0_ffn_bs2': (0.0, 0.1)}
    factors = {}
    for name, (base, spread) in spreads.items():
        noise = np.random.default_rng([zlib.crc32(name.encode()), seed]).standard_normal(out[name].shape)
        drawn = base * np.exp(spread * noise) if base else spread * noise
        out[name] = jnp.asarray(drawn.astype(out[name].dtype))
    for name, factor in factors.items():
        out[name] = (out[name] * factor).astype(out[name].dtype)
    return out
```

```python
from contextlib import ExitStack

import concourse.bass as bass
from concourse import mybir

F32 = mybir.dt.float32
F32R = mybir.dt.float32r
BF16 = mybir.dt.bfloat16
U32 = mybir.dt.uint32
I32 = mybir.dt.int32
ALU = mybir.AluOpType
ACT = mybir.ActivationFunctionType
AX = mybir.AxisListType

P = 128


def wait(eng, sem, value):
    if not isinstance(value, int) or value > 0:
        eng.wait_ge(sem, value)


def exists(k, count):
    return not isinstance(k, int) or 0 <= k < count


def steps(eng, first, last, loop_from, loop_to, body):
    for k in range(first, loop_from):
        body(k, k % 2, k // 2)
    if loop_to > loop_from:
        with eng.Fori(loop_from // 2, loop_to // 2) as i:
            for par in range(2):
                body(i * 2 + par, par, i)
    for k in range(loop_to, last):
        body(k, k % 2, k // 2)


def macaron(nc, x_in, Wq, bq, Wk, bk, Wv, bv, Wo, bo, Wg, W1, b1, W2, b2, Ws1, bs1, Ws2, bs2, out):
    BATCH, SEQ, D = x_in.shape
    E, _, F = W1.shape
    H = 16
    HD = D // H
    SCALE = 1.0 / float(HD) ** 0.5
    TOP = 2
    T = BATCH * SEQ
    NT = T // P
    QT = SEQ // P
    BLK = 512
    SUB = BLK // P
    FC = F // P
    NSH = T // BLK
    NEX = TOP * T // BLK + E
    SLOTS = NEX * BLK
    LOGBLK = BLK.bit_length() - 1
    G = 4
    R = H // G
    RP = P // R
    assert D == P and SEQ == BLK and E == 8 and G * R == H

    x_rows = x_in.rearrange("b s d -> (b s) d")
    out_rows = out.rearrange("b s d -> (b s) d")

    xs = nc.dram_tensor("sorted_rows", (SLOTS, D), F32, kind="Internal").ap()
    ys = nc.dram_tensor("expert_rows", (SLOTS, D), F32, kind="Internal").ap()
    HK = 3 * HD
    q_dram, k_dram = [[nc.dram_tensor(f"{n}_stacks_{par}", (H, HK, SEQ), F32, kind="Internal").ap()
                       for par in range(2)] for n in ("q", "k")]
    zero_dram = nc.dram_tensor("zeros", (P - R * HK, SEQ), F32, kind="Internal").ap()
    nmax_dram = [nc.dram_tensor(f"neg_max_{g}", (R * 2, QT * P), F32, kind="Internal").ap() for g in range(G)]

    ctx = ExitStack()
    with ctx:
        def sb(name, shape, dt=F32):
            return ctx.enter_context(nc.sbuf_tensor("sb_" + name, shape, dt))

        def sem(name):
            return ctx.enter_context(nc.semaphore(name))

        def sem2(name):
            return [sem(f"{name}_{i}") for i in range(2)]

        ident = sb("ident", [P, P])
        ones_bf = sb("ones_bf", [P, P], BF16)
        before_bf = sb("before_bf", [P, P], BF16)
        iota_e = sb("iota_e", [P, E])
        iota_b = sb("iota_b", [1, NEX])
        neg_half = sb("neg_half", [P, QT])
        ones_row = sb("ones_row", [1, P])
        scan_one = sb("scan_one", [P, E * NT])
        wq = sb("wq", [P, D]); wk = sb("wk", [P, D]); wv = sb("wv", [P, D]); wo = sb("wo", [P, D])
        bq_col = sb("bq_col", [P, 1]); bk_col = sb("bk_col", [P, 1]); bqs_col = sb("bqs_col", [P, 1])
        bv_row = sb("bv_row", [1, D]); bo_row = sb("bo_row", [1, D])
        wg = sb("wg", [P, E]); wg_hi = sb("wg_hi", [P, E], F32R); wg_lo = sb("wg_lo", [P, E], F32R)
        b1_col = sb("b1_col", [P, E * FC]); b2_col = sb("b2_col", [P, E])
        bs1_col = sb("bs1_col", [P, FC]); bs2_col = sb("bs2_col", [P, 1])

        X = sb("X", [P, NT, D])
        xn = sb("xn", [P, NT, D])
        bn = sb("bn", [P, 2, QT, 6]); mv = sb("mv", [P, 2, QT, 2])
        vare = sb("vare", [P, QT]); rstd = sb("rstd", [P, 2, QT])

        xT = sb("xT", [P, 2 * NSH, BLK], F32R)
        xT_hi, xT_lo = xT[:, 0:NSH, :], xT[:, NSH:2 * NSH, :]
        logits = sb("logits", [P, NT, E]); top_v = sb("top_v", [P, NT, E]); top_i = sb("top_i", [P, NT, E], U32)
        top_f = sb("top_f", [P, 2, NT]); gap = sb("gap", [P, NT]); gate = sb("gate", [P, 2, NT])
        hot = [sb(f"hot{j}", [P, NT, E]) for j in range(2)]
        hot_bf = sb("hot_bf", [P, NT, E], BF16)
        count = sb("count", [P, E, NT]); upto = sb("upto", [P, E, NT])
        size = sb("size", [P, E]); size_i = sb("size_i", [P, E], I32); blocks = sb("blocks", [P, E])
        blocks_upto = sb("blocks_upto", [P, E]); first_slot = sb("first_slot", [P, E])
        slot = sb("slot", [P, NT, E]); slot_f = sb("slot_f", [P, 2, NT]); slot_i = sb("slot_i", [P, 2, NT], U32)
        blk_cmp = sb("blk_cmp", [1, NEX, E]); blk_f = sb("blk_f", [1, NEX]); blk_e = sb("blk_e", [1, NEX], I32)

        w1_raw = sb("w1_raw", [P, 2, F]); w2_raw = sb("w2_raw", [P, 2, F])
        w1_hi = sb("w1_hi", [P, 2, FC, P], F32R); w1_lo = sb("w1_lo", [P, 2, FC, P], F32R)
        w2_hi = sb("w2_hi", [P, 2, FC, P], F32R); w2_lo = sb("w2_lo", [P, 2, FC, P], F32R)
        x_rows_sb = sb("x_rows", [P, 2, SUB, D])
        ws1_raw = w1_raw[:, 1]; ws2_raw = w2_raw[:, 1]
        ws1_hi = sb("ws1_hi", [P, FC, P], F32R); ws1_lo = sb("ws1_lo", [P, FC, P], F32R)
        ws2_hi = sb("ws2_hi", [P, FC, P], F32R); ws2_lo = sb("ws2_lo", [P, FC, P], F32R)
        xb = sb("xb", [P, 4, BLK], F32R)
        xb_hi, xb_lo = xb[:, 0:2, :], xb[:, 2:4, :]
        h_hi = sb("h_hi", [P, FC, BLK], F32R); h_lo = sb("h_lo", [P, FC, BLK], F32R)
        yT = sb("yT", [P, 2, BLK]); y_rows = sb("y_rows", [P, 2, SUB, D])
        picked = sb("picked", [P, 2, QT, 2, D])

        q_st = xb
        k_st = xT[:, :, :].rearrange("p (g r) n -> p g r n", r=R)
        MAX_ROW = R * HK
        v_st = sb("v_st", [P, 2, QT, G * R, RP])
        qk_hi = sb("qk_hi", [P, 2, SEQ], F32R); qk_lo = sb("qk_lo", [P, 2, SEQ], F32R)
        xnT = sb("xnT", [P, SEQ])
        RING = 8
        probs = sb("probs", [P, RING, SEQ])
        ctx_raw = sb("ctx_raw", [P, SEQ]); rden = sb("rden", [P, QT, R])
        ctx_n = sb("ctx_n", [P, QT, D]); ctxT = sb("ctxT", [P, SEQ])
        nmax = sb("nmax", [P, 2, R, QT]); nmax_parts = sb("nmax_parts", [P, 2, R, 2, QT])
        nmaxT = sb("nmaxT", [R * 2 * QT, P], F32R)

        bank = ctx.enter_context(nc.psum_tensor("banks", [P, 8, BLK], F32))

        const_in = sem("const_in"); aside = sem("aside"); x_loaded = sem("x_loaded")
        pool_const = sem("pool_const"); dve_const = sem("dve_const"); xs_zero = sem("xs_zero")
        out_done = sem("out_done")

        def sems(tag, names):
            return {n: sem(f"{n}_{tag}") for n in names.split()}

        rt, sh, ex = [], [], []
        for f in range(2):
            s = sems(f"route{f}", "stats mv var rstd xn xT_ps xT_hi xT_lo logit_ps logits maths gap exp hot count_ps "
                                  "slots blk scattered combined")
            s["picked"] = sem2(f"picked_{f}")
            rt.append(s)
            for kind, group in (("shared", sh), ("expert", ex)):
                s = sems(f"{kind}{f}", "h_ps relu h_hi h_lo h_used yT rows_ps rows")
                if kind == "expert":
                    s |= sems(f"{kind}{f}", "w1_hi w1_lo w2_hi w2_lo x_ps x_hi x_lo")
                    s["loaded"] = sem2(f"loaded_{kind}{f}")
                    s["stored"] = sem2(f"stored_{kind}{f}")
                group.append(s)
        at = sems("att", "init stats mv var rstd xn nmax_parts s_ps s_read st_ps probs pv_ps ctx_raw rden "
                         "nmaxT_ps nmaxT turn_ps turned ctxT_ps ctxT o_ps added v_ps v xT_ps xT q_ps q k_ps k "
                         "q_z k_z q_hi k_hi")
        nmax_out = sem("nmax_out")
        nmax_in = [sem(f"nmax_in_{g}") for g in range(G)]
        qk_out = sem("qk_out"); stack_const = sem("stack_const")
        stack_in = [sem(f"stack_in_{g}") for g in range(G)]

        block = ctx.enter_context(nc.Block())

        def alone(eng):
            eng.sem_inc(aside, 1)

        H_BANK, O_BANK, T_BANK, Y_BANK = 0, 4, 6, 7
        L_BANK = T_BANK

        def pe_route(pe, f):
            s = rt[f]
            if f:
                wait(pe, at["added"], BATCH)
            for t in range(NSH):
                pe.wait_ge(s["xn"], SUB * (t + 1))
                wait(pe, s["xT_lo"], t - 1)
                for j in range(SUB):
                    mm = pe.transpose(bank[:, t % 2, j * P:(j + 1) * P], xn[:, SUB * t + j, :], ident[:, :])
                mm.then_inc(s["xT_ps"], 1)
                if t:
                    pe_logits(pe, s, t - 1)
            pe_logits(pe, s, NSH - 1)
            pe.wait_ge(s["hot"], 1)
            pe.matmul(bank[:, L_BANK, 0:NT * E], before_bf[:, :], hot_bf[:, :, :].rearrange("p t e -> p (t e)"),
                      start=True, stop=True)
            pe.matmul(bank[:, L_BANK, NT * E:2 * NT * E], ones_bf[:, :], hot_bf[:, :, :].rearrange("p t e -> p (t e)"),
                      start=True, stop=True).then_inc(s["count_ps"], 1)

        def pe_logits(pe, s, t):
            pe.wait_ge(s["xT_lo"], t + 1)
            for j in range(SUB):
                o = bank[:, L_BANK, (SUB * t + j) * E:(SUB * t + j + 1) * E]
                xh, xl = xT_hi[:, t, j * P:(j + 1) * P], xT_lo[:, t, j * P:(j + 1) * P]
                pe.matmul(o, xh, wg_hi[:, :], start=True, stop=False)
                pe.matmul(o, xh, wg_lo[:, :], start=False, stop=False)
                mm = pe.matmul(o, xl, wg_hi[:, :], start=False, stop=True)
            mm.then_inc(s["logit_ps"], 1)

        def pe_blocks(pe, s, count, routed):
            def product(o, wh, wl, xh, xl, first, last):
                pe.matmul(o, wh, xh, start=first, stop=False)
                pe.matmul(o, wh, xl, start=False, stop=False)
                return pe.matmul(o, wl, xh, start=False, stop=last)

            def turn_x(k, par, half):
                pe.wait_ge(s["loaded"][par], 48 * (half + 1))
                wait(pe, s["x_lo"], k)
                for j in range(SUB):
                    mm = pe.transpose(bank[:, T_BANK, j * P:(j + 1) * P], x_rows_sb[:, par, j, :], ident[:, :])
                mm.then_inc(s["x_ps"], 1)

            def hidden(k, par, c):
                if routed:
                    wh, wl, xh, xl = w1_hi[:, par, c, :], w1_lo[:, par, c, :], xb_hi[:, par, :], xb_lo[:, par, :]
                    if c == 0:
                        pe.wait_ge(s["w1_lo"], k + 1)
                        pe.wait_ge(s["x_lo"], k + 1)
                else:
                    kk = k if isinstance(k, int) else None
                    at_k = slice(k, k + 1) if kk is not None else bass.ds(k, 1)
                    wh, wl = ws1_hi[:, c, :], ws1_lo[:, c, :]
                    xh = xT_hi[:, at_k, :].rearrange("p o n -> p (o n)")
                    xl = xT_lo[:, at_k, :].rearrange("p o n -> p (o n)")
                wait(pe, s["h_lo"], FC * (k - 1) + c + 1)
                product(bank[:, H_BANK + c, :], wh, wl, xh, xl, True, True).then_inc(s["h_ps"], 1)

            def output(k, par, c):
                if routed:
                    wh, wl = w2_hi[:, par, c, :], w2_lo[:, par, c, :]
                    if c == 0:
                        pe.wait_ge(s["w2_lo"], k + 1)
                else:
                    wh, wl = ws2_hi[:, c, :], ws2_lo[:, c, :]
                if c == 0:
                    wait(pe, s["yT"], k - 1)
                pe.wait_ge(s["h_lo"], FC * k + c + 1)
                product(bank[:, O_BANK + par, :], wh, wl, h_hi[:, c, :], h_lo[:, c, :],
                        c == 0, c == FC - 1).then_inc(s["h_used"], 1)

            def turn_y(k, par):
                pe.wait_ge(s["yT"], k + 1)
                wait(pe, s["rows"], k)
                for j in range(SUB):
                    mm = pe.transpose(bank[:, Y_BANK, j * P:(j + 1) * P], yT[:, par, j * P:(j + 1) * P], ident[:, :])
                mm.then_inc(s["rows_ps"], 1)

            def body(k, par, half):
                if routed and exists(k + 1, count):
                    turn_x(k + 1, 1 - par, half + par)
                for c in range(FC):
                    if exists(k, count):
                        hidden(k, par, c)
                    if exists(k - 1, count):
                        output(k - 1, 1 - par, c)
                    if c == 1 and exists(k - 2, count):
                        turn_y(k - 2, par)

            if routed:
                turn_x(0, 0, 0)
            steps(pe, 0, count + 2, 2, count - 2, body)

        def act_route(act, f):
            s = rt[f]
            for t in range(NSH):
                act.wait_ge(s["xT_ps"], t + 1)
                act.activation(xT_hi[:, t, :], bank[:, t % 2, :], ACT.Copy).then_inc(s["xT_hi"], 1)
            act.wait_ge(s["gap"], 1)
            act.activation(gap[:, :], gap[:, :], ACT.Exp).then_inc(s["exp"], 1)

        def act_blocks(act, s, f, count, routed):
            def expert(k):
                at_k = slice(k, k + 1) if isinstance(k, int) else bass.ds(k, 1)
                return act.value_load(blk_e[0:1, at_k], min_val=0, max_val=E - 1)

            def x_hi(k, par):
                act.wait_ge(s["x_ps"], k + 1)
                wait(act, s["h_ps"], FC * (k - 1))
                act.activation(xb_hi[:, par, :], bank[:, T_BANK, :], ACT.Copy).then_inc(s["x_hi"], 1)

            def relu(k, c, e):
                bias = bs1_col[:, c:c + 1] if e is None else b1_col[:, bass.ds(e * FC + c, 1)]
                act.wait_ge(s["h_ps"], FC * k + c + 1)
                act.activation(bank[:, H_BANK + c, :], bank[:, H_BANK + c, :], ACT.Relu, bias=bias)\
                   .then_inc(s["relu"], 1)

            def hi(k, c):
                act.wait_ge(s["relu"], FC * k + c + 1)
                wait(act, s["h_used"], FC * (k - 1) + c + 1)
                act.activation(h_hi[:, c, :], bank[:, H_BANK + c, :], ACT.Copy).then_inc(s["h_hi"], 1)

            def y(k, par):
                e = expert(k) if routed else None
                bias = bs2_col[:, 0:1] if e is None else b2_col[:, bass.ds(e, 1)]
                act.wait_ge(s["h_used"], FC * (k + 1))
                wait(act, s["rows_ps"], k - 1)
                act.activation(yT[:, par, :], bank[:, O_BANK + par, :], ACT.Identity, bias=bias)\
                   .then_inc(s["yT"], 1)

            def body(k, par, half):
                if exists(k, count):
                    e = expert(k) if routed else None
                    relu(k, 0, e)
                    if routed and exists(k + 1, count):
                        x_hi(k + 1, 1 - par)
                    for c in range(1, FC):
                        relu(k, c, e)
                        hi(k, c - 1)
                    hi(k, FC - 1)
                if exists(k - 1, count):
                    y(k - 1, 1 - par)

            if routed:
                act.wait_ge(rt[f]["blk"], 1)
                x_hi(0, 0)
            steps(act, 0, count + 1, 2, count - 2, body)

        def tile(k, j=0):
            return slice(k + j, k + j + 1) if isinstance(k, int) else bass.ds(k + j, 1)

        def dve_stats(dve, s, t, par, n):
            alone(dve)
            for j in range(QT):
                dve.bn_stats(bn[:, par, j, :], X[:, tile(t * QT, j), :].rearrange("p o d -> p (o d)")).then_inc(s["stats"], 1)
            dve.wait_ge(s["stats"], QT * (n + 1))
            wait(dve, s["xn"], QT * (n - 1))
            alone(dve)
            for j in range(QT):
                dve.bn_aggr(mv[:, par, j, :], bn[:, par, j, :]).then_inc(s["mv"], 1)

        def pool_rstd(pool, s, t, par):
            pool.wait_ge(s["mv"], QT * (t + 1))
            wait(pool, s["rstd"], t)
            pool.tensor_scalar(vare[:, :], mv[:, par, :, 1], 1e-5, None, ALU.add).then_inc(s["var"], 1)
            pool.wait_ge(s["var"], t + 1)
            pool.tensor_tensor(rstd[:, par, :], vare[:, :], neg_half[:, :], ALU.pow).then_inc(s["rstd"], 1)

        def dve_norm(dve, s, t, par, to):
            dve.wait_ge(s["rstd"], t + 1)
            for j in range(QT):
                dve.tensor_scalar(xn[:, to + j, :], X[:, tile(t * QT, j), :].rearrange("p o d -> p (o d)"),
                                  mv[:, par, j, 0:1], rstd[:, par, j:j + 1], ALU.subtract, ALU.mult)\
                   .then_inc(s["xn"], 1)

        def dve_route(dve, f):
            s = rt[f]
            if f == 0:
                dve.wait_ge(x_loaded, 16)
            dve_stats(dve, s, 0, 0, 0)
            for t in range(NSH):
                if t + 1 < NSH:
                    dve_stats(dve, s, t + 1, (t + 1) % 2, t + 1)
                dve_norm(dve, s, t, t % 2, SUB * t)
                if t:
                    dve_xT_lo(dve, s, t - 1)
            dve_xT_lo(dve, s, NSH - 1)
            dve.wait_ge(s["logit_ps"], NSH)
            dve.tensor_copy(logits[:, :, :].rearrange("p t e -> p (t e)"), bank[:, L_BANK, 0:NT * E])\
               .then_inc(s["logits"], 1)
            dve.wait_ge(s["logits"], 1)

            for t in range(NT):
                dve.max(top_v[:, t, :], logits[:, t, :]).then_inc(s["maths"], 1)
            for t in range(NT):
                dve.wait_ge(s["maths"], t + 1)
                op = dve.max_index(top_i[:, t, :], top_v[:, t, :], logits[:, t, :])
            op.then_inc(s["maths"], 1)
            done = NT + 1

            def then(op):
                nonlocal done
                op.then_inc(s["maths"], 1)
                done += 1
                dve.wait_ge(s["maths"], done)

            def wide(ap, n, at_end=True):
                shape = list(ap.shape)
                if at_end:
                    return ap.unsqueeze(len(shape)).to_broadcast(shape + [n])
                return ap.unsqueeze(1).to_broadcast([shape[0], n] + shape[1:])

            dve.wait_ge(s["maths"], done)
            dve.tensor_tensor(gap[:, :], top_v[:, :, 1], top_v[:, :, 0], ALU.subtract).then_inc(s["gap"], 1)
            for j in range(2):
                then(dve.tensor_copy(top_f[:, j, :], top_i[:, :, j]))
            for j in range(2):
                then(dve.tensor_tensor(hot[j][:, :, :], wide(iota_e[:, :], NT, False), wide(top_f[:, j, :], E),
                                       ALU.is_equal))
            dve.tensor_tensor(hot_bf[:, :, :], hot[0][:, :, :], hot[1][:, :, :], ALU.add).then_inc(s["hot"], 1)
            dve.wait_ge(s["exp"], 1)
            then(dve.tensor_scalar(gate[:, 1, :], gap[:, :], 1.0, 2.0, ALU.add, ALU.mult))
            then(dve.reciprocal(gate[:, 0, :], gate[:, 1, :]))
            then(dve.tensor_tensor(gate[:, 1, :], gate[:, 0, :], gap[:, :], ALU.mult))

            dve.wait_ge(s["count_ps"], 1)
            then(dve.tensor_copy(count[:, :, :], bank[:, L_BANK, NT * E:2 * NT * E].rearrange("p (t e) -> p e t", e=E)))
            then(dve.tensor_tensor_scan(upto[:, :, :].rearrange("p e t -> p (e t)"), scan_one[:, :],
                                        count[:, :, :].rearrange("p e t -> p (e t)"), 0.0, ALU.mult, ALU.add))
            then(dve.tensor_copy(size[:, 0:1], upto[:, 0:1, NT - 1]))
            then(dve.tensor_tensor(size[:, 1:E], upto[:, 1:E, NT - 1], upto[:, 0:E - 1, NT - 1], ALU.subtract))
            then(dve.tensor_scalar(size_i[:, :], size[:, :], float(BLK - 1), None, ALU.add))
            then(dve.tensor_scalar(size_i[:, :], size_i[:, :], LOGBLK, None, ALU.logical_shift_right))
            then(dve.tensor_copy(blocks[:, :], size_i[:, :]))
            then(dve.tensor_tensor_scan(blocks_upto[:, :], scan_one[:, 0:E], blocks[:, :], 0.0, ALU.mult, ALU.add))
            then(dve.tensor_tensor(blk_cmp[:, :, :], wide(blocks_upto[0:1, :], NEX, False),
                                   wide(iota_b[:, :], E), ALU.is_le))
            then(dve.tensor_reduce(blk_f[:, :], blk_cmp[:, :, :], AX.X, ALU.add))
            dve.tensor_scalar(blk_e[:, :], blk_f[:, :], float(E - 1), None, ALU.min).then_inc(s["blk"], 1)
            then(dve.tensor_tensor(first_slot[:, :], blocks_upto[:, :], blocks[:, :], ALU.subtract))
            then(dve.tensor_scalar(first_slot[:, :], first_slot[:, :], float(BLK), None, ALU.mult))
            then(dve.tensor_tensor(first_slot[:, :], first_slot[:, :], upto[:, :, NT - 1], ALU.subtract))
            then(dve.tensor_tensor(first_slot[:, :], first_slot[:, :], size[:, :], ALU.add))
            then(dve.tensor_tensor(upto[:, :, :], upto[:, :, :], count[:, :, :], ALU.subtract))
            then(dve.tensor_tensor(upto[:, :, :], upto[:, :, :], wide(first_slot[:, :], NT), ALU.add))
            then(dve.tensor_tensor(slot[:, :, :], bank[:, L_BANK, 0:NT * E].rearrange("p (t e) -> p t e", e=E),
                                   upto[:, :, :].rearrange("p e t -> p t e"), ALU.add))
            for j in range(2):
                then(dve.tensor_tensor(hot[j][:, :, :], hot[j][:, :, :], slot[:, :, :], ALU.mult))
            for j in range(2):
                then(dve.tensor_reduce(slot_f[:, j, :], hot[j][:, :, :], AX.X, ALU.add))
            dve.tensor_copy(slot_i[:, :, :], slot_f[:, :, :]).then_inc(s["slots"], 1)

        def dve_xT_lo(dve, s, t):
            dve.wait_ge(s["xT_hi"], t + 1)
            dve.tensor_tensor(xT_lo[:, t, :], bank[:, t % 2, :], xT_hi[:, t, :].bitcast(F32), ALU.subtract)\
               .then_inc(s["xT_lo"], 1)

        def dve_blocks(dve, s, count, routed):
            def w1(k, par, half):
                dve.wait_ge(s["loaded"][par], 48 * (half + 1))
                wait(dve, s["h_ps"], FC * (k - 1))
                dve.tensor_copy(w1_hi[:, par, :, :], w1_raw[:, par, :].rearrange("d (p c) -> d c p", c=FC))\
                   .then_inc(s["w1_hi"], 1)

            def w2(k, par, half):
                dve.wait_ge(s["loaded"][par], 48 * (half + 1))
                wait(dve, s["h_used"], FC * (k - 1))
                dve.tensor_copy(w2_hi[:, par, :, :].rearrange("p c d -> p (c d)"), w2_raw[:, par, :])\
                   .then_inc(s["w2_hi"], 1)

            def x_lo(k, par):
                dve.wait_ge(s["x_hi"], k + 1)
                dve.tensor_tensor(xb_lo[:, par, :], bank[:, T_BANK, :], xb_hi[:, par, :].bitcast(F32), ALU.subtract)\
                   .then_inc(s["x_lo"], 1)

            def h_low(k, c):
                dve.wait_ge(s["h_hi"], FC * k + c + 1)
                dve.tensor_tensor(h_lo[:, c, :], bank[:, H_BANK + c, :], h_hi[:, c, :].bitcast(F32), ALU.subtract)\
                   .then_inc(s["h_lo"], 1)

            def rows(k, par, half):
                dve.wait_ge(s["rows_ps"], k + 1)
                if routed:
                    wait(dve, s["stored"][par], 16 * half)
                    dve.tensor_copy(y_rows[:, par, :, :].rearrange("p s d -> p (s d)"), bank[:, Y_BANK, :])\
                       .then_inc(s["rows"], 1)
                else:
                    at_k = slice(k * SUB, (k + 1) * SUB) if isinstance(k, int) else bass.ds(k * SUB, SUB)
                    xk = X[:, at_k, :]
                    dve.scalar_tensor_tensor(xk, bank[:, Y_BANK, :].rearrange("p (s d) -> p s d", d=D), 0.5, xk,
                                             ALU.mult, ALU.add).then_inc(s["rows"], 1)

            def body(k, par, half):
                if exists(k, count):
                    if routed:
                        w2(k, par, half)
                    h_low(k, 0)
                    if routed and exists(k + 1, count):
                        w1(k + 1, 1 - par, half + par)
                    h_low(k, 1)
                    if routed and exists(k + 1, count):
                        x_lo(k + 1, 1 - par)
                    h_low(k, 2)
                if exists(k - 2, count):
                    rows(k - 2, par, half - 1)
                if exists(k, count):
                    h_low(k, 3)

            if routed:
                w1(0, 0, 0)
                x_lo(0, 0)
            steps(dve, 0, count + 2, 2, count - 2, body)

        def dve_combine(dve, s, t, par, half, n):
            dve.wait_ge(s["picked"][par], 16 * 2 * QT * (half + 1))
            for e in range(2):
                for j in range(QT):
                    x = X[:, tile(t * QT, j), :].rearrange("p o d -> p (o d)")
                    if e:
                        dve.wait_ge(s["combined"], 2 * QT * n + j + 1)
                    dve.scalar_tensor_tensor(x, picked[:, par, j, e, :], gate[:, e, tile(t * QT, j)], x,
                                             ALU.mult, ALU.add).then_inc(s["combined"], 1)
            dve.wait_ge(s["combined"], 2 * QT * (n + 1))

        def pool_route(pool, f):
            s = rt[f]
            for t in range(NSH):
                pool_rstd(pool, s, t, t % 2)

        def pool_scatter(pool, f):
            s = rt[f]
            if f == 0:
                pool.wait_ge(xs_zero, 16 * (SLOTS * D // P // 2048))
            pool.wait_ge(s["slots"], 1)
            for t in range(NT):
                for j in range(2):
                    pool.indirect_dma_start(xs, bass.IndirectOffsetOnAxis(ap=slot_i[:, j, t:t + 1], axis=0),
                                            xn[:, t, :], None).then_inc(s["scattered"], 16)

        def pool_weights(pool, s, count):
            def w1(k, par):
                pool.wait_ge(s["w1_hi"], k + 1)
                pool.tensor_tensor(w1_lo[:, par, :, :], w1_raw[:, par, :].rearrange("d (p c) -> d c p", c=FC),
                                   w1_hi[:, par, :, :].bitcast(F32), ALU.subtract).then_inc(s["w1_lo"], 1)

            def w2(k, par):
                pool.wait_ge(s["w2_hi"], k + 1)
                pool.tensor_tensor(w2_lo[:, par, :, :].rearrange("p c d -> p (c d)"), w2_raw[:, par, :],
                                   w2_hi[:, par, :, :].rearrange("p c d -> p (c d)").bitcast(F32), ALU.subtract)\
                    .then_inc(s["w2_lo"], 1)

            def body(k, par, half):
                w2(k, par)
                if exists(k + 1, count):
                    w1(k + 1, 1 - par)
                if s is ex[0] and isinstance(k, int):
                    if k == 0:
                        pool.wait_ge(sh[0]["h_ps"], FC * NSH)
                    g = k if k < 2 else k - count + 4
                    pool.memset(k_st[:, g, :, :].bitcast(F32), 0.0).then_inc(at["init"], 1)

            w1(0, 0)
            steps(pool, 0, count, 2, count - 2, body)

        def pool_gather(pool, f, t):
            s = rt[f]
            if t == 0:
                for par in range(2):
                    pool.wait_ge(ex[f]["stored"][par], 16 * NEX // 2)
            wait(pool, s["combined"], 2 * QT * (t - 1))
            for j in range(QT):
                for e in range(2):
                    pool.indirect_dma_start(picked[:, t % 2, j, e, :], None, ys,
                                            bass.IndirectOffsetOnAxis(ap=slot_i[:, e, QT * t + j:QT * t + j + 1], axis=0))\
                        .then_inc(s["picked"][t % 2], 16)

        def sp_blocks(sp, s, f, count):
            def load(k, par, half):
                at_k = slice(k, k + 1) if isinstance(k, int) else bass.ds(k, 1)
                rows_k = slice(k * BLK, (k + 1) * BLK) if isinstance(k, int) else bass.ds(k * BLK, BLK)
                e = sp.value_load(blk_e[0:1, at_k], min_val=0, max_val=E - 1)
                wait(sp, s["w1_lo"], k - 1)
                wait(sp, s["w2_lo"], k - 1)
                wait(sp, s["x_ps"], k - 1)
                alone(sp)
                sp.dma_start(w1_raw[:, par, :], W1[bass.ds(e, 1), :, :].rearrange("o d f -> (o d) f"))\
                  .then_inc(s["loaded"][par], 16)
                sp.dma_start(x_rows_sb[:, par, :, :], xs[rows_k, :].rearrange("(s p) d -> p s d", p=P))\
                  .then_inc(s["loaded"][par], 16)
                sp.dma_start(w2_raw[:, par, :], W2[bass.ds(e, 1), :, :].rearrange("o (p c) d -> (o p) (c d)", c=FC))\
                  .then_inc(s["loaded"][par], 16)

            def store(k, par):
                rows_k = slice(k * BLK, (k + 1) * BLK) if isinstance(k, int) else bass.ds(k * BLK, BLK)
                sp.wait_ge(s["rows"], k + 1)
                alone(sp)
                sp.dma_start(ys[rows_k, :].rearrange("(s p) d -> p s d", p=P), y_rows[:, par, :, :])\
                  .then_inc(s["stored"][par], 16)

            def body(k, par, half):
                if exists(k, count):
                    load(k, par, half)
                if exists(k - 4, count):
                    store(k - 4, par)

            sp.wait_ge(rt[f]["blk"], 1)
            sp.wait_ge(rt[f]["scattered"], 16 * 2 * NT)
            steps(sp, 0, count + 4, 4, count, body)

        FIRST_ROUND, ROUNDS = -2, BATCH + 1
        ST_BANK, S_BANK, CTX_BANK, MISC_BANK = 0, 2, 6, 7
        STEPS = G * QT * R
        MISC = {2: ("nmaxT", 0, 1), 6: ("turn", -1, G - 1), 9: ("ctxT", -1, 0), 12: ("v", 1, 0), 15: ("o", -1, 0),
                18: ("nmaxT", 0, 2), 24: ("turn", 0, 0), 34: ("nmaxT", 0, 3), 40: ("turn", 0, 1),
                44: ("xT", 2, 0), 47: ("q", 2, 0), 50: ("nmaxT", 1, 0), 54: ("k", 2, 0), 57: ("turn", 0, 2)}
        READ = {"nmaxT": "nmaxT", "turn": "turned", "ctxT": "ctxT", "o": "added", "v": "v", "xT": "xT", "q": "q", "k": "k"}

        def number(what, b, g):
            return G * b + g + 1 if what in ("nmaxT", "turn") else b + 1

        def present(t, what, db, g):
            return exists(t + db, BATCH)

        def misc_before(t, step):
            keys = sorted(MISC)
            i, u = keys.index(step), t
            while True:
                i -= 1
                if i < 0:
                    i, u = len(keys) - 1, (u - 1 if isinstance(u, int) else t - 1)
                    if isinstance(u, int) and u < FIRST_ROUND:
                        return None
                what, db, g = MISC[keys[i]]
                if present(u, what, db, g):
                    return what, number(what, u + db, g)

        def entry_ahead(t, s):
            ahead = s + 2 * QT * R
            return t + ahead // STEPS, ahead % STEPS

        def heads(ap, r, rows):
            return ap[RP * r:RP * r + rows]

        def pe_attention(pe):
            def scores(b, pair):
                g, qt, rp = pair // (2 * QT), pair // 2 % QT, pair % 2
                if pair % (2 * QT) == 0:
                    pe.wait_ge(stack_in[g], 16 * (R + 2) * (b + 1))
                wait(pe, at["s_read"], 2 * G * QT * b + pair - 1)
                for i in range(2):
                    r = 2 * rp + i
                    mm = pe.matmul(bank[:, S_BANK + 2 * (pair % 2) + i, :],
                                   q_st[:, g, qt * P:(qt + 1) * P], k_st[:, g, r, :], start=True, stop=True)
                mm.then_inc(at["s_ps"], 1)

            def scores_t(b, s):
                g, kt, r = s // (QT * R), s // R % QT, s % R
                if s % (QT * R) == 0:
                    pe.wait_ge(nmax_in[g], 16 * (b + 1))
                wait(pe, at["probs"], STEPS * b + s - 1)
                pe.matmul(bank[:, ST_BANK + s % 2, :], k_st[:, g, r, kt * P:(kt + 1) * P],
                          q_st[:, g, :], start=True, stop=True).then_inc(at["st_ps"], 1)

            def context(b, par, q):
                g, kt = q // QT, q % QT
                pe.wait_ge(at["probs"], STEPS * b + R * (q + 1))
                if q == 0:
                    pe.wait_ge(at["v"], b + 1)
                if kt == 0:
                    wait(pe, at["ctx_raw"], G * b + g)
                for r in range(R):
                    mm = pe.matmul(heads(bank, r, RP)[:, CTX_BANK, :], v_st[:, par, kt, g * R + r, :],
                                   probs[:, (R * q + r) % RING, :], start=kt == 0, stop=kt == QT - 1)
                mm.then_inc(at["pv_ps"], 1)

            def misc(t, par, step):
                what, db, g = MISC[step]
                b = t + db
                before = misc_before(t, step)
                if before:
                    pe.wait_ge(at[READ[before[0]]], before[1])
                o = bank[:, MISC_BANK, :]
                if what == "nmaxT":
                    pe.wait_ge(at["nmax_parts"], 2 * (G * b + g + 1))
                    mm = pe.transpose(o[0:2 * R * QT, 0:P],
                                      nmax_parts[:, g % 2].rearrange("p r h q -> p (r h q)"), ident[:, :])
                elif what == "turn":
                    pe.wait_ge(at["ctx_raw"], G * b + g + 1)
                    for j in range(QT):
                        mm = pe.transpose(o[:, j * P:(j + 1) * P], ctx_raw[:, j * P:(j + 1) * P], ident[:, :])
                elif what == "ctxT":
                    pe.wait_ge(at["turned"], G * (b + 1))
                    for j in range(QT):
                        mm = pe.transpose(o[:, j * P:(j + 1) * P], ctx_n[:, j, :], ident[:, :])
                elif what == "o":
                    pe.wait_ge(at["ctxT"], b + 1)
                    for j in range(QT):
                        pe.matmul(o[:, j * P:(j + 1) * P], ones_row[:, :], bo_row[:, :], start=True, stop=False)
                        mm = pe.matmul(o[:, j * P:(j + 1) * P], ctxT[:, j * P:(j + 1) * P], wo[:, :],
                                       start=False, stop=True)
                elif what == "v":
                    pe.wait_ge(at["xT"], b + 1)
                    for j in range(QT):
                        pe.matmul(o[:, j * P:(j + 1) * P], ones_row[:, :], bv_row[:, :], start=True, stop=False)
                        mm = pe.matmul(o[:, j * P:(j + 1) * P], xnT[:, j * P:(j + 1) * P], wv[:, :],
                                       start=False, stop=True)
                elif what == "xT":
                    pe.wait_ge(at["xn"], QT * (b + 1))
                    for j in range(QT):
                        mm = pe.transpose(o[:, j * P:(j + 1) * P], xn[:, QT * par + j, :], ident[:, :])
                elif what in ("q", "k"):
                    pe.wait_ge(at["xT"], b + 1)
                    mm = pe.matmul(o, (wq if what == "q" else wk)[:, :], xnT[:, :], start=True, stop=True)
                mm.then_inc(at[what + "_ps"], 1)

            def round_(t, par, half):
                for s in range(STEPS):
                    if exists(t, BATCH):
                        scores_t(t, s)
                    ahead, of = entry_ahead(t, s)
                    if s % 2 == 0 and exists(ahead, BATCH):
                        scores(ahead, of // 2)
                    if s == 1 and exists(t - 1, BATCH):
                        context(t - 1, 1 - par, G * QT - 1)
                    if s % R == 1 and s > R and exists(t, BATCH):
                        context(t, par, s // R - 1)
                    if s in MISC and present(t, *MISC[s]):
                        misc(t, par, s)

            pe.wait_ge(stack_const, 16 * STACK_CONSTS)
            pe.wait_ge(ex[0]["rows"], NEX)
            steps(pe, FIRST_ROUND, ROUNDS, LOOP[0], LOOP[1], round_)

        LOOP = (2, BATCH - 2)
        QK_PARTS = 2 * 3
        STACK_CONSTS = 1 + R

        def act_attention(act):
            def prob(b, s):
                act.wait_ge(at["st_ps"], STEPS * b + s + 1)
                wait(act, at["pv_ps"], G * QT * b + s // R - 1)
                act.activation(probs[:, s % RING, :], bank[:, ST_BANK + s % 2, :], ACT.Exp).then_inc(at["probs"], 1)

            def context_out(b, g):
                act.wait_ge(at["pv_ps"], QT * (G * b + g + 1))
                wait(act, at["turn_ps"], G * b + g)
                act.activation(ctx_raw[:, :], bank[:, CTX_BANK, :], ACT.Copy).then_inc(at["ctx_raw"], 1)

            def misc(t, par, half, step):
                what, db, g = MISC[step]
                b = t + db
                m = bank[:, MISC_BANK, :]
                act.wait_ge(at[what + "_ps"], number(what, b, g))
                if what == "ctxT":
                    act.activation(ctxT[:, :], m, ACT.Copy).then_inc(at["ctxT"], 1)
                elif what == "v":
                    v_par = 1 - par
                    act.activation(v_st[:, v_par, :, :, 0:HD].rearrange("p k h d -> p (k h) d"),
                                   m.rearrange("p (kh d) -> p kh d", d=HD), ACT.Copy).then_inc(at["v"], 1)
                elif what == "xT":
                    act.activation(xnT[:, :], m, ACT.Copy).then_inc(at["xT"], 1)
                elif what in ("q", "k"):
                    i = 0 if what == "q" else 1
                    act.activation(m, m, ACT.Identity, bias=(bqs_col if what == "q" else bk_col)[:, 0:1],
                                   scale=SCALE if what == "q" else 1.0).then_inc(at[what + "_z"], 1)
                    act.wait_ge(at[what + "_z"], b + 1)
                    wait(act, qk_out, 16 * QK_PARTS * b)
                    act.activation(qk_hi[:, i, :], m, ACT.Copy).then_inc(at[what + "_hi"], 1)

            def round_(t, par, half):
                for s in range(STEPS):
                    if s == 4 and exists(t - 1, BATCH):
                        context_out(t - 1, G - 1)
                    if s % (QT * R) == 4 and s > QT * R and exists(t, BATCH):
                        context_out(t, s // (QT * R) - 1)
                    if exists(t, BATCH):
                        prob(t, s)
                    if s in MISC and MISC[s][0] in ("ctxT", "v", "xT", "q", "k") and present(t, *MISC[s]):
                        misc(t, par, half, s)

            steps(act, FIRST_ROUND, ROUNDS, LOOP[0], LOOP[1], round_)

        def dve_attention(dve):
            def maxima(b, pair):
                g, qt, rp = pair // (2 * QT), pair // 2 % QT, pair % 2
                dve.wait_ge(at["s_ps"], 2 * G * QT * b + pair + 1)
                slot2 = S_BANK + 2 * (pair % 2)
                dve.tensor_reduce(nmax[:, g % 2, 2 * rp:2 * rp + 2, qt], bank[:, slot2:slot2 + 2, :],
                                  AX.X, ALU.max, negate=True).then_inc(at["s_read"], 1)

            def max_parts(b, g):
                n = G * b + g
                hi, lo = nmax_parts[:, g % 2, :, 0, :], nmax_parts[:, g % 2, :, 1, :]
                dve.wait_ge(at["s_read"], 2 * QT * (n + 1))
                wait(dve, at["nmaxT_ps"], n - 1)
                dve.tensor_copy(hi.bitcast(F32R), nmax[:, g % 2, :, :]).then_inc(at["nmax_parts"], 1)
                dve.wait_ge(at["nmax_parts"], 2 * n + 1)
                dve.tensor_tensor(lo.bitcast(F32R), nmax[:, g % 2, :, :], hi, ALU.subtract)\
                   .then_inc(at["nmax_parts"], 1)

            def misc(t, par, half, step):
                what, db, g = MISC[step]
                b = t + db
                m = bank[:, MISC_BANK, :]
                if what == "nmaxT":
                    n = G * b + g
                    dve.wait_ge(at["nmaxT_ps"], n + 1)
                    wait(dve, nmax_out, 16 * n)
                    dve.tensor_copy(nmaxT[:, :], m[0:2 * R * QT, 0:P]).then_inc(at["nmaxT"], 1)
                elif what == "turn":
                    n = G * b + g
                    mv4 = m.rearrange("p (q r c) -> p q r c", r=R, c=RP)
                    dve.wait_ge(at["turn_ps"], n + 1)
                    if g == 0:
                        wait(dve, at["ctxT_ps"], b)
                    dve.reciprocal(rden[:, :, :], mv4[:, :, :, HD]).then_inc(at["rden"], 1)
                    dve.wait_ge(at["rden"], n + 1)
                    dve.tensor_tensor(ctx_n[:, :, g * R * HD:(g + 1) * R * HD].rearrange("p q (r d) -> p q r d", d=HD),
                                      mv4[:, :, :, 0:HD],
                                      rden[:, :, :].unsqueeze(3).to_broadcast([P, QT, R, HD]),
                                      ALU.mult).then_inc(at["turned"], 1)
                elif what == "o":
                    dve.wait_ge(at["o_ps"], b + 1)
                    at_b = slice(b * QT, (b + 1) * QT) if isinstance(b, int) else bass.ds(b * QT, QT)
                    dve.tensor_tensor(X[:, at_b, :], m.rearrange("p (q d) -> p q d", d=D), X[:, at_b, :],
                                      ALU.add).then_inc(at["added"], 1)
                elif what in ("q", "k"):
                    dve.wait_ge(at[what + "_hi"], b + 1)
                    i = 0 if what == "q" else 1
                    dve.tensor_tensor(qk_lo[:, i, :], m, qk_hi[:, i, :].bitcast(F32), ALU.subtract)\
                       .then_inc(at[what], 1)

            def round_(t, par, half):
                for s in range(STEPS):
                    if s == 8 and exists(t + 2, BATCH):
                        dve_combine(dve, rt[0], t + 2, par, half + 1, t + 2)
                        dve_stats(dve, at, t + 2, par, t + 2)
                    if s == 28 and exists(t + 2, BATCH):
                        dve_norm(dve, at, t + 2, par, QT * par)
                    ahead, of = entry_ahead(t, s)
                    if s % 2 == 0 and exists(ahead, BATCH):
                        maxima(ahead, of // 2)
                        if of // 2 % (2 * QT) == 2 * QT - 1:
                            max_parts(ahead, of // (QT * R))
                    if s in MISC and MISC[s][0] in ("nmaxT", "turn", "o", "q", "k") and present(t, *MISC[s]):
                        misc(t, par, half, s)

            steps(dve, FIRST_ROUND, ROUNDS, LOOP[0], LOOP[1], round_)

        def pool_attention(pool):
            for t in range(BATCH + 1):
                if t < BATCH:
                    pool_gather(pool, 0, t)
                if t:
                    pool_rstd(pool, at, t - 1, (t - 1) % 2)

        def sp_attention(sp):
            def stack(b, par, g):
                if g == 0:
                    sp.wait_ge(qk_out, 16 * QK_PARTS * (b + 1))
                    alone(sp)
                if not isinstance(b, int) or b > 0:
                    sp.wait_ge(at["st_ps"], STEPS * (b - 1) + QT * R * (g + 1))
                    alone(sp)
                sp.dma_start(q_st[0:MAX_ROW, g, :].bitcast(F32),
                             q_dram[par][R * g:R * (g + 1)].rearrange("r x n -> (r x) n")).then_inc(stack_in[g], 16)
                sp.dma_start(q_st[MAX_ROW:P, g, :].bitcast(F32), zero_dram).then_inc(stack_in[g], 16)
                for r in range(R):
                    sp.dma_start(k_st[HK * r:HK * (r + 1), g, r, :].bitcast(F32), k_dram[par][R * g + r])\
                      .then_inc(stack_in[g], 16)

            def maxima(b, g):
                n = G * b + g
                sp.wait_ge(at["nmaxT"], n + 1)
                alone(sp)
                sp.dma_start(nmax_dram[g].rearrange("a (q p) -> (a q) p", p=P), nmaxT[:, :].bitcast(F32))\
                  .then_inc(nmax_out, 16)
                sp.wait_ge(nmax_out, 16 * (n + 1))
                alone(sp)
                sp.dma_start(q_st[MAX_ROW:MAX_ROW + 2 * R, g, :].bitcast(F32), nmax_dram[g]).then_inc(nmax_in[g], 16)

            def parts(b, par):
                for i, (what, to, order) in enumerate((("q", q_dram[par], (qk_hi, qk_hi, qk_lo)),
                                                       ("k", k_dram[par], (qk_lo, qk_hi, qk_hi)))):
                    sp.wait_ge(at[what], b + 1)
                    alone(sp)
                    for x in range(3):
                        sp.dma_start(to[:, HD * x:HD * (x + 1), :], order[x][:, i, :].bitcast(F32)).then_inc(qk_out, 16)

            def round_(t, par, half):
                for g in range(G):
                    b, of = (t, g + 3) if g == 0 else (t + 1, g - 1)
                    if exists(b, BATCH):
                        stack(b, par if g == 0 else 1 - par, of)
                    b, of = (t, g + 1) if g + 1 < G else (t + 1, 0)
                    if exists(b, BATCH):
                        maxima(b, of)
                if exists(t + 2, BATCH):
                    parts(t + 2, par)

            sp.wait_ge(at["init"], G)
            for r in range(R):
                row = MAX_ROW + 2 * r
                sp.dma_start(k_st[row:row + 2, :, r, :].bitcast(F32), probs[0:2 * G, 4, :])\
                  .then_inc(stack_const, 16)
            steps(sp, FIRST_ROUND, ROUNDS, LOOP[0], LOOP[1], round_)

        @block.sync
        def _(sp):
            sp.dma_start(X[:, :, :], x_rows.rearrange("(t p) d -> p t d", p=P)).then_inc(x_loaded, 16)
            column = lambda v: v.rearrange("(p o) -> p o", o=1)
            row = lambda v: v.rearrange("(o n) -> o n", o=1)
            loads = [(wg[:, :], Wg), (ws1_raw, Ws1), (ws2_raw, Ws2.rearrange("(p c) d -> p (c d)", c=FC)),
                     (bs1_col[:, :], bs1.rearrange("(p c) -> p c", c=FC)), (bs2_col[:, :], column(bs2)),
                     (b1_col[:, :].rearrange("p (e c) -> p e c", c=FC), b1.rearrange("e (p c) -> p e c", c=FC)),
                     (b2_col[:, :], b2.rearrange("e d -> d e")),
                     (wq[:, :], Wq), (wk[:, :], Wk), (wv[:, :], Wv), (wo[:, :], Wo),
                     (bq_col[:, :], column(bq)), (bk_col[:, :], column(bk)), (bv_row[:, :], row(bv)),
                     (bo_row[:, :], row(bo))]
            assert len(loads) == LOADS
            for to, of in loads:
                sp.dma_start(to, of, allow_slow_non_contiguous=True).then_inc(const_in, 16)
            sp.wait_ge(dve_const, 1)
            zero_rows = xs.rearrange("(z p s) d -> z p (s d)", p=P, s=2048 // D)
            for z in range(SLOTS * D // P // 2048):
                sp.dma_start(zero_rows[z], probs[:, 0:4, :].rearrange("p a n -> p (a n)")).then_inc(xs_zero, 16)
            sp.dma_start(zero_dram, probs[MAX_ROW:P, 0, :]).then_inc(stack_const, 16)
            sp_blocks(sp, ex[0], 0, NEX)
            sp_attention(sp)
            sp_blocks(sp, ex[1], 1, NEX)
            for b in range(BATCH):
                sp.wait_ge(rt[1]["combined"], 2 * QT * (b + 1))
                sp.dma_start(out_rows[b * SEQ:(b + 1) * SEQ, :].rearrange("(t p) d -> p t d", p=P),
                             X[:, b * QT:(b + 1) * QT, :]).then_inc(out_done, 16)
            sp.wait_ge(out_done, 16 * BATCH)

        @block.gpsimd
        def _(pool):
            pool.memset(ident[:, :], 0.0).then_inc(pool_const, 1)
            pool.memset(ones_bf[:, :], 1.0).then_inc(pool_const, 1)
            pool.memset(neg_half[:, :], -0.5).then_inc(pool_const, 1)
            pool.iota(iota_e[:, :], [[1, E]], 0, 0, allow_small_or_imprecise_dtypes=True).then_inc(pool_const, 1)
            pool.iota(iota_b[:, :], [[1, NEX]], 0, 0, allow_small_or_imprecise_dtypes=True).then_inc(pool_const, 1)
            pool.wait_ge(pool_const, 5)
            pool.affine_select(out=ident[:, :], in_=ident[:, :], compare_op=ALU.not_equal, fill=1.0,
                               base=0, pattern=[[-1, P]], channel_multiplier=1).then_inc(pool_const, 1)
            pool.affine_select(out=before_bf[:, :], in_=ones_bf[:, :], compare_op=ALU.is_gt, fill=0.0,
                               base=0, pattern=[[1, P]], channel_multiplier=-1).then_inc(pool_const, 1)
            pool_route(pool, 0)
            pool_scatter(pool, 0)
            pool_weights(pool, ex[0], NEX)
            pool_attention(pool)
            pool_route(pool, 1)
            pool_scatter(pool, 1)
            pool_weights(pool, ex[1], NEX)
            for b in range(BATCH):
                pool_gather(pool, 1, b)

        @block.vector
        def _(dve):
            dve.memset(probs[:, 0:4, :], 0.0).then_inc(dve_const, 1)
            dve.memset(scan_one[:, :], 1.0).then_inc(dve_const, 1)
            dve.memset(ones_row[:, :], 1.0).then_inc(dve_const, 1)
            dve.memset(v_st[:, :, :, :, :], 0.0).then_inc(dve_const, 1)
            dve.wait_ge(dve_const, 4)
            dve.memset(v_st[:, :, :, :, HD], 1.0).then_inc(dve_const, 1)
            dve.wait_ge(const_in, 16 * LOADS)
            dve.tensor_copy(wg_hi[:, :], wg[:, :]).then_inc(dve_const, 1)
            dve.tensor_copy(ws1_hi[:, :, :], ws1_raw.rearrange("d (p c) -> d c p", c=FC)).then_inc(dve_const, 1)
            dve.tensor_copy(ws2_hi[:, :, :].rearrange("p c d -> p (c d)"), ws2_raw).then_inc(dve_const, 1)
            dve.tensor_scalar(bqs_col[:, :], bq_col[:, :], SCALE, None, ALU.mult).then_inc(dve_const, 1)
            dve.memset(probs[:, 4, :], 1.0).then_inc(dve_const, 1)
            dve.wait_ge(dve_const, 10)
            dve.tensor_tensor(wg_lo[:, :], wg[:, :], wg_hi[:, :].bitcast(F32), ALU.subtract).then_inc(dve_const, 1)
            dve.tensor_tensor(ws1_lo[:, :, :], ws1_raw.rearrange("d (p c) -> d c p", c=FC),
                              ws1_hi[:, :, :].bitcast(F32), ALU.subtract).then_inc(dve_const, 1)
            dve.tensor_tensor(ws2_lo[:, :, :].rearrange("p c d -> p (c d)"), ws2_raw,
                              ws2_hi[:, :, :].rearrange("p c d -> p (c d)").bitcast(F32), ALU.subtract)\
               .then_inc(dve_const, 1)
            dve.wait_ge(pool_const, 7)
            dve_route(dve, 0)
            dve_blocks(dve, sh[0], NSH, False)
            dve_blocks(dve, ex[0], NEX, True)
            dve_attention(dve)
            dve_route(dve, 1)
            dve_blocks(dve, sh[1], NSH, False)
            dve_blocks(dve, ex[1], NEX, True)
            for b in range(BATCH):
                dve_combine(dve, rt[1], b, b % 2, b // 2, b)

        @block.scalar
        def _(act):
            act.wait_ge(const_in, 16 * LOADS)
            act_route(act, 0)
            act_blocks(act, sh[0], 0, NSH, False)
            act_blocks(act, ex[0], 0, NEX, True)
            act.wait_ge(dve_const, DVE_CONSTS)
            act_attention(act)
            act_route(act, 1)
            act_blocks(act, sh[1], 1, NSH, False)
            act_blocks(act, ex[1], 1, NEX, True)

        @block.tensor
        def _(pe):
            pe.wait_ge(pool_const, 7)
            pe.wait_ge(dve_const, DVE_CONSTS)
            pe_route(pe, 0)
            pe_blocks(pe, sh[0], NSH, False)
            pe_blocks(pe, ex[0], NEX, True)
            pe_attention(pe)
            pe_route(pe, 1)
            pe_blocks(pe, sh[1], NSH, False)
            pe_blocks(pe, ex[1], NEX, True)


LOADS = 15
DVE_CONSTS = 13

_INS = ["L0_attn_x", "L0_attn_Wq", "L0_attn_bq", "L0_attn_Wk", "L0_attn_bk", "L0_attn_Wv", "L0_attn_bv",
        "L0_attn_Wo", "L0_attn_bo", "L0_ffn_Wg", "L0_ffn_W1", "L0_ffn_b1", "L0_ffn_W2", "L0_ffn_b2",
        "L0_ffn_Ws1", "L0_ffn_bs1", "L0_ffn_Ws2", "L0_ffn_bs2"]


def kernel(**inputs):
    import numpy as _np
    import concourse.bacc as _bacc
    from concourse import mybir as _mybir
    from concourse.bass_utils import run_bass_kernel_spmd as _run

    nc = _bacc.Bacc("TRN2", target_bir_lowering=False, num_devices=1)
    arrays, args = {}, []
    for name in _INS:
        a = _np.ascontiguousarray(inputs[name])
        arrays[f"in_{name}_dram"] = a
        args.append(nc.dram_tensor(f"in_{name}_dram", a.shape, _mybir.dt.from_np(a.dtype), kind="ExternalInput").ap())
    shape = inputs["L0_attn_x"].shape
    args.append(nc.dram_tensor("out_0_dram", shape, _mybir.dt.float32, kind="ExternalOutput").ap())
    macaron(nc, *args)
    r = _run(nc, [arrays], core_ids=[0])
    return r.results[0]["out_0_dram"]
```

```python
from contextlib import ExitStack

import concourse.bass as bass
from concourse import mybir

F32 = mybir.dt.float32
F32R = mybir.dt.float32r
BF16 = mybir.dt.bfloat16
U32 = mybir.dt.uint32
I32 = mybir.dt.int32
ALU = mybir.AluOpType
ACT = mybir.ActivationFunctionType
AX = mybir.AxisListType

P = 128


def wait(eng, sem, value):
    if not isinstance(value, int) or value > 0:
        eng.wait_ge(sem, value)


def exists(k, count):
    return not isinstance(k, int) or 0 <= k < count


def steps(eng, first, last, loop_from, loop_to, body):
    for k in range(first, loop_from):
        body(k, k % 2, k // 2)
    if loop_to > loop_from:
        with eng.Fori(loop_from // 2, loop_to // 2) as i:
            for par in range(2):
                body(i * 2 + par, par, i)
    for k in range(loop_to, last):
        body(k, k % 2, k // 2)


def macaron(nc, x_in, Wq, bq, Wk, bk, Wv, bv, Wo, bo, Wg, W1, b1, W2, b2, Ws1, bs1, Ws2, bs2, out):
    BATCH, SEQ, D = x_in.shape
    E, _, F = W1.shape
    H = 16
    HD = D // H
    SCALE = 1.0 / float(HD) ** 0.5
    TOP = 2
    T = BATCH * SEQ
    NT = T // P
    QT = SEQ // P
    BLK = 512
    SUB = BLK // P
    FC = F // P
    NSH = T // BLK
    NEX = TOP * T // BLK + E
    REGION = T + BLK
    PAD = E * REGION
    PAD_BLOCKS = NEX - TOP * T // BLK
    ROWS = PAD + PAD_BLOCKS * BLK
    LOGBLK = BLK.bit_length() - 1
    G = 4
    R = H // G
    RP = P // R
    assert D == P and SEQ == BLK and E == 8 and G * R == H

    x_rows = x_in.rearrange("b s d -> (b s) d")
    out_rows = out.rearrange("b s d -> (b s) d")

    xs = nc.dram_tensor("sorted_rows", (ROWS, D), F32, kind="Internal").ap()
    ys = nc.dram_tensor("expert_rows", (NEX * BLK, D), F32, kind="Internal").ap()
    HK = 3 * HD
    q_dram, k_dram = [[nc.dram_tensor(f"{n}_stacks_{par}", (H, HK, SEQ), F32, kind="Internal").ap()
                       for par in range(2)] for n in ("q", "k")]
    zero_rows = xs[PAD:PAD + BLK, :]
    nmax_dram = [nc.dram_tensor(f"neg_max_{g}", (R * 2, QT * P), F32, kind="Internal").ap() for g in range(G)]

    ctx = ExitStack()
    with ctx:
        def sb(name, shape, dt=F32):
            return ctx.enter_context(nc.sbuf_tensor("sb_" + name, shape, dt))

        def sem(name):
            return ctx.enter_context(nc.semaphore(name))

        def sem2(name):
            return [sem(f"{name}_{i}") for i in range(2)]

        ident = sb("ident", [P, P])
        ones_bf = sb("ones_bf", [P, P], BF16)
        before_bf = sb("before_bf", [P, P], BF16)
        iota_e = sb("iota_e", [P, E])
        iota_b = sb("iota_b", [1, NEX])
        neg_half = sb("neg_half", [P, QT])
        scan_one = sb("scan_one", [P, E]); region_start = sb("region_start", [P, E])
        wq = sb("wq", [P, D]); wk = sb("wk", [P, D]); wv = sb("wv", [P, D]); wo = sb("wo", [P, D])
        bq_col = sb("bq_col", [P, 1]); bk_col = sb("bk_col", [P, 1]); bqs_col = sb("bqs_col", [P, 1])
        bv_col = sb("bv_col", [P, 1]); bo_rows = sb("bo_rows", [P, D])
        wg = sb("wg", [P, E]); wg_hi = sb("wg_hi", [P, E], F32R); wg_lo = sb("wg_lo", [P, E], F32R)
        b1_col = sb("b1_col", [P, E * FC]); b2_col = sb("b2_col", [P, E])
        bs1_col = sb("bs1_col", [P, FC]); bs2_col = sb("bs2_col", [P, 1])

        X = sb("X", [P, NT, D])
        xn = sb("xn", [P, NT, D])
        bn = sb("bn", [P, 2, 2, QT, 6]); mv = sb("mv", [P, 2, 2, QT, 2])
        vare = sb("vare", [P, 2, QT]); rstd = sb("rstd", [P, 2, 2, QT])

        xT = sb("xT", [P, 2 * NSH, BLK], F32R)
        xT_hi, xT_lo = xT[:, 0:NSH, :], xT[:, NSH:2 * NSH, :]
        logits = sb("logits", [P, QT, E]); top_v = sb("top_v", [P, QT, E]); top_i = sb("top_i", [P, QT, E], U32)
        top_f = sb("top_f", [P, NT, 2]); gap = sb("gap", [P, NT]); gate = sb("gate", [P, 2, NT])
        hot = sb("hot", [P, QT, 2, E]); hot_bf = sb("hot_bf", [P, QT, E], BF16)
        next_row = sb("next_row", [P, E])
        row = sb("row", [P, QT, E]); row_f = sb("row_f", [P, NT, 2])
        row_i = sb("row_i", [P, NT, 2], U32); result_i = sb("result_i", [P, NT, 2], U32)
        shift = sb("shift", [P, E])
        size = sb("size", [P, E]); size_i = sb("size_i", [1, E], I32)
        blocks_i = sb("blocks_i", [P, E], I32); blocks = sb("blocks", [P, E]); blocks_upto = sb("blocks_upto", [P, E])
        unused = sb("unused", [1, E]); blk_cmp = sb("blk_cmp", [1, NEX, E]); blk_f = sb("blk_f", [1, NEX])
        blk_e = sb("blk_e", [1, NEX], I32); blk_at = sb("blk_at", [1, NEX], I32)

        w1_raw = sb("w1_raw", [P, 2, F]); w2_raw = sb("w2_raw", [P, 2, F])
        w1_hi = sb("w1_hi", [P, 2, FC, P], F32R); w1_lo = sb("w1_lo", [P, 2, FC, P], F32R)
        w2_hi = sb("w2_hi", [P, 2, FC, P], F32R); w2_lo = sb("w2_lo", [P, 2, FC, P], F32R)
        x_rows_sb = sb("x_rows", [P, 2, SUB, D])
        ws1_raw = w1_raw[:, 1]; ws2_raw = w2_raw[:, 1]
        ws1_hi = sb("ws1_hi", [P, FC, P], F32R); ws1_lo = sb("ws1_lo", [P, FC, P], F32R)
        ws2_hi = sb("ws2_hi", [P, FC, P], F32R); ws2_lo = sb("ws2_lo", [P, FC, P], F32R)
        xb = sb("xb", [P, 4, BLK], F32R)
        xb_hi, xb_lo = xb[:, 0:2, :], xb[:, 2:4, :]
        h_hi = sb("h_hi", [P, FC, BLK], F32R); h_lo = sb("h_lo", [P, FC, BLK], F32R)
        yT = sb("yT", [P, 2, BLK]); y_rows = sb("y_rows", [P, 2, SUB, D])
        xa = x_rows_sb
        xr = y_rows
        xrT_hi, xrT_lo = (w1_hi[:, p, :, :].rearrange("p c n -> p (c n)") for p in range(2))
        picked = sb("picked", [P, 2, QT, 2, D])
        of_expert = picked[:, :, :, :, :].rearrange("p a b c d -> p (a b c d)")[:, 0:NT * 2 * E]\
            .rearrange("p (t e) -> p t e", e=E)

        q_st = xb
        k_st = xT[:, :, :].rearrange("p (g r) n -> p g r n", r=R)
        MAX_ROW = R * HK
        v_st = sb("v_st", [P, 2, QT, G * R, RP])
        qk_hi = sb("qk_hi", [P, 2, SEQ], F32R); qk_lo = sb("qk_lo", [P, 2, SEQ], F32R)
        xnT = sb("xnT", [P, SEQ])
        RING = 8
        probs = sb("probs", [P, RING, SEQ])
        ctx_raw = sb("ctx_raw", [P, SEQ]); rden = sb("rden", [P, QT, R])
        ctx_n = sb("ctx_n", [P, QT, D]); ctxT = sb("ctxT", [P, SEQ])
        nmax = sb("nmax", [P, 2, R, QT]); nmax_parts = sb("nmax_parts", [P, 2, R, 2, QT])
        nmaxT = sb("nmaxT", [R * 2 * QT, P], F32R)

        bank = ctx.enter_context(nc.psum_tensor("banks", [P, 8, BLK], F32))

        const_in = sem("const_in"); aside = sem("aside"); x_first = sem("x_first"); x_loaded = sem("x_loaded")
        wg_in = sem("wg_in"); wg_parts = sem("wg_parts")
        pool_const = sem("pool_const"); dve_const = sem("dve_const"); pads_zero = sem("pads_zero")
        out_done = sem("out_done")

        def sems(tag, names):
            return {n: sem(f"{n}_{tag}") for n in names.split()}

        rt, sh, ex = [], [], []
        for f in range(2):
            s = sems(f"route{f}", "stats mv var rstd xn xT_ps xT_hi xT_lo logit_ps logits maths hot count_ps counted "
                                  "rows results gap exp blk filled combined")
            s["picked"] = sem2(f"picked_{f}"); s["scattered"] = sem2(f"scattered_{f}")
            rt.append(s)
            for kind, group in (("shared", sh), ("expert", ex)):
                s = sems(f"{kind}{f}", "h_ps relu h_hi h_lo h_used yT rows_ps rows")
                if kind == "expert":
                    s |= sems(f"{kind}{f}", "w1_hi w1_lo w2_hi w2_lo x_ps x_hi x_lo")
                    s["loaded"] = sem2(f"loaded_{kind}{f}")
                    s["stored"] = sem2(f"stored_{kind}{f}")
                group.append(s)
        at = sems("att", "init biased stats mv var rstd xn nmax_parts s_ps s_read st_ps probs pv_ps ctx_raw rden "
                         "nmaxT_ps nmaxT turn_ps turned ctxT_ps ctxT o_ps added v_ps v xT_ps xT q_ps q k_ps k "
                         "qk_z qk_hi")
        kept = sem("kept")
        nmax_out = sem("nmax_out")
        nmax_in = sem2("nmax_in")
        qk_out = sem("qk_out"); stack_const = sem("stack_const")
        stack_in = sem2("stack_in")

        block = ctx.enter_context(nc.Block())

        def alone(eng):
            eng.sem_inc(aside, 1)

        H_BANK, O_BANK, T_BANK, Y_BANK = 0, 4, 6, 7
        LOGIT_BANK, COUNT_BANK = T_BANK, Y_BANK

        def pe_turn(pe, s, t, rows, to):
            for j in range(SUB):
                mm = pe.transpose(to[:, j * P:(j + 1) * P], rows[:, j, :], ident[:, :])
            mm.then_inc(s["xT_ps"], 1)

        def pe_turn_all(pe, s, before):
            pe.wait_ge(before["rows"], NEX)
            for t in range(NSH):
                pe.wait_ge(s["xT_lo"], NSH + t - 1)
                pe_turn(pe, s, t, xn[:, SUB * t:SUB * (t + 1), :], bank[:, t % 2, :])
            pe.wait_ge(s["xT_lo"], 2 * NSH)

        def pe_logits(pe, s, o, xT_hi, xT_lo):
            for j in range(SUB):
                oj, xh, xl = o[:, j * E:(j + 1) * E], xT_hi[:, j * P:(j + 1) * P], xT_lo[:, j * P:(j + 1) * P]
                pe.matmul(oj, xh, wg_hi[:, :], start=True, stop=False)
                pe.matmul(oj, xh, wg_lo[:, :], start=False, stop=False)
                mm = pe.matmul(oj, xl, wg_hi[:, :], start=False, stop=True)
            mm.then_inc(s["logit_ps"], 1)

        def pe_count(pe, s, o):
            for j in range(QT):
                for i in range(j):
                    pe.matmul(o[:, j * E:(j + 1) * E], ones_bf[:, :], hot_bf[:, i, :], start=i == 0, stop=False)
                pe.matmul(o[:, j * E:(j + 1) * E], before_bf[:, :], hot_bf[:, j, :], start=j == 0, stop=True)
            for j in range(QT):
                mm = pe.matmul(o[:, QT * E:(QT + 1) * E], ones_bf[:, :], hot_bf[:, j, :], start=j == 0, stop=j == QT - 1)
            mm.then_inc(s["count_ps"], 1)

        def pe_route(pe):
            s = rt[0]
            for t in range(-1, NSH):
                if t + 1 < NSH:
                    pe.wait_ge(s["xn"], SUB * (t + 2))
                    wait(pe, s["xT_lo"], t)
                    pe_turn(pe, s, t + 1, xn[:, SUB * (t + 1):SUB * (t + 2), :], bank[:, (t + 1) % 2, :])
                if t >= 0:
                    pe.wait_ge(s["hot"], t + 1)
                    wait(pe, s["counted"], t)
                    pe_count(pe, s, bank[:, COUNT_BANK, :])
                if t + 1 < NSH:
                    pe.wait_ge(s["xT_lo"], t + 2)
                    wait(pe, s["logits"], t + 1)
                    pe_logits(pe, s, bank[:, LOGIT_BANK, :], xT_hi[:, t + 1, :], xT_lo[:, t + 1, :])

        def pe_blocks(pe, s, count, routed):
            def product(o, wh, wl, xh, xl, first, last):
                pe.matmul(o, wh, xh, start=first, stop=False)
                pe.matmul(o, wh, xl, start=False, stop=False)
                return pe.matmul(o, wl, xh, start=False, stop=last)

            def turn_x(k, par, half):
                pe.wait_ge(s["loaded"][par], 48 * (half + 1))
                wait(pe, s["x_lo"], k)
                for j in range(SUB):
                    mm = pe.transpose(bank[:, T_BANK, j * P:(j + 1) * P], x_rows_sb[:, par, j, :], ident[:, :])
                mm.then_inc(s["x_ps"], 1)

            def hidden(k, par, c):
                if routed:
                    wh, wl, xh, xl = w1_hi[:, par, c, :], w1_lo[:, par, c, :], xb_hi[:, par, :], xb_lo[:, par, :]
                    if c == 0:
                        pe.wait_ge(s["w1_lo"], k + 1)
                        pe.wait_ge(s["x_lo"], k + 1)
                else:
                    kk = k if isinstance(k, int) else None
                    at_k = slice(k, k + 1) if kk is not None else bass.ds(k, 1)
                    wh, wl = ws1_hi[:, c, :], ws1_lo[:, c, :]
                    xh = xT_hi[:, at_k, :].rearrange("p o n -> p (o n)")
                    xl = xT_lo[:, at_k, :].rearrange("p o n -> p (o n)")
                wait(pe, s["h_lo"], FC * (k - 1) + c + 1)
                product(bank[:, H_BANK + c, :], wh, wl, xh, xl, True, True).then_inc(s["h_ps"], 1)

            def output(k, par, c):
                if routed:
                    wh, wl = w2_hi[:, par, c, :], w2_lo[:, par, c, :]
                    if c == 0:
                        pe.wait_ge(s["w2_lo"], k + 1)
                else:
                    wh, wl = ws2_hi[:, c, :], ws2_lo[:, c, :]
                if c == 0:
                    wait(pe, s["yT"], k - 1)
                pe.wait_ge(s["h_lo"], FC * k + c + 1)
                product(bank[:, O_BANK + par, :], wh, wl, h_hi[:, c, :], h_lo[:, c, :],
                        c == 0, c == FC - 1).then_inc(s["h_used"], 1)

            def turn_y(k, par):
                pe.wait_ge(s["yT"], k + 1)
                wait(pe, s["rows"], k)
                for j in range(SUB):
                    mm = pe.transpose(bank[:, Y_BANK, j * P:(j + 1) * P], yT[:, par, j * P:(j + 1) * P], ident[:, :])
                mm.then_inc(s["rows_ps"], 1)

            def body(k, par, half):
                for c in range(FC):
                    if exists(k, count):
                        hidden(k, par, c)
                    if exists(k - 1, count):
                        output(k - 1, 1 - par, c)
                    if c == 1 and routed and exists(k + 1, count):
                        turn_x(k + 1, 1 - par, half + par)
                    if c == 2 and exists(k - 2, count):
                        turn_y(k - 2, par)

            if routed:
                turn_x(0, 0, 0)
            steps(pe, 0, count + 2, 2, count - 2, body)

        def act_turned(act, s, before):
            for t in range(NSH):
                act.wait_ge(s["xT_ps"], before + t + 1)
                act.activation(xT_hi[:, t, :], bank[:, t % 2, :], ACT.Copy).then_inc(s["xT_hi"], 1)

        def act_gates(act, s):
            act.wait_ge(s["counted"], NSH)
            act.activation(gap[:, :], gap[:, :], ACT.Exp).then_inc(s["exp"], 1)

        def act_blocks(act, s, f, count, routed):
            def expert(k):
                at_k = slice(k, k + 1) if isinstance(k, int) else bass.ds(k, 1)
                return act.value_load(blk_e[0:1, at_k], min_val=0, max_val=E - 1)

            def x_hi(k, par):
                act.wait_ge(s["x_ps"], k + 1)
                wait(act, s["h_ps"], FC * (k - 1))
                act.activation(xb_hi[:, par, :], bank[:, T_BANK, :], ACT.Copy).then_inc(s["x_hi"], 1)

            def relu(k, c, e):
                bias = bs1_col[:, c:c + 1] if e is None else b1_col[:, bass.ds(e * FC + c, 1)]
                act.wait_ge(s["h_ps"], FC * k + c + 1)
                act.activation(bank[:, H_BANK + c, :], bank[:, H_BANK + c, :], ACT.Relu, bias=bias)\
                   .then_inc(s["relu"], 1)

            def hi(k, c):
                act.wait_ge(s["relu"], FC * k + c + 1)
                wait(act, s["h_used"], FC * (k - 1) + c + 1)
                act.activation(h_hi[:, c, :], bank[:, H_BANK + c, :], ACT.Copy).then_inc(s["h_hi"], 1)

            def y(k, par):
                e = expert(k) if routed else None
                bias = bs2_col[:, 0:1] if e is None else b2_col[:, bass.ds(e, 1)]
                act.wait_ge(s["h_used"], FC * (k + 1))
                wait(act, s["rows_ps"], k - 1)
                act.activation(yT[:, par, :], bank[:, O_BANK + par, :], ACT.Identity, bias=bias)\
                   .then_inc(s["yT"], 1)

            def body(k, par, half):
                if exists(k, count):
                    e = expert(k) if routed else None
                    for c in range(FC):
                        relu(k, c, e)
                        if c == 1 and routed and exists(k + 1, count):
                            x_hi(k + 1, 1 - par)
                        hi(k, c)
                if exists(k - 1, count):
                    y(k - 1, 1 - par)

            if routed:
                act.wait_ge(rt[f]["blk"], 1)
                x_hi(0, 0)
            steps(act, 0, count + 1, 2, count - 2, body)

        def tile(k, j=0):
            return slice(k + j, k + j + 1) if isinstance(k, int) else bass.ds(k + j, 1)

        def kind(s):
            return 1 if s is at else 0

        def entry(b):
            return slice(b * QT, (b + 1) * QT) if isinstance(b, int) else bass.ds(b * QT, QT)

        def dve_stats(dve, s, t, par, j):
            if j == 0:
                alone(dve)
            dve.bn_stats(bn[:, kind(s), par, j, :], X[:, tile(t * QT, j), :].rearrange("p o d -> p (o d)"))\
               .then_inc(s["stats"], 1)

        def dve_aggregate(dve, s, t, par):
            dve.wait_ge(s["stats"], QT * (t + 1))
            wait(dve, s["xn"], QT * (t - 1))
            alone(dve)
            for j in range(QT):
                dve.bn_aggr(mv[:, kind(s), par, j, :], bn[:, kind(s), par, j, :]).then_inc(s["mv"], 1)

        def pool_rstd(pool, s, t, par):
            k = kind(s)
            pool.wait_ge(s["mv"], QT * (t + 1))
            wait(pool, s["rstd"], t)
            pool.tensor_scalar(vare[:, k, :], mv[:, k, par, :, 1], 1e-5, None, ALU.add).then_inc(s["var"], 1)
            pool.wait_ge(s["var"], t + 1)
            pool.tensor_tensor(rstd[:, k, par, :], vare[:, k, :], neg_half[:, :], ALU.pow).then_inc(s["rstd"], 1)

        def dve_norm(dve, s, t, par, to, j):
            k = kind(s)
            if j == 0:
                dve.wait_ge(s["rstd"], t + 1)
            dve.tensor_scalar(to[:, j, :], X[:, tile(t * QT, j), :].rearrange("p o d -> p (o d)"),
                              mv[:, k, par, j, 0:1], rstd[:, k, par, j:j + 1], ALU.subtract, ALU.mult)\
               .then_inc(s["xn"], 1)

        def wide(ap, n, axis):
            shape = list(ap.shape)
            return ap.unsqueeze(axis).to_broadcast(shape[:axis] + [n] + shape[axis:])

        TOP_STEPS, MATHS = 6, 2 * QT + 6
        MATHS_ALL = MATHS * NSH

        def dve_top(dve, s, b, o, i):
            at_b, done = entry(b), MATHS * b
            if i == 0:
                dve.wait_ge(s["logit_ps"], b + 1)
                dve.tensor_copy(logits[:, :, :].rearrange("p t e -> p (t e)"), o[:, 0:QT * E]).then_inc(s["logits"], 1)
            elif i == 1:
                dve.wait_ge(s["logits"], b + 1)
                alone(dve)
                for j in range(QT):
                    dve.max(top_v[:, j, :], logits[:, j, :]).then_inc(s["maths"], 1)
            elif i == 2:
                dve.wait_ge(s["maths"], done + QT)
                alone(dve)
                for j in range(QT):
                    dve.max_index(top_i[:, j, :], top_v[:, j, :], logits[:, j, :]).then_inc(s["maths"], 1)
            elif i == 3:
                dve.wait_ge(s["maths"], done + 2 * QT)
                dve.tensor_tensor(gap[:, at_b], top_v[:, :, 1], top_v[:, :, 0], ALU.subtract).then_inc(s["maths"], 1)
                dve.tensor_copy(top_f[:, at_b, :], top_i[:, :, 0:2]).then_inc(s["maths"], 1)
            elif i == 4:
                dve.wait_ge(s["maths"], done + 2 * QT + 2)
                dve.tensor_tensor(hot[:, :, :, :].rearrange("p t j e -> p (t j) e"), wide(iota_e[:, :], 2 * QT, 1),
                                  wide(top_f[:, at_b, :].rearrange("p t j -> p (t j)"), E, 2), ALU.is_equal)\
                   .then_inc(s["maths"], 1)
            elif i == 5:
                dve.wait_ge(s["maths"], done + 2 * QT + 3)
                dve.tensor_tensor(hot_bf[:, :, :], hot[:, :, 0, :], hot[:, :, 1, :], ALU.add).then_inc(s["hot"], 1)

        PLACE_STEPS = 4

        def dve_place(dve, s, b, o, i):
            done = MATHS * b + 2 * QT + 3
            if i == 0:
                dve.wait_ge(s["count_ps"], b + 1)
                dve.tensor_tensor(row[:, :, :], o[:, 0:QT * E].rearrange("p (t e) -> p t e", e=E),
                                  wide(next_row[:, :], QT, 1), ALU.add).then_inc(s["maths"], 1)
                dve.wait_ge(s["maths"], done + 1)
                dve.tensor_tensor(next_row[:, :], next_row[:, :], o[:, QT * E:(QT + 1) * E], ALU.add)\
                   .then_inc(s["counted"], 1)
            elif i == 1:
                dve.wait_ge(s["counted"], b + 1)
                dve.tensor_tensor(hot[:, :, :, :], hot[:, :, :, :], wide(row[:, :, :], 2, 2), ALU.mult)\
                   .then_inc(s["maths"], 1)
            elif i == 2:
                dve.wait_ge(s["maths"], done + 2)
                dve.tensor_reduce(row_f[:, entry(b), :], hot[:, :, :, :], AX.X, ALU.add).then_inc(s["maths"], 1)
            elif i == 3:
                dve.wait_ge(s["maths"], done + 3)
                dve.tensor_copy(row_i[:, entry(b), :], row_f[:, entry(b), :]).then_inc(s["rows"], 1)

        def dve_blocks_of(dve, s):
            done = MATHS_ALL

            def then(op):
                nonlocal done
                op.then_inc(s["maths"], 1)
                done += 1
                dve.wait_ge(s["maths"], done)

            dve.wait_ge(s["counted"], NSH)
            then(dve.tensor_tensor(size[:, :], next_row[:, :], region_start[:, :], ALU.subtract))
            then(dve.tensor_copy(size_i[:, :], size[0:1, :]))
            then(dve.tensor_scalar(blocks_i[:, :], size[:, :], float(BLK - 1), None, ALU.add))
            then(dve.tensor_scalar(blocks_i[:, :], blocks_i[:, :], LOGBLK, None, ALU.logical_shift_right))
            then(dve.tensor_copy(blocks[:, :], blocks_i[:, :]))
            then(dve.tensor_tensor_scan(blocks_upto[:, :], scan_one[:, :], blocks[:, :], 0.0, ALU.mult, ALU.add))
            then(dve.tensor_tensor(blk_cmp[:, :, :], wide(blocks_upto[0:1, :], NEX, 1), wide(iota_b[:, :], E, 2), ALU.is_le))
            then(dve.tensor_reduce(blk_f[:, :], blk_cmp[:, :, :], AX.X, ALU.add))
            then(dve.tensor_scalar(blk_e[:, :], blk_f[:, :], float(E - 1), None, ALU.min))
            then(dve.tensor_scalar(unused[:, :], blocks[0:1, :], -1.0, float(REGION // BLK), ALU.mult, ALU.add))
            then(dve.tensor_tensor(blk_cmp[:, :, :], blk_cmp[:, :, :], wide(unused[:, :], NEX, 1), ALU.mult))
            then(dve.tensor_reduce(blk_f[:, :], blk_cmp[:, :, :], AX.X, ALU.add))
            dve.tensor_tensor(blk_at[:, :], blk_f[:, :], iota_b[:, :], ALU.add).then_inc(s["blk"], 1)
            then(dve.tensor_tensor(shift[:, :], blocks_upto[:, :], blocks[:, :], ALU.subtract))
            then(dve.tensor_scalar(shift[:, :], shift[:, :], float(BLK), None, ALU.mult))
            then(dve.tensor_tensor(shift[:, :], shift[:, :], region_start[:, :], ALU.subtract))
            then(dve.tensor_tensor(of_expert, wide(iota_e[:, :], 2 * NT, 1),
                                   wide(top_f[:, :, :].rearrange("p t j -> p (t j)"), E, 2), ALU.is_equal))
            then(dve.tensor_tensor(of_expert, of_expert, wide(shift[:, :], 2 * NT, 1), ALU.mult))
            then(dve.tensor_reduce(top_f[:, :, :].rearrange("p t j -> p (t j)"), of_expert, AX.X, ALU.add))
            dve.wait_ge(s["rows"], NSH)
            dve.tensor_tensor(result_i[:, :, :], row_f[:, :, :], top_f[:, :, :], ALU.add).then_inc(s["results"], 1)

        def dve_gates(dve, s):
            dve.wait_ge(s["exp"], 1)
            dve.tensor_scalar(gate[:, 1, :], gap[:, :], 1.0, 2.0, ALU.add, ALU.mult).then_inc(s["gap"], 1)
            dve.wait_ge(s["gap"], 1)
            dve.reciprocal(gate[:, 0, :], gate[:, 1, :]).then_inc(s["gap"], 1)
            dve.wait_ge(s["gap"], 2)
            dve.tensor_tensor(gate[:, 1, :], gate[:, 0, :], gap[:, :], ALU.mult).then_inc(s["gap"], 1)
            dve.wait_ge(s["gap"], 3)

        def dve_route(dve):
            s = rt[0]
            for t in range(-2, NSH + 1):
                if t == -1:
                    dve.wait_ge(x_loaded, 16)
                if t == 2:
                    dve_shared_weights(dve)
                if t + 2 < NSH:
                    for j in range(QT):
                        dve_stats(dve, s, t + 2, t % 2, j)
                    dve_aggregate(dve, s, t + 2, t % 2)
                if t >= 1:
                    for i in range(PLACE_STEPS):
                        dve_place(dve, s, t - 1, bank[:, COUNT_BANK, :], i)
                if 0 <= t + 1 < NSH:
                    for j in range(QT):
                        dve_norm(dve, s, t + 1, (t + 1) % 2, xn[:, SUB * (t + 1):SUB * (t + 2), :], j)
                if 0 <= t < NSH:
                    for i in range(TOP_STEPS):
                        dve_top(dve, s, t, bank[:, LOGIT_BANK, :], i)
                if 0 <= t + 1 < NSH:
                    dve_xT_lo(dve, s, t + 1)
            dve_blocks_of(dve, s)
            dve_gates(dve, s)

        def dve_shared_weights(dve):
            dve.wait_ge(const_in, 16 * LOADS)
            dve.tensor_copy(ws1_hi[:, :, :], ws1_raw.rearrange("d (p c) -> d c p", c=FC)).then_inc(dve_const, 1)
            dve.tensor_copy(ws2_hi[:, :, :].rearrange("p c d -> p (c d)"), ws2_raw).then_inc(dve_const, 1)
            dve.tensor_scalar(bqs_col[:, :], bq_col[:, :], SCALE, None, ALU.mult).then_inc(dve_const, 1)
            dve.wait_ge(dve_const, 8)
            dve.tensor_tensor(ws1_lo[:, :, :], ws1_raw.rearrange("d (p c) -> d c p", c=FC),
                              ws1_hi[:, :, :].bitcast(F32), ALU.subtract).then_inc(dve_const, 1)
            dve.tensor_tensor(ws2_lo[:, :, :].rearrange("p c d -> p (c d)"), ws2_raw,
                              ws2_hi[:, :, :].rearrange("p c d -> p (c d)").bitcast(F32), ALU.subtract)\
               .then_inc(dve_const, 1)

        def dve_xT_lo(dve, s, t, before=0):
            dve.wait_ge(s["xT_hi"], before + t + 1)
            dve.tensor_tensor(xT_lo[:, t, :], bank[:, t % 2, :], xT_hi[:, t, :].bitcast(F32), ALU.subtract)\
               .then_inc(s["xT_lo"], 1)

        def dve_blocks(dve, s, count, routed):
            def w1(k, par, half):
                dve.wait_ge(s["loaded"][par], 48 * (half + 1))
                wait(dve, s["h_ps"], FC * (k - 1))
                dve.tensor_copy(w1_hi[:, par, :, :], w1_raw[:, par, :].rearrange("d (p c) -> d c p", c=FC))\
                   .then_inc(s["w1_hi"], 1)

            def w2(k, par, half):
                dve.wait_ge(s["loaded"][par], 48 * (half + 1))
                wait(dve, s["h_used"], FC * (k - 1))
                dve.tensor_copy(w2_hi[:, par, :, :].rearrange("p c d -> p (c d)"), w2_raw[:, par, :])\
                   .then_inc(s["w2_hi"], 1)

            def x_lo(k, par):
                dve.wait_ge(s["x_hi"], k + 1)
                dve.tensor_tensor(xb_lo[:, par, :], bank[:, T_BANK, :], xb_hi[:, par, :].bitcast(F32), ALU.subtract)\
                   .then_inc(s["x_lo"], 1)

            def h_low(k, c):
                dve.wait_ge(s["h_hi"], FC * k + c + 1)
                dve.tensor_tensor(h_lo[:, c, :], bank[:, H_BANK + c, :], h_hi[:, c, :].bitcast(F32), ALU.subtract)\
                   .then_inc(s["h_lo"], 1)

            def rows(k, par, half):
                dve.wait_ge(s["rows_ps"], k + 1)
                if routed:
                    wait(dve, s["stored"][par], 16 * half)
                    dve.tensor_copy(y_rows[:, par, :, :].rearrange("p s d -> p (s d)"), bank[:, Y_BANK, :])\
                       .then_inc(s["rows"], 1)
                else:
                    at_k = slice(k * SUB, (k + 1) * SUB) if isinstance(k, int) else bass.ds(k * SUB, SUB)
                    xk = X[:, at_k, :]
                    dve.scalar_tensor_tensor(xk, bank[:, Y_BANK, :].rearrange("p (s d) -> p s d", d=D), 0.5, xk,
                                             ALU.mult, ALU.add).then_inc(s["rows"], 1)

            def body(k, par, half):
                if exists(k, count):
                    if routed:
                        w2(k, par, half)
                    h_low(k, 0)
                    if routed and exists(k + 1, count):
                        w1(k + 1, 1 - par, half + par)
                    h_low(k, 1)
                    if routed and exists(k + 1, count):
                        x_lo(k + 1, 1 - par)
                    h_low(k, 2)
                    h_low(k, 3)
                if exists(k - 2, count):
                    rows(k - 2, par, half - 1)
                    if s is sh[1]:
                        dve.wait_ge(s["rows"], k - 1)
                        for i in range(2 * QT):
                            dve_combine(dve, rt[1], k - 2, par, half - 1, i)

            if routed:
                w1(0, 0, 0)
                x_lo(0, 0)
            steps(dve, 0, count + 2, 2, count - 2, body)

        def dve_combine(dve, s, t, par, half, i):
            e, j = i // QT, i % QT
            if i == 0:
                dve.wait_ge(s["picked"][par], 16 * 2 * QT * (half + 1))
            x = X[:, tile(t * QT, j), :].rearrange("p o d -> p (o d)")
            if e:
                dve.wait_ge(s["combined"], 2 * QT * t + j + 1)
            dve.scalar_tensor_tensor(x, picked[:, par, j, e, :], gate[:, e, tile(t * QT, j)], x,
                                     ALU.mult, ALU.add).then_inc(s["combined"], 1)
            if i == 2 * QT - 1:
                dve.wait_ge(s["combined"], 2 * QT * (t + 1))

        def pool_scatter(pool, f, b, rows):
            s = rt[f]
            if f == 0 and b == 0:
                pool.wait_ge(pads_zero, 16)
            pool.wait_ge(s["rows"], b + 1)
            for t in range(QT):
                for j in range(2):
                    pool.indirect_dma_start(xs, bass.IndirectOffsetOnAxis(ap=row_i[:, QT * b + t, j:j + 1], axis=0),
                                            rows[:, t, :], None).then_inc(s["scattered"][b % 2], 16)

        def pool_route(pool):
            for t in range(-2, NSH + 1):
                if t + 2 < NSH:
                    pool_rstd(pool, rt[0], t + 2, t % 2)
                if t >= 1:
                    pool_scatter(pool, 0, t - 1, xn[:, QT * (t - 1):QT * t, :])

        def pool_weights(pool, s, count):
            def w1(k, par):
                pool.wait_ge(s["w1_hi"], k + 1)
                pool.tensor_tensor(w1_lo[:, par, :, :], w1_raw[:, par, :].rearrange("d (p c) -> d c p", c=FC),
                                   w1_hi[:, par, :, :].bitcast(F32), ALU.subtract).then_inc(s["w1_lo"], 1)

            def w2(k, par):
                pool.wait_ge(s["w2_hi"], k + 1)
                pool.tensor_tensor(w2_lo[:, par, :, :].rearrange("p c d -> p (c d)"), w2_raw[:, par, :],
                                   w2_hi[:, par, :, :].rearrange("p c d -> p (c d)").bitcast(F32), ALU.subtract)\
                    .then_inc(s["w2_lo"], 1)

            def body(k, par, half):
                w2(k, par)
                if exists(k + 1, count):
                    w1(k + 1, 1 - par)
                if s is ex[0] and isinstance(k, int):
                    if k == 0:
                        pool.wait_ge(sh[0]["h_ps"], FC * NSH)
                    g = k if k < 2 else k - count + 4
                    pool.memset(k_st[:, g, :, :].bitcast(F32), 0.0).then_inc(at["init"], 1)
                    if g == 1:
                        pool.memset(v_st[:, :, :, :, :], 0.0).then_inc(at["init"], 1)
                    if g == 3:
                        pool.wait_ge(at["init"], 4)
                        pool.memset(v_st[:, :, :, :, HD], 1.0).then_inc(at["init"], 1)

            w1(0, 0)
            steps(pool, 0, count, 2, count - 2, body)

        def pool_gather(pool, f, t):
            s = rt[f]
            if t == 0:
                pool.wait_ge(s["results"], 1)
                for par in range(2):
                    pool.wait_ge(ex[f]["stored"][par], 16 * NEX // 2)
            wait(pool, s["combined"], 2 * QT * (t - 1))
            for j in range(QT):
                for e in range(2):
                    pool.indirect_dma_start(picked[:, t % 2, j, e, :], None, ys,
                                            bass.IndirectOffsetOnAxis(ap=result_i[:, QT * t + j, e:e + 1], axis=0))\
                        .then_inc(s["picked"][t % 2], 16)

        def sp_blocks(sp, s, f, count):
            def load(k, par, half):
                at_k = slice(k, k + 1) if isinstance(k, int) else bass.ds(k, 1)
                e = sp.value_load(blk_e[0:1, at_k], min_val=0, max_val=E - 1)
                rows_k = bass.ds(sp.value_load(blk_at[0:1, at_k], min_val=0, max_val=ROWS // BLK - 1) * BLK, BLK)
                wait(sp, s["w1_lo"], k - 1)
                wait(sp, s["w2_lo"], k - 1)
                wait(sp, s["x_ps"], k - 1)
                alone(sp)
                sp.dma_start(w1_raw[:, par, :], W1[bass.ds(e, 1), :, :].rearrange("o d f -> (o d) f"))\
                  .then_inc(s["loaded"][par], 16)
                sp.dma_start(x_rows_sb[:, par, :, :], xs[rows_k, :].rearrange("(s p) d -> p s d", p=P))\
                  .then_inc(s["loaded"][par], 16)
                sp.dma_start(w2_raw[:, par, :], W2[bass.ds(e, 1), :, :].rearrange("o (p c) d -> (o p) (c d)", c=FC))\
                  .then_inc(s["loaded"][par], 16)

            def store(k, par):
                rows_k = slice(k * BLK, (k + 1) * BLK) if isinstance(k, int) else bass.ds(k * BLK, BLK)
                sp.wait_ge(s["rows"], k + 1)
                alone(sp)
                sp.dma_start(ys[rows_k, :].rearrange("(s p) d -> p s d", p=P), y_rows[:, par, :, :])\
                  .then_inc(s["stored"][par], 16)

            def body(k, par, half):
                if exists(k, count):
                    load(k, par, half)
                if exists(k - 4, count):
                    store(k - 4, par)

            sp.wait_ge(rt[f]["maths"], MATHS_ALL + 2)
            for e in range(E):
                used = sp.value_load(size_i[0:1, e:e + 1], min_val=0, max_val=T)
                sp.dma_start(xs[bass.ds(used + e * REGION, BLK), :], zero_rows).then_inc(rt[f]["filled"], 16)
            sp.wait_ge(rt[f]["blk"], 1)
            sp.wait_ge(rt[f]["filled"], 16 * E)
            for p in range(2):
                sp.wait_ge(rt[f]["scattered"][p], 16 * 2 * NT // 2)
            if f:
                sp.wait_ge(kept, NSH)
            steps(sp, 0, count + 4, 4, count, body)

        FIRST_ROUND, ROUNDS = -2, BATCH + 2
        ST_BANK, S_BANK, CTX_BANK, MISC_BANK = 0, 2, 6, 7
        STEPS = G * QT * R
        MISC = {2: ("logit", -2, 0), 36: ("count", -2, 0), 62: ("rT", -1, 0),
                6: ("nmaxT", 0, 1), 10: ("turn", -1, G - 1), 14: ("ctxT", -1, 0), 18: ("o", -1, 0),
                22: ("nmaxT", 0, 2), 26: ("turn", 0, 0), 30: ("v", 1, 0), 34: ("xT", 2, 0),
                38: ("nmaxT", 0, 3), 42: ("turn", 0, 1), 46: ("q", 2, 0), 50: ("k", 2, 0),
                54: ("nmaxT", 1, 0), 58: ("turn", 0, 2)}
        for name, (made, read) in dict(rT=("xT_ps", "xT_lo"), logit=("logit_ps", "logits"),
                                       count=("count_ps", "counted")).items():
            at[name + "_ps"], at[name] = rt[1][made], rt[1][read]
        READ = {"rT": "rT", "logit": "logit", "count": "count", "nmaxT": "nmaxT", "turn": "turned", "ctxT": "ctxT", "o": "added", "v": "v", "xT": "xT", "q": "q", "k": "k"}

        def number(what, b, g):
            return G * b + g + 1 if what in ("nmaxT", "turn") else b + 1

        def present(t, what, db, g):
            return exists(t + db, BATCH)

        def misc_before(t, step):
            keys = sorted(MISC)
            i, u = keys.index(step), t
            while True:
                i -= 1
                if i < 0:
                    i, u = len(keys) - 1, (u - 1 if isinstance(u, int) else t - 1)
                    if isinstance(u, int) and u < FIRST_ROUND:
                        return None
                what, db, g = MISC[keys[i]]
                if present(u, what, db, g):
                    return what, number(what, u + db, g)

        def entry_ahead(t, j):
            ahead = j + 2 * QT * R
            return t + ahead // STEPS, ahead % STEPS

        def heads(ap, r, rows):
            return ap[RP * r:RP * r + rows]

        def pe_attention(pe):
            def scores(b, j):
                g, qt, r = j // (QT * R), j // R % QT, j % R
                if j % (QT * R) == 0:
                    pe.wait_ge(stack_in[g % 2], 16 * (R + 2) * (G // 2 * b + g // 2 + 1))
                if j % 2 == 0:
                    wait(pe, at["s_read"], STEPS // 2 * b + j // 2 - 1)
                mm = pe.matmul(bank[:, S_BANK + j % 4, :], q_st[:, g, qt * P:(qt + 1) * P], k_st[:, g, r, :],
                               start=True, stop=True)
                if j % 2:
                    mm.then_inc(at["s_ps"], 1)

            def scores_t(b, s):
                g, kt, r = s // (QT * R), s // R % QT, s % R
                if s % (QT * R) == 0:
                    pe.wait_ge(nmax_in[g % 2], 16 * (G // 2 * b + g // 2 + 1))
                wait(pe, at["probs"], STEPS * b + s - 1)
                pe.matmul(bank[:, ST_BANK + s % 2, :], k_st[:, g, r, kt * P:(kt + 1) * P],
                          q_st[:, g, :], start=True, stop=True).then_inc(at["st_ps"], 1)

            def context(b, par, q):
                g, kt = q // QT, q % QT
                pe.wait_ge(at["probs"], STEPS * b + R * (q + 1))
                if q == 0:
                    pe.wait_ge(at["v"], b + 1)
                if kt == 0:
                    wait(pe, at["ctx_raw"], G * b + g)
                for r in range(R):
                    mm = pe.matmul(heads(bank, r, RP)[:, CTX_BANK, :], v_st[:, par, kt, g * R + r, :],
                                   probs[:, (R * q + r) % RING, :], start=kt == 0, stop=kt == QT - 1)
                mm.then_inc(at["pv_ps"], 1)

            def misc(t, par, step):
                what, db, g = MISC[step]
                b = t + db
                before = misc_before(t, step)
                if before:
                    pe.wait_ge(at[READ[before[0]]], before[1])
                o = bank[:, MISC_BANK, :]
                if what == "rT":
                    pe.wait_ge(rt[1]["xn"], QT * (b + 1))
                    return pe_turn(pe, rt[1], b, xr[:, 1 - par, :, :], o)
                if what == "logit":
                    pe.wait_ge(rt[1]["xT_lo"], b + 1)
                    return pe_logits(pe, rt[1], o, xrT_hi, xrT_lo)
                if what == "count":
                    pe.wait_ge(rt[1]["hot"], b + 1)
                    return pe_count(pe, rt[1], o)
                if what == "nmaxT":
                    pe.wait_ge(at["nmax_parts"], 2 * (G * b + g + 1))
                    mm = pe.transpose(o[0:2 * R * QT, 0:P],
                                      nmax_parts[:, g % 2].rearrange("p r h q -> p (r h q)"), ident[:, :])
                elif what == "turn":
                    pe.wait_ge(at["ctx_raw"], G * b + g + 1)
                    for j in range(QT):
                        mm = pe.transpose(o[:, j * P:(j + 1) * P], ctx_raw[:, j * P:(j + 1) * P], ident[:, :])
                elif what == "ctxT":
                    pe.wait_ge(at["turned"], G * (b + 1))
                    for j in range(QT):
                        mm = pe.transpose(o[:, j * P:(j + 1) * P], ctx_n[:, j, :], ident[:, :])
                elif what == "o":
                    pe.wait_ge(at["ctxT"], b + 1)
                    for j in range(QT):
                        mm = pe.matmul(o[:, j * P:(j + 1) * P], ctxT[:, j * P:(j + 1) * P], wo[:, :],
                                       start=True, stop=True)
                elif what == "v":
                    pe.wait_ge(at["xT"], b + 1)
                    for j in range(QT):
                        mm = pe.matmul(o[:, j * P:(j + 1) * P], xnT[:, j * P:(j + 1) * P], wv[:, :],
                                       start=True, stop=True)
                elif what == "xT":
                    pe.wait_ge(at["xn"], QT * (b + 1))
                    for j in range(QT):
                        mm = pe.transpose(o[:, j * P:(j + 1) * P], xa[:, par, j, :], ident[:, :])
                elif what in ("q", "k"):
                    pe.wait_ge(at["xT"], b + 1)
                    mm = pe.matmul(o, (wq if what == "q" else wk)[:, :], xnT[:, :], start=True, stop=True)
                mm.then_inc(at[what + "_ps"], 1)

            def round_(t, par, half):
                for s in range(STEPS):
                    if exists(t, BATCH):
                        scores_t(t, s)
                    for j in {0: (s - 1,), 1: (), 2: (s - 2,), 3: (s - 2, s - 1)}[s % 4]:
                        ahead, of = entry_ahead(t, j)
                        if exists(ahead, BATCH):
                            scores(ahead, of)
                    if s == 1 and exists(t - 1, BATCH):
                        context(t - 1, 1 - par, G * QT - 1)
                    if s % R == 1 and s > R and exists(t, BATCH):
                        context(t, par, s // R - 1)
                    if s in MISC and present(t, *MISC[s]):
                        misc(t, par, s)

            pe.wait_ge(stack_const, 16 * STACK_CONSTS)
            pe.wait_ge(ex[0]["rows"], NEX)
            steps(pe, FIRST_ROUND, ROUNDS, LOOP[0], LOOP[1], round_)

        LOOP = (2, BATCH - 2)
        QK_PARTS = 2 * 3
        STACK_CONSTS = R

        def act_attention(act):
            def prob(b, s):
                act.wait_ge(at["st_ps"], STEPS * b + s + 1)
                wait(act, at["pv_ps"], G * QT * b + s // R - 1)
                act.activation(probs[:, s % RING, :], bank[:, ST_BANK + s % 2, :], ACT.Exp).then_inc(at["probs"], 1)

            def context_out(b, g):
                act.wait_ge(at["pv_ps"], QT * (G * b + g + 1))
                wait(act, at["turn_ps"], G * b + g)
                act.activation(ctx_raw[:, :], bank[:, CTX_BANK, :], ACT.Copy).then_inc(at["ctx_raw"], 1)

            def misc(t, par, half, step):
                what, db, g = MISC[step]
                b = t + db
                m = bank[:, MISC_BANK, :]
                act.wait_ge(at[what + "_ps"], number(what, b, g))
                if what == "ctxT":
                    act.activation(ctxT[:, :], m, ACT.Identity, bias=bv_col[:, 0:1]).then_inc(at["ctxT"], 1)
                elif what == "v":
                    v_par = 1 - par
                    act.activation(v_st[:, v_par, :, :, 0:HD].rearrange("p k h d -> p (k h) d"),
                                   m.rearrange("p (kh d) -> p kh d", d=HD), ACT.Copy).then_inc(at["v"], 1)
                elif what == "xT":
                    act.activation(xnT[:, :], m, ACT.Copy).then_inc(at["xT"], 1)
                elif what == "rT":
                    act.activation(xrT_hi, m, ACT.Copy).then_inc(rt[1]["xT_hi"], 1)
                elif what in ("q", "k"):
                    i = 0 if what == "q" else 1
                    act.activation(m, m, ACT.Identity, bias=(bqs_col if what == "q" else bk_col)[:, 0:1],
                                   scale=SCALE if what == "q" else 1.0).then_inc(at["qk_z"], 1)
                    act.wait_ge(at["qk_z"], 2 * b + i + 1)
                    wait(act, qk_out, 16 * QK_PARTS * b)
                    act.activation(qk_hi[:, i, :], m, ACT.Copy).then_inc(at["qk_hi"], 1)

            def round_(t, par, half):
                for s in range(STEPS):
                    if s == 4 and exists(t - 1, BATCH):
                        context_out(t - 1, G - 1)
                    if s % (QT * R) == 4 and s > QT * R and exists(t, BATCH):
                        context_out(t, s // (QT * R) - 1)
                    if exists(t, BATCH):
                        prob(t, s)
                    if s in MISC and MISC[s][0] in ("ctxT", "v", "xT", "q", "k", "rT") and present(t, *MISC[s]):
                        misc(t, par, half, s)

            steps(act, FIRST_ROUND, ROUNDS, LOOP[0], LOOP[1], round_)

        TOP_AT, PLACE_AT = (5, 8, 12, 14, 17), (40, 42, 44)

        def dve_attention(dve):
            def maxima(b, j):
                g, qt, r = j // (QT * R), j // R % QT, j % R
                dve.wait_ge(at["s_ps"], STEPS // 2 * b + j // 2 + 1)
                slot2 = S_BANK + j % 4 - 1
                dve.tensor_reduce(nmax[:, g % 2, r - 1:r + 1, qt], bank[:, slot2:slot2 + 2, :],
                                  AX.X, ALU.max, negate=True).then_inc(at["s_read"], 1)

            def max_parts(b, g):
                n = G * b + g
                hi, lo = nmax_parts[:, g % 2, :, 0, :], nmax_parts[:, g % 2, :, 1, :]
                dve.wait_ge(at["s_read"], 2 * QT * (n + 1))
                wait(dve, at["nmaxT_ps"], n - 1)
                dve.tensor_copy(hi.bitcast(F32R), nmax[:, g % 2, :, :]).then_inc(at["nmax_parts"], 1)
                dve.wait_ge(at["nmax_parts"], 2 * n + 1)
                dve.tensor_tensor(lo.bitcast(F32R), nmax[:, g % 2, :, :], hi, ALU.subtract)\
                   .then_inc(at["nmax_parts"], 1)

            def misc(t, par, half, step):
                what, db, g = MISC[step]
                b = t + db
                m = bank[:, MISC_BANK, :]
                if what == "rT":
                    dve.wait_ge(rt[1]["xT_hi"], b + 1)
                    dve.tensor_tensor(xrT_lo, m, xrT_hi.bitcast(F32), ALU.subtract).then_inc(rt[1]["xT_lo"], 1)
                elif what == "logit":
                    dve_top(dve, rt[1], b, m, 0)
                elif what == "count":
                    dve_place(dve, rt[1], b, m, 0)
                elif what == "nmaxT":
                    n = G * b + g
                    dve.wait_ge(at["nmaxT_ps"], n + 1)
                    wait(dve, nmax_out, 16 * n)
                    dve.tensor_copy(nmaxT[:, :], m[0:2 * R * QT, 0:P]).then_inc(at["nmaxT"], 1)
                elif what == "turn":
                    n = G * b + g
                    mv4 = m.rearrange("p (q r c) -> p q r c", r=R, c=RP)
                    dve.wait_ge(at["turn_ps"], n + 1)
                    if g == 0:
                        wait(dve, at["ctxT_ps"], b)
                    dve.reciprocal(rden[:, :, :], mv4[:, :, :, HD]).then_inc(at["rden"], 1)
                    dve.wait_ge(at["rden"], n + 1)
                    dve.tensor_tensor(ctx_n[:, :, g * R * HD:(g + 1) * R * HD].rearrange("p q (r d) -> p q r d", d=HD),
                                      mv4[:, :, :, 0:HD],
                                      rden[:, :, :].unsqueeze(3).to_broadcast([P, QT, R, HD]),
                                      ALU.mult).then_inc(at["turned"], 1)
                elif what == "o":
                    dve.wait_ge(at["biased"], b + 1)
                    dve.wait_ge(at["o_ps"], b + 1)
                    at_b = slice(b * QT, (b + 1) * QT) if isinstance(b, int) else bass.ds(b * QT, QT)
                    dve.tensor_tensor(X[:, at_b, :], m.rearrange("p (q d) -> p q d", d=D), X[:, at_b, :],
                                      ALU.add).then_inc(at["added"], 1)
                elif what in ("q", "k"):
                    i = 0 if what == "q" else 1
                    dve.wait_ge(at["qk_hi"], 2 * b + i + 1)
                    dve.tensor_tensor(qk_lo[:, i, :], m, qk_hi[:, i, :].bitcast(F32), ALU.subtract)\
                       .then_inc(at[what], 1)

            def round_(t, par, half):
                for s in range(STEPS):
                    if exists(t + 2, BATCH):
                        if s % 2 and s < 4 * QT:
                            dve_combine(dve, rt[0], t + 2, par, half + 1, s // 2)
                        if s % 2 and 4 * QT < s < 6 * QT:
                            dve_stats(dve, at, t + 2, par, s // 2 - 2 * QT)
                        if s == 6 * QT + 1:
                            dve_aggregate(dve, at, t + 2, par)
                        if 28 <= s < 28 + QT:
                            dve_norm(dve, at, t + 2, par, xa[:, par, :, :], s - 28)
                    if exists(t - 1, BATCH):
                        if s % 2 and 33 <= s < 33 + 2 * QT:
                            if s == 33:
                                dve.wait_ge(at["added"], t)
                            dve_stats(dve, rt[1], t - 1, 1 - par, (s - 33) // 2)
                        if s == 33 + 2 * QT:
                            dve_aggregate(dve, rt[1], t - 1, 1 - par)
                        if 45 <= s < 45 + QT:
                            if s == 45 and exists(t - 3, BATCH):
                                dve.wait_ge(rt[1]["scattered"][1 - par], 16 * 2 * QT * (half - 1 + par))
                                dve.wait_ge(kept, t - 2)
                            dve_norm(dve, rt[1], t - 1, 1 - par, xr[:, 1 - par, :, :], s - 45)
                    if exists(t - 2, BATCH):
                        if s in TOP_AT:
                            dve_top(dve, rt[1], t - 2, None, TOP_AT.index(s) + 1)
                        if s in PLACE_AT:
                            dve_place(dve, rt[1], t - 2, None, PLACE_AT.index(s) + 1)
                    if s % 4 in (0, 3):
                        j = s - 1 if s % 4 == 0 else s - 2
                        ahead, of = entry_ahead(t, j)
                        if exists(ahead, BATCH):
                            maxima(ahead, of)
                            if of % (QT * R) == QT * R - 1:
                                max_parts(ahead, of // (QT * R))
                    if s in MISC and MISC[s][0] in ("nmaxT", "turn", "o", "q", "k", "rT", "logit", "count") and present(t, *MISC[s]):
                        misc(t, par, half, s)

            steps(dve, FIRST_ROUND, ROUNDS, LOOP[0], LOOP[1], round_)

        def pool_attention(pool):
            pool_gather(pool, 0, 0)
            for t in range(FIRST_ROUND, ROUNDS):
                if t > FIRST_ROUND and t + 3 < BATCH:
                    pool_gather(pool, 0, t + 3)
                if t + 2 < BATCH:
                    pool_rstd(pool, at, t + 2, t % 2)
                    x = X[:, QT * (t + 2):QT * (t + 3), :]
                    pool.wait_ge(at["xn"], QT * (t + 3))
                    pool.tensor_tensor(x, x, bo_rows[:, :].unsqueeze(1).to_broadcast([P, QT, D]), ALU.add)\
                        .then_inc(at["biased"], 1)
                if t == FIRST_ROUND:
                    pool_gather(pool, 0, t + 3)
                if 0 <= t - 1 < BATCH:
                    pool_rstd(pool, rt[1], t - 1, (t - 1) % 2)
                if 0 <= t - 2:
                    pool_scatter(pool, 1, t - 2, xr[:, t % 2, :, :])
                    pool.tensor_copy(xn[:, QT * (t - 2):QT * (t - 1), :], xr[:, t % 2, :, :]).then_inc(kept, 1)

        def sp_attention(sp):
            def stack(b, par, g):
                if g == 0:
                    sp.wait_ge(qk_out, 16 * QK_PARTS * (b + 1))
                    alone(sp)
                if not isinstance(b, int) or b > 0:
                    sp.wait_ge(at["st_ps"], STEPS * (b - 1) + QT * R * (g + 1))
                    alone(sp)
                elif g >= 2:
                    sp.wait_ge(at["s_ps"], QT * R // 2 * (g - 2) + 1)
                sp.dma_start(q_st[0:MAX_ROW, g, :].bitcast(F32),
                             q_dram[par][R * g:R * (g + 1)].rearrange("r x n -> (r x) n")).then_inc(stack_in[g % 2], 16)
                sp.dma_start(q_st[MAX_ROW:P, g, :].bitcast(F32),
                             zero_rows[0:(P - MAX_ROW) * SEQ // D, :].rearrange("(p a) d -> p (a d)", p=P - MAX_ROW))\
                  .then_inc(stack_in[g % 2], 16)
                for r in range(R):
                    sp.dma_start(k_st[HK * r:HK * (r + 1), g, r, :].bitcast(F32), k_dram[par][R * g + r])\
                      .then_inc(stack_in[g % 2], 16)

            def maxima(b, g):
                n = G * b + g
                sp.wait_ge(at["nmaxT"], n + 1)
                alone(sp)
                sp.dma_start(nmax_dram[g].rearrange("a (q p) -> (a q) p", p=P), nmaxT[:, :].bitcast(F32))\
                  .then_inc(nmax_out, 16)
                sp.wait_ge(nmax_out, 16 * (n + 1))
                alone(sp)
                sp.dma_start(q_st[MAX_ROW:MAX_ROW + 2 * R, g, :].bitcast(F32), nmax_dram[g]).then_inc(nmax_in[g % 2], 16)

            def parts(b, par):
                for i, (what, to, order) in enumerate((("q", q_dram[par], (qk_hi, qk_hi, qk_lo)),
                                                       ("k", k_dram[par], (qk_lo, qk_hi, qk_hi)))):
                    sp.wait_ge(at[what], b + 1)
                    alone(sp)
                    for x in range(3):
                        sp.dma_start(to[:, HD * x:HD * (x + 1), :], order[x][:, i, :].bitcast(F32)).then_inc(qk_out, 16)

            def round_(t, par, half):
                for g in range(G):
                    b, of = (t, g + 3) if g == 0 else (t + 1, g - 1)
                    if exists(b, BATCH):
                        stack(b, par if g == 0 else 1 - par, of)
                    b, of = (t, g + 1) if g + 1 < G else (t + 1, 0)
                    if exists(b, BATCH):
                        maxima(b, of)
                if exists(t + 2, BATCH):
                    parts(t + 2, par)

            sp.wait_ge(at["init"], G + 2)
            for r in range(R):
                row = MAX_ROW + 2 * r
                sp.dma_start(k_st[row:row + 2, :, r, :].bitcast(F32), probs[0:2 * G, 4, :])\
                  .then_inc(stack_const, 16)
            steps(sp, FIRST_ROUND, ROUNDS, LOOP[0], LOOP[1], round_)

        @block.sync
        def _(sp):
            first = QT * P
            sp.dma_start(X[:, 0:QT, :], x_rows[0:first, :].rearrange("(t p) d -> p t d", p=P)).then_inc(x_first, 16)
            sp.dma_start(wg[:, :], Wg).then_inc(wg_in, 16)
            sp.dma_start(X[:, QT:NT, :], x_rows[first:T, :].rearrange("(t p) d -> p t d", p=P)).then_inc(x_loaded, 16)
            column = lambda v: v.rearrange("(p o) -> p o", o=1)
            loads = [(ws1_raw, Ws1), (ws2_raw, Ws2.rearrange("(p c) d -> p (c d)", c=FC)),
                     (bs1_col[:, :], bs1.rearrange("(p c) -> p c", c=FC)), (bs2_col[:, :], column(bs2)),
                     (b1_col[:, :].rearrange("p (e c) -> p e c", c=FC), b1.rearrange("e (p c) -> p e c", c=FC)),
                     (b2_col[:, :], b2.rearrange("e d -> d e")),
                     (wq[:, :], Wq), (wk[:, :], Wk), (wv[:, :], Wv), (wo[:, :], Wo),
                     (bq_col[:, :], column(bq)), (bk_col[:, :], column(bk)), (bv_col[:, :], column(bv)),
                     (bo_rows[:, :], bo.unsqueeze(0).to_broadcast([P, D]))]
            assert len(loads) == LOADS
            for to, of in loads:
                sp.dma_start(to, of, allow_slow_non_contiguous=True).then_inc(const_in, 16)
            sp.wait_ge(dve_const, 1)
            sp.dma_start(xs[PAD:ROWS, :].rearrange("(p s) d -> p s d", p=P),
                         probs[:, 0:4, :].rearrange("p a n -> p (a n)").unsqueeze(1).to_broadcast([P, PAD_BLOCKS * BLK * D // P // 2048, 2048]))\
              .then_inc(pads_zero, 16)
            sp.wait_ge(pads_zero, 16)
            sp_blocks(sp, ex[0], 0, NEX)
            sp_attention(sp)
            sp_blocks(sp, ex[1], 1, NEX)
            for b in range(BATCH):
                sp.wait_ge(rt[1]["combined"], 2 * QT * (b + 1))
                sp.dma_start(out_rows[b * SEQ:(b + 1) * SEQ, :].rearrange("(t p) d -> p t d", p=P),
                             X[:, b * QT:(b + 1) * QT, :]).then_inc(out_done, 16)
            sp.wait_ge(out_done, 16 * BATCH)

        @block.gpsimd
        def _(pool):
            pool.memset(ident[:, :], 0.0).then_inc(pool_const, 1)
            pool.memset(ones_bf[:, :], 1.0).then_inc(pool_const, 1)
            pool.memset(neg_half[:, :], -0.5).then_inc(pool_const, 1)
            pool.iota(iota_e[:, :], [[1, E]], 0, 0, allow_small_or_imprecise_dtypes=True).then_inc(pool_const, 1)
            pool.iota(iota_b[:, :], [[1, NEX]], 0, 0, allow_small_or_imprecise_dtypes=True).then_inc(pool_const, 1)
            pool.wait_ge(pool_const, 5)
            pool.affine_select(out=ident[:, :], in_=ident[:, :], compare_op=ALU.not_equal, fill=1.0,
                               base=0, pattern=[[-1, P]], channel_multiplier=1).then_inc(pool_const, 1)
            pool.affine_select(out=before_bf[:, :], in_=ones_bf[:, :], compare_op=ALU.is_gt, fill=0.0,
                               base=0, pattern=[[1, P]], channel_multiplier=-1).then_inc(pool_const, 1)
            pool_route(pool)
            pool_weights(pool, ex[0], NEX)
            pool_attention(pool)
            pool_weights(pool, ex[1], NEX)
            for b in range(BATCH):
                pool_gather(pool, 1, b)

        @block.vector
        def _(dve):
            dve.memset(probs[:, 0:4, :], 0.0).then_inc(dve_const, 1)
            dve.memset(probs[:, 4, :], 1.0).then_inc(dve_const, 1)
            dve.memset(scan_one[:, :], 1.0).then_inc(dve_const, 1)
            dve.wait_ge(wg_in, 16)
            dve.tensor_copy(wg_hi[:, :], wg[:, :]).then_inc(wg_parts, 1)
            dve.wait_ge(pool_const, POOL_CONSTS)
            dve.tensor_scalar(region_start[:, :], iota_e[:, :], float(REGION), None, ALU.mult).then_inc(dve_const, 1)
            dve.wait_ge(wg_parts, 1)
            dve.tensor_tensor(wg_lo[:, :], wg[:, :], wg_hi[:, :].bitcast(F32), ALU.subtract).then_inc(wg_parts, 1)
            dve.wait_ge(dve_const, 4)
            dve.tensor_copy(next_row[:, :], region_start[:, :]).then_inc(dve_const, 1)
            dve.wait_ge(dve_const, 5)
            dve.wait_ge(x_first, 16)
            dve_route(dve)
            dve_blocks(dve, sh[0], NSH, False)
            dve_blocks(dve, ex[0], NEX, True)
            dve.tensor_copy(next_row[:, :], region_start[:, :]).then_inc(dve_const, 1)
            dve.wait_ge(dve_const, DVE_CONSTS + 1)
            dve_attention(dve)
            dve_blocks_of(dve, rt[1])
            dve_gates(dve, rt[1])
            dve_blocks(dve, ex[1], NEX, True)
            for t in range(NSH):
                dve_xT_lo(dve, rt[0], t, NSH)
            dve_blocks(dve, sh[1], NSH, False)

        @block.scalar
        def _(act):
            act_turned(act, rt[0], 0)
            act_gates(act, rt[0])
            act.wait_ge(const_in, 16 * LOADS)
            act_blocks(act, sh[0], 0, NSH, False)
            act_blocks(act, ex[0], 0, NEX, True)
            act.wait_ge(dve_const, DVE_CONSTS)
            act.wait_ge(at["init"], G + 2)
            act_attention(act)
            act_gates(act, rt[1])
            act_blocks(act, ex[1], 1, NEX, True)
            act_turned(act, rt[0], NSH)
            act_blocks(act, sh[1], 1, NSH, False)

        @block.tensor
        def _(pe):
            pe.wait_ge(pool_const, POOL_CONSTS)
            pe.wait_ge(wg_parts, 2)
            pe_route(pe)
            pe.wait_ge(rt[0]["counted"], NSH)
            pe.wait_ge(dve_const, DVE_CONSTS)
            pe_blocks(pe, sh[0], NSH, False)
            pe_blocks(pe, ex[0], NEX, True)
            pe_attention(pe)
            pe.wait_ge(rt[1]["counted"], NSH)
            pe_blocks(pe, ex[1], NEX, True)
            pe_turn_all(pe, rt[0], ex[1])
            pe_blocks(pe, sh[1], NSH, False)


LOADS = 14
POOL_CONSTS = 7
DVE_CONSTS = 10

_INS = ["L0_attn_x", "L0_attn_Wq", "L0_attn_bq", "L0_attn_Wk", "L0_attn_bk", "L0_attn_Wv", "L0_attn_bv",
        "L0_attn_Wo", "L0_attn_bo", "L0_ffn_Wg", "L0_ffn_W1", "L0_ffn_b1", "L0_ffn_W2", "L0_ffn_b2",
        "L0_ffn_Ws1", "L0_ffn_bs1", "L0_ffn_Ws2", "L0_ffn_bs2"]


def kernel(**inputs):
    import numpy as _np
    import concourse.bacc as _bacc
    from concourse import mybir as _mybir
    from concourse.bass_utils import run_bass_kernel_spmd as _run

    nc = _bacc.Bacc("TRN2", target_bir_lowering=False, num_devices=1)
    arrays, args = {}, []
    for name in _INS:
        a = _np.ascontiguousarray(inputs[name])
        arrays[f"in_{name}_dram"] = a
        args.append(nc.dram_tensor(f"in_{name}_dram", a.shape, _mybir.dt.from_np(a.dtype), kind="ExternalInput").ap())
    shape = inputs["L0_attn_x"].shape
    args.append(nc.dram_tensor("out_0_dram", shape, _mybir.dt.float32, kind="ExternalOutput").ap())
    macaron(nc, *args)
    r = _run(nc, [arrays], core_ids=[0])
    return r.results[0]["out_0_dram"]
```

```python
from contextlib import ExitStack

import concourse.bass as bass
from concourse import mybir

F32 = mybir.dt.float32
F32R = mybir.dt.float32r
BF16 = mybir.dt.bfloat16
U32 = mybir.dt.uint32
I32 = mybir.dt.int32
ALU = mybir.AluOpType
ACT = mybir.ActivationFunctionType
AX = mybir.AxisListType

P = 128


def wait(eng, sem, value):
    if not isinstance(value, int) or value > 0:
        eng.wait_ge(sem, value)


def exists(k, count):
    return not isinstance(k, int) or 0 <= k < count


def steps(eng, first, last, loop_from, loop_to, body):
    for k in range(first, loop_from):
        body(k, k % 2, k // 2)
    if loop_to > loop_from:
        with eng.Fori(loop_from // 2, loop_to // 2) as i:
            for par in range(2):
                body(i * 2 + par, par, i)
    for k in range(loop_to, last):
        body(k, k % 2, k // 2)


def macaron(nc, x_in, Wq, bq, Wk, bk, Wv, bv, Wo, bo, Wg, W1, b1, W2, b2, Ws1, bs1, Ws2, bs2, out):
    BATCH, SEQ, D = x_in.shape
    E, _, F = W1.shape
    H = 16
    HD = D // H
    SCALE = 1.0 / float(HD) ** 0.5
    TOP = 2
    T = BATCH * SEQ
    NT = T // P
    QT = SEQ // P
    BLK = 512
    SUB = BLK // P
    FC = F // P
    NSH = T // BLK
    NEX = TOP * T // BLK + E
    REGION = T + BLK
    PAD = E * REGION
    PAD_BLOCKS = NEX - TOP * T // BLK
    ROWS = PAD + PAD_BLOCKS * BLK
    LOGBLK = BLK.bit_length() - 1
    G = 4
    R = H // G
    RP = P // R
    assert D == P and SEQ == BLK and E == 8 and G * R == H

    x_rows = x_in.rearrange("b s d -> (b s) d")
    out_rows = out.rearrange("b s d -> (b s) d")

    W = D + 2
    xs = nc.dram_tensor("sorted_rows", (ROWS, W), F32, kind="Internal").ap()
    ys = nc.dram_tensor("expert_rows", (TOP * T + 2 * BLK + 1, D), F32, kind="Internal").ap()
    HK = 3 * HD
    q_dram, k_dram = [[nc.dram_tensor(f"{n}_stacks_{par}", (H, HK, SEQ), F32, kind="Internal").ap()
                       for par in range(2)] for n in ("q", "k")]
    zero_dram = nc.dram_tensor("zeros", (P - R * HK, SEQ), F32, kind="Internal").ap()

    ctx = ExitStack()
    with ctx:
        def sb(name, shape, dt=F32):
            return ctx.enter_context(nc.sbuf_tensor("sb_" + name, shape, dt))

        def sem(name):
            return ctx.enter_context(nc.semaphore(name))

        def sem2(name):
            return [sem(f"{name}_{i}") for i in range(2)]

        ident = sb("ident", [P, P])
        ones_bf = sb("ones_bf", [P, P], BF16)
        before_bf = sb("before_bf", [P, P], BF16)
        iota_e = sb("iota_e", [P, E])
        iota_b = sb("iota_b", [P, NEX])
        token_row = sb("token_row", [P, NT]); no_tokens = sb("no_tokens", [P, SUB, W])
        neg_half = sb("neg_half", [P, QT])
        scan_one = sb("scan_one", [P, E]); region_start = sb("region_start", [P, E])
        wq = sb("wq", [P, D]); wk = sb("wk", [P, D]); wv = sb("wv", [P, D]); wo = sb("wo", [P, D])
        bq_col = sb("bq_col", [P, 1]); bk_col = sb("bk_col", [P, 1]); bqs_col = sb("bqs_col", [P, 1])
        bv_col = sb("bv_col", [P, 1]); bo_rows = sb("bo_rows", [P, D])
        wg = sb("wg", [P, E]); wg_hi = sb("wg_hi", [P, E], F32R); wg_lo = sb("wg_lo", [P, E], F32R)
        b1_col = sb("b1_col", [P, E * FC]); b2_col = sb("b2_col", [P, E])
        bs1_col = sb("bs1_col", [P, FC]); bs2_col = sb("bs2_col", [P, 1])

        X = sb("X", [P, NT, D])
        xn = sb("xn", [P, NT, W])
        bn = sb("bn", [P, 2, 2, QT, 6]); mv = sb("mv", [P, 2, 2, QT, 2])
        vare = sb("vare", [P, 2, QT]); rstd = sb("rstd", [P, 2, 2, QT])

        xT = sb("xT", [P, 2 * NSH, BLK], F32R)
        xT_hi, xT_lo = xT[:, 0:NSH, :], xT[:, NSH:2 * NSH, :]
        logits = sb("logits", [P, QT, E]); top_v = sb("top_v", [P, QT, E]); top_i = sb("top_i", [P, QT, E], U32)
        top_f = sb("top_f", [P, NT, 2]); gap = sb("gap", [P, NT]); gate = sb("gate", [P, 2, NT])
        hot = sb("hot", [P, QT, 2, E]); hot_bf = sb("hot_bf", [P, QT, E], BF16)
        next_row = sb("next_row", [P, E])
        row = sb("row", [P, QT, E]); row_f = sb("row_f", [P, NT, 2])
        row_i = sb("row_i", [P, NT, 2], U32)
        size = sb("size", [P, E]); size_i = sb("size_i", [1, E], I32)
        blocks_i = sb("blocks_i", [P, E], I32); blocks = sb("blocks", [P, E]); blocks_upto = sb("blocks_upto", [P, E])
        unused = sb("unused", [P, E]); blk_cmp = sb("blk_cmp", [P, NEX, E]); blk_f = sb("blk_f", [P, NEX])
        blk_expert = sb("blk_expert", [P, NEX]); blk_e = sb("blk_e", [1, NEX], I32); blk_at = sb("blk_at", [1, NEX], I32)
        result = sb("result", [P, NEX, SUB]); result_i = sb("result_i", [P, 2, SUB], U32)
        aside_rows = sb("aside_rows", [P, SUB])

        w1_raw = sb("w1_raw", [P, 2, F]); w2_raw = sb("w2_raw", [P, 2, F])
        w1_hi = sb("w1_hi", [P, 2, FC, P], F32R); w1_lo = sb("w1_lo", [P, 2, FC, P], F32R)
        w2_hi = sb("w2_hi", [P, 2, FC, P], F32R); w2_lo = sb("w2_lo", [P, 2, FC, P], F32R)
        x_rows_sb = sb("x_rows", [P, 2, SUB, W])
        ws1_raw = w1_raw[:, 1]; ws2_raw = w2_raw[:, 1]
        ws1_hi = sb("ws1_hi", [P, FC, P], F32R); ws1_lo = sb("ws1_lo", [P, FC, P], F32R)
        ws2_hi = sb("ws2_hi", [P, FC, P], F32R); ws2_lo = sb("ws2_lo", [P, FC, P], F32R)
        xb = sb("xb", [P, 4, BLK], F32R)
        xb_hi, xb_lo = xb[:, 0:2, :], xb[:, 2:4, :]
        h_hi = sb("h_hi", [P, FC, BLK], F32R); h_lo = sb("h_lo", [P, FC, BLK], F32R)
        yT = sb("yT", [P, 2, BLK]); y_rows = sb("y_rows", [P, 2, SUB, W])
        xa = x_rows_sb
        xr = y_rows
        xrT_hi, xrT_lo = (w1_hi[:, p, :, :].rearrange("p c n -> p (c n)") for p in range(2))
        picked = sb("picked", [P, 2, QT, 2, D])


        q_st = xb
        k_st = xT[:, :, :].rearrange("p (g r) n -> p g r n", r=R)
        MAX_ROW = R * HK
        v_st = sb("v_st", [P, 2, QT, G * R, RP])
        qk_hi = sb("qk_hi", [P, 2, SEQ], F32R); qk_lo = sb("qk_lo", [P, 2, SEQ], F32R)
        xnT = sb("xnT", [P, SEQ])
        RING = 8
        probs = sb("probs", [P, RING, SEQ])
        ctx_raw = sb("ctx_raw", [P, SEQ]); rden = sb("rden", [P, QT, R])
        ctx_n = sb("ctx_n", [P, QT, D]); ctxT = sb("ctxT", [P, SEQ])
        nmax = sb("nmax", [P, 2, R, QT]); nmax_parts = sb("nmax_parts", [P, 2, R, 2, QT])
        nmaxT = sb("nmaxT", [R * 2 * QT, P], F32R)

        bank = ctx.enter_context(nc.psum_tensor("banks", [P, 8, BLK], F32))

        const_in = sem("const_in"); aside = sem("aside"); x_first = sem("x_first"); x_loaded = sem("x_loaded")
        wg_in = sem("wg_in"); wg_parts = sem("wg_parts")
        pool_const = sem("pool_const"); dve_const = sem("dve_const"); pads_in = sem("pads_in")
        out_done = sem("out_done")

        def sems(tag, names):
            return {n: sem(f"{n}_{tag}") for n in names.split()}

        rt, sh, ex = [], [], []
        for f in range(2):
            s = sems(f"route{f}", "stats mv var rstd xn xT_ps xT_hi xT_lo logit_ps logits maths hot count_ps counted "
                                  "rows gap exp blk filled combined")
            s["picked"] = sem2(f"picked_{f}"); s["scattered"] = sem2(f"scattered_{f}")
            rt.append(s)
            for kind, group in (("shared", sh), ("expert", ex)):
                s = sems(f"{kind}{f}", "h_ps relu h_hi h_lo h_used yT rows_ps rows")
                if kind == "expert":
                    s |= sems(f"{kind}{f}", "result w1_hi w1_lo w2_hi w2_lo x_ps x_hi x_lo")
                    s["loaded"] = sem2(f"loaded_{kind}{f}")
                    s["stored"] = sem2(f"stored_{kind}{f}")
                group.append(s)
        at = sems("att", "init biased stats mv var rstd xn nmax_parts s_ps s_read st_ps probs pv_ps ctx_raw rden "
                         "nmaxT_ps nmaxT turn_ps turned ctxT_ps ctxT o_ps added v_ps v xT_ps xT q_ps q k_ps k "
                         "qk_z qk_hi")
        kept = sem("kept")
        nmax_in = sem2("nmax_in")
        qk_out = sem("qk_out"); stack_const = sem("stack_const")
        stack_in = sem2("stack_in")

        block = ctx.enter_context(nc.Block())

        def alone(eng):
            eng.sem_inc(aside, 1)

        H_BANK, O_BANK, T_BANK, Y_BANK = 0, 4, 6, 7
        AHEAD = 2

        def pe_turn(pe, s, t, rows, to):
            for j in range(SUB):
                mm = pe.transpose(to[:, j * P:(j + 1) * P], rows[:, j, 0:D], ident[:, :])
            mm.then_inc(s["xT_ps"], 1)

        def pe_logits(pe, s, o, xT_hi, xT_lo):
            for j in range(SUB):
                oj, xh, xl = o[:, j * E:(j + 1) * E], xT_hi[:, j * P:(j + 1) * P], xT_lo[:, j * P:(j + 1) * P]
                pe.matmul(oj, xh, wg_hi[:, :], start=True, stop=False)
                pe.matmul(oj, xh, wg_lo[:, :], start=False, stop=False)
                mm = pe.matmul(oj, xl, wg_hi[:, :], start=False, stop=True)
            mm.then_inc(s["logit_ps"], 1)

        def pe_count(pe, s, o):
            for j in range(QT):
                for i in range(j):
                    pe.matmul(o[:, j * E:(j + 1) * E], ones_bf[:, :], hot_bf[:, i, :], start=i == 0, stop=False)
                pe.matmul(o[:, j * E:(j + 1) * E], before_bf[:, :], hot_bf[:, j, :], start=j == 0, stop=True)
            for j in range(QT):
                mm = pe.matmul(o[:, QT * E:(QT + 1) * E], ones_bf[:, :], hot_bf[:, j, :], start=j == 0, stop=j == QT - 1)
            mm.then_inc(s["count_ps"], 1)

        def pe_route(pe):
            s = rt[0]
            o = bank[:, T_BANK, :]

            def beside(k, place):
                b = k + AHEAD
                if b >= NSH:
                    return
                if place == 0:
                    pe.wait_ge(s["xn"], SUB * (b + 1))
                    wait(pe, s["counted"], b)
                    pe_turn(pe, s, b, xn[:, SUB * b:SUB * (b + 1), :], o)
                elif place == 1:
                    pe.wait_ge(s["xT_lo"], b + 1)
                    pe_logits(pe, s, o, xT_hi[:, b, :], xT_lo[:, b, :])
                elif place == 3:
                    pe.wait_ge(s["hot"], b + 1)
                    pe_count(pe, s, o)

            for k in range(-AHEAD, 0):
                for place in range(4):
                    beside(k, place)
            pe.wait_ge(dve_const, DVE_CONSTS)
            return beside

        EARLY = 2

        def pe_turned(pe, first):
            def beside(k, place):
                b = k + 1
                if place == 0 and b < (NSH if first else EARLY + 1):
                    pe.wait_ge(kept, b + 2)
                    wait(pe, rt[0]["xT_lo"], NSH + b)
                    pe_turn(pe, rt[0], b, xn[:, SUB * b:SUB * (b + 1), :], bank[:, T_BANK, :])

            if not first:
                beside(-1, 0)
            return beside

        def pe_blocks(pe, s, count, routed, beside=None, lo=0, after=None):
            def product(o, wh, wl, xh, xl, first, last):
                pe.matmul(o, wh, xh, start=first, stop=False)
                pe.matmul(o, wh, xl, start=False, stop=False)
                return pe.matmul(o, wl, xh, start=False, stop=last)

            def turn_x(k, par, half):
                pe.wait_ge(s["loaded"][par], 48 * (half + 1))
                wait(pe, s["x_lo"], k)
                for j in range(SUB):
                    mm = pe.transpose(bank[:, T_BANK, j * P:(j + 1) * P], x_rows_sb[:, par, j, 0:D], ident[:, :])
                mm.then_inc(s["x_ps"], 1)

            def hidden(k, par, c):
                if routed:
                    wh, wl, xh, xl = w1_hi[:, par, c, :], w1_lo[:, par, c, :], xb_hi[:, par, :], xb_lo[:, par, :]
                    if c == 0:
                        pe.wait_ge(s["w1_lo"], k + 1)
                        pe.wait_ge(s["x_lo"], k + 1)
                else:
                    at_k = slice(k, k + 1)
                    if s is sh[1] and c == 0:
                        pe.wait_ge(rt[0]["xT_lo"], NSH + k + 1)
                    wh, wl = ws1_hi[:, c, :], ws1_lo[:, c, :]
                    xh = xT_hi[:, at_k, :].rearrange("p o n -> p (o n)")
                    xl = xT_lo[:, at_k, :].rearrange("p o n -> p (o n)")
                wait(pe, s["h_lo"], FC * (k - 1) + c + 1)
                product(bank[:, H_BANK + c, :], wh, wl, xh, xl, True, True).then_inc(s["h_ps"], 1)

            def output(k, par, c):
                if routed:
                    wh, wl = w2_hi[:, par, c, :], w2_lo[:, par, c, :]
                    if c == 0:
                        pe.wait_ge(s["w2_lo"], k + 1)
                else:
                    wh, wl = ws2_hi[:, c, :], ws2_lo[:, c, :]
                if c == 0:
                    wait(pe, s["yT"], k - 1)
                pe.wait_ge(s["h_lo"], FC * k + c + 1)
                product(bank[:, O_BANK + par, :], wh, wl, h_hi[:, c, :], h_lo[:, c, :],
                        c == 0, c == FC - 1).then_inc(s["h_used"], 1)

            def turn_y(k, par):
                pe.wait_ge(s["yT"], k + 1)
                wait(pe, s["rows"], k * (2 if routed else 1))
                if after and k == lo:
                    pe.wait_ge(after["rows"], 2 * NEX)
                for j in range(SUB):
                    mm = pe.transpose(bank[:, Y_BANK, j * P:(j + 1) * P], yT[:, par, j * P:(j + 1) * P], ident[:, :])
                mm.then_inc(s["rows_ps"], 1)

            def body(k, par, half):
                for c in range(FC):
                    if beside:
                        beside(k, c)
                    if exists(k - lo, count - lo):
                        hidden(k, par, c)
                    if exists(k - 1 - lo, count - lo):
                        output(k - 1, 1 - par, c)
                    if c == 1 and routed and exists(k + 1, count):
                        turn_x(k + 1, 1 - par, half + par)
                    if c == 2 and exists(k - 2 - lo, count - lo):
                        turn_y(k - 2, par)

            if routed:
                turn_x(0, 0, 0)
            steps(pe, lo, count + 2, lo if beside else 4, lo if beside else count - 2, body)

        def act_turned(act, s, t, before, o):
            act.wait_ge(s["xT_ps"], before + t + 1)
            act.activation(xT_hi[:, t, :], o, ACT.Copy).then_inc(s["xT_hi"], 1)

        def act_route(act):
            def beside(k, place):
                if k + AHEAD < NSH and place == 0:
                    act_turned(act, rt[0], k + AHEAD, 0, bank[:, T_BANK, :])

            for k in range(-AHEAD, 0):
                beside(k, 0)
            return beside

        def act_gates(act, s):
            act.wait_ge(s["counted"], NSH)
            act.activation(gap[:, :], gap[:, :], ACT.Exp).then_inc(s["exp"], 1)

        def act_turned_again(act, first):
            def beside(k, place):
                b = k + 1
                if place == 0 and b < (NSH if first else EARLY + 1):
                    act_turned(act, rt[0], b, NSH, bank[:, T_BANK, :])

            if not first:
                beside(-1, 0)
            return beside

        def act_blocks(act, s, f, count, routed, beside=None, lo=0):
            def expert(k):
                at_k = slice(k, k + 1) if isinstance(k, int) else bass.ds(k, 1)
                return act.value_load(blk_e[0:1, at_k], min_val=0, max_val=E - 1)

            def x_hi(k, par):
                act.wait_ge(s["x_ps"], k + 1)
                wait(act, s["h_ps"], FC * (k - 1))
                act.activation(xb_hi[:, par, :], bank[:, T_BANK, :], ACT.Copy).then_inc(s["x_hi"], 1)

            def relu(k, c, e):
                bias = bs1_col[:, c:c + 1] if e is None else b1_col[:, bass.ds(e * FC + c, 1)]
                act.wait_ge(s["h_ps"], FC * k + c + 1)
                act.activation(bank[:, H_BANK + c, :], bank[:, H_BANK + c, :], ACT.Relu, bias=bias)\
                   .then_inc(s["relu"], 1)

            def hi(k, c):
                act.wait_ge(s["relu"], FC * k + c + 1)
                wait(act, s["h_used"], FC * (k - 1) + c + 1)
                act.activation(h_hi[:, c, :], bank[:, H_BANK + c, :], ACT.Copy).then_inc(s["h_hi"], 1)

            def y(k, par):
                e = expert(k) if routed else None
                bias = bs2_col[:, 0:1] if e is None else b2_col[:, bass.ds(e, 1)]
                act.wait_ge(s["h_used"], FC * (k + 1))
                wait(act, s["rows_ps"], k - 1)
                act.activation(yT[:, par, :], bank[:, O_BANK + par, :], ACT.Identity, bias=bias)\
                   .then_inc(s["yT"], 1)

            def body(k, par, half):
                if exists(k - lo, count - lo):
                    e = expert(k) if routed else None
                    for c in range(FC):
                        if beside:
                            beside(k, c)
                        relu(k, c, e)
                        if c == 1 and routed and exists(k + 1, count):
                            x_hi(k + 1, 1 - par)
                        hi(k, c)
                if exists(k - 1 - lo, count - lo):
                    y(k - 1, 1 - par)

            if routed:
                act.wait_ge(rt[f]["blk"], 1)
                x_hi(0, 0)
            steps(act, lo, count + 1, lo if beside else 4, lo if beside else count - 2, body)

        def tile(k, j=0):
            return slice(k + j, k + j + 1) if isinstance(k, int) else bass.ds(k + j, 1)

        def kind(s):
            return 1 if s is at else 0

        def entry(b):
            return slice(b * QT, (b + 1) * QT) if isinstance(b, int) else bass.ds(b * QT, QT)

        def dve_stats(dve, s, t, par, j):
            if j == 0:
                alone(dve)
            dve.bn_stats(bn[:, kind(s), par, j, :], X[:, tile(t * QT, j), :].rearrange("p o d -> p (o d)"))\
               .then_inc(s["stats"], 1)

        def dve_aggregate(dve, s, t, par):
            dve.wait_ge(s["stats"], QT * (t + 1))
            wait(dve, s["xn"], QT * (t - 1 if isinstance(t, int) else t))
            alone(dve)
            for j in range(QT):
                dve.bn_aggr(mv[:, kind(s), par, j, :], bn[:, kind(s), par, j, :]).then_inc(s["mv"], 1)

        def pool_rstd(pool, s, t, par):
            k = kind(s)
            pool.wait_ge(s["mv"], QT * (t + 1))
            wait(pool, s["rstd"], t)
            pool.tensor_scalar(vare[:, k, :], mv[:, k, par, :, 1], 1e-5, None, ALU.add).then_inc(s["var"], 1)
            pool.wait_ge(s["var"], t + 1)
            pool.tensor_tensor(rstd[:, k, par, :], vare[:, k, :], neg_half[:, :], ALU.pow).then_inc(s["rstd"], 1)

        def dve_norm(dve, s, t, par, to, j):
            k = kind(s)
            if j == 0:
                dve.wait_ge(s["rstd"], t + 1)
            dve.tensor_scalar(to[:, j, 0:D], X[:, tile(t * QT, j), :].rearrange("p o d -> p (o d)"),
                              mv[:, k, par, j, 0:1], rstd[:, k, par, j:j + 1], ALU.subtract, ALU.mult)\
               .then_inc(s["xn"], 1)

        def wide(ap, n, axis):
            shape = list(ap.shape)
            return ap.unsqueeze(axis).to_broadcast(shape[:axis] + [n] + shape[axis:])

        TOP_STEPS, MATHS = 6, 2 * QT + 8
        MATHS_ALL = MATHS * NSH

        def dve_top(dve, s, b, o, to, i):
            at_b, done = entry(b), MATHS * b
            if i == 0:
                dve.wait_ge(s["logit_ps"], b + 1)
                dve.tensor_copy(logits[:, :, :].rearrange("p t e -> p (t e)"), o[:, 0:QT * E]).then_inc(s["logits"], 1)
            elif i == 1:
                dve.wait_ge(s["logits"], b + 1)
                alone(dve)
                for j in range(QT):
                    dve.max(top_v[:, j, :], logits[:, j, :]).then_inc(s["maths"], 1)
            elif i == 2:
                dve.wait_ge(s["maths"], done + QT)
                alone(dve)
                for j in range(QT):
                    dve.max_index(top_i[:, j, :], top_v[:, j, :], logits[:, j, :]).then_inc(s["maths"], 1)
            elif i == 3:
                dve.wait_ge(s["maths"], done + 2 * QT)
                dve.tensor_tensor(gap[:, at_b], top_v[:, :, 1], top_v[:, :, 0], ALU.subtract).then_inc(s["maths"], 1)
                dve.tensor_copy(to[:, :, D], token_row[:, at_b]).then_inc(s["maths"], 1)
                dve.tensor_copy(to[:, :, D + 1], top_i[:, :, 0]).then_inc(s["maths"], 1)
                dve.tensor_copy(top_f[:, at_b, :], top_i[:, :, 0:2]).then_inc(s["maths"], 1)
            elif i == 4:
                dve.wait_ge(s["maths"], done + 2 * QT + 4)
                dve.tensor_tensor(hot[:, :, :, :].rearrange("p t j e -> p (t j) e"), wide(iota_e[:, :], 2 * QT, 1),
                                  wide(top_f[:, at_b, :].rearrange("p t j -> p (t j)"), E, 2), ALU.is_equal)\
                   .then_inc(s["maths"], 1)
            elif i == 5:
                dve.wait_ge(s["maths"], done + 2 * QT + 5)
                dve.tensor_tensor(hot_bf[:, :, :], hot[:, :, 0, :], hot[:, :, 1, :], ALU.add).then_inc(s["hot"], 1)

        PLACE_STEPS = 4

        def dve_place(dve, s, b, o, i):
            done = MATHS * b + 2 * QT + 5
            if i == 0:
                dve.wait_ge(s["count_ps"], b + 1)
                dve.tensor_tensor(row[:, :, :], o[:, 0:QT * E].rearrange("p (t e) -> p t e", e=E),
                                  wide(next_row[:, :], QT, 1), ALU.add).then_inc(s["maths"], 1)
                dve.wait_ge(s["maths"], done + 1)
                dve.tensor_tensor(next_row[:, :], next_row[:, :], o[:, QT * E:(QT + 1) * E], ALU.add)\
                   .then_inc(s["counted"], 1)
            elif i == 1:
                dve.wait_ge(s["counted"], b + 1)
                dve.tensor_tensor(hot[:, :, :, :], hot[:, :, :, :], wide(row[:, :, :], 2, 2), ALU.mult)\
                   .then_inc(s["maths"], 1)
            elif i == 2:
                dve.wait_ge(s["maths"], done + 2)
                dve.tensor_reduce(row_f[:, entry(b), :], hot[:, :, :, :], AX.X, ALU.add).then_inc(s["maths"], 1)
            elif i == 3:
                dve.wait_ge(s["maths"], done + 3)
                dve.tensor_copy(row_i[:, entry(b), :], row_f[:, entry(b), :]).then_inc(s["rows"], 1)

        def dve_blocks_of(dve, s):
            done = MATHS_ALL

            def then(op):
                nonlocal done
                op.then_inc(s["maths"], 1)
                done += 1
                dve.wait_ge(s["maths"], done)

            dve.wait_ge(s["counted"], NSH)
            then(dve.tensor_tensor(size[:, :], next_row[:, :], region_start[:, :], ALU.subtract))
            then(dve.tensor_copy(size_i[:, :], size[0:1, :]))
            then(dve.tensor_scalar(blocks_i[:, :], size[:, :], float(BLK - 1), None, ALU.add))
            then(dve.tensor_scalar(blocks_i[:, :], blocks_i[:, :], LOGBLK, None, ALU.logical_shift_right))
            then(dve.tensor_copy(blocks[:, :], blocks_i[:, :]))
            then(dve.tensor_tensor_scan(blocks_upto[:, :], scan_one[:, :], blocks[:, :], 0.0, ALU.mult, ALU.add))
            then(dve.tensor_tensor(blk_cmp[:, :, :], wide(blocks_upto[:, :], NEX, 1), wide(iota_b[:, :], E, 2), ALU.is_le))
            then(dve.tensor_reduce(blk_f[:, :], blk_cmp[:, :, :], AX.X, ALU.add))
            then(dve.tensor_scalar(blk_expert[:, :], blk_f[:, :], float(E - 1), None, ALU.min))
            then(dve.tensor_copy(blk_e[:, :], blk_expert[0:1, :]))
            then(dve.tensor_scalar(unused[:, :], blocks[:, :], -1.0, float(REGION // BLK), ALU.mult, ALU.add))
            then(dve.tensor_tensor(blk_cmp[:, :, :], blk_cmp[:, :, :], wide(unused[:, :], NEX, 1), ALU.mult))
            then(dve.tensor_reduce(blk_f[:, :], blk_cmp[:, :, :], AX.X, ALU.add))
            dve.tensor_tensor(blk_at[:, :], blk_f[0:1, :], iota_b[0:1, :], ALU.add).then_inc(s["blk"], 1)

        def dve_gates(dve, s):
            dve.wait_ge(s["exp"], 1)
            dve.tensor_scalar(gate[:, 1, :], gap[:, :], 1.0, 2.0, ALU.add, ALU.mult).then_inc(s["gap"], 1)
            dve.wait_ge(s["gap"], 1)
            dve.reciprocal(gate[:, 0, :], gate[:, 1, :]).then_inc(s["gap"], 1)
            dve.wait_ge(s["gap"], 2)
            dve.tensor_tensor(gate[:, 1, :], gate[:, 0, :], gap[:, :], ALU.mult).then_inc(s["gap"], 1)
            dve.wait_ge(s["gap"], 3)

        def dve_route(dve):
            s = rt[0]
            o = bank[:, T_BANK, :]

            def stats(b):
                for j in range(QT):
                    dve_stats(dve, s, b, b % 2, j)

            def norm(b):
                for j in range(QT):
                    dve_norm(dve, s, b, b % 2, xn[:, SUB * b:SUB * (b + 1), :], j)

            def beside(k, place):
                b = k + AHEAD
                if place == 0 and b < NSH:
                    dve_xT_lo(dve, s, b, 0, o)
                    if b + 2 < NSH:
                        stats(b + 2)
                elif place == 1 and b < NSH:
                    if b + 2 < NSH:
                        dve_aggregate(dve, s, b + 2, b % 2)
                    for i in range(TOP_STEPS):
                        dve_top(dve, s, b, o, xn[:, QT * b:QT * (b + 1), :], i)
                elif place == 2 and b + 1 < NSH:
                    norm(b + 1)
                elif place == 3 and b < NSH:
                    for i in range(PLACE_STEPS):
                        dve_place(dve, s, b, o, i)
                    if b == NSH - 1:
                        dve_blocks_of(dve, s)
                elif place == 4 and k == NSH + 1:
                    dve_gates(dve, s)

            dve.wait_ge(x_first, 16)
            stats(0)
            dve_aggregate(dve, s, 0, 0)
            norm(0)
            dve.wait_ge(x_loaded, 16)
            stats(1)
            dve_aggregate(dve, s, 1, 1)
            for k in range(-AHEAD, 0):
                for place in range(4):
                    beside(k, place)
            dve_shared_weights(dve)
            return beside

        def dve_shared_weights(dve):
            dve.wait_ge(const_in, 16 * LOADS)
            dve.tensor_copy(ws1_hi[:, :, :], ws1_raw.rearrange("d (p c) -> d c p", c=FC)).then_inc(dve_const, 1)
            dve.tensor_copy(ws2_hi[:, :, :].rearrange("p c d -> p (c d)"), ws2_raw).then_inc(dve_const, 1)
            dve.tensor_scalar(bqs_col[:, :], bq_col[:, :], SCALE, None, ALU.mult).then_inc(dve_const, 1)
            dve.wait_ge(dve_const, 8)
            dve.tensor_tensor(ws1_lo[:, :, :], ws1_raw.rearrange("d (p c) -> d c p", c=FC),
                              ws1_hi[:, :, :].bitcast(F32), ALU.subtract).then_inc(dve_const, 1)
            dve.tensor_tensor(ws2_lo[:, :, :].rearrange("p c d -> p (c d)"), ws2_raw,
                              ws2_hi[:, :, :].rearrange("p c d -> p (c d)").bitcast(F32), ALU.subtract)\
               .then_inc(dve_const, 1)

        def dve_xT_lo(dve, s, t, before, o):
            dve.wait_ge(s["xT_hi"], before + t + 1)
            dve.tensor_tensor(xT_lo[:, t, :], o, xT_hi[:, t, :].bitcast(F32), ALU.subtract)\
               .then_inc(s["xT_lo"], 1)

        COMBINED_AT = ((), (), (0, 1), (2,), (3, 4), (5,), (6,), (7,))

        def dve_turned_again(dve, first):
            def beside(k, place):
                b = k + 1
                if place == 0 and b < (NSH if first else EARLY + 1):
                    dve_xT_lo(dve, rt[0], b, NSH, bank[:, T_BANK, :])
                if place == FC and first:
                    for e in COMBINED_AT[k - first]:
                        if e <= k - 2:
                            dve.wait_ge(sh[1]["rows"], e + 1)
                        for i in range(2 * QT):
                            dve_combine(dve, rt[1], e, e % 2, e // 2, i)

            if not first:
                beside(-1, 0)
            return beside

        def dve_blocks(dve, s, count, routed, beside=None, lo=0):
            def w1(k, par, half):
                dve.wait_ge(s["loaded"][par], 48 * (half + 1))
                wait(dve, s["h_ps"], FC * (k - 1))
                dve.tensor_copy(w1_hi[:, par, :, :], w1_raw[:, par, :].rearrange("d (p c) -> d c p", c=FC))\
                   .then_inc(s["w1_hi"], 1)

            def results(k, par, half):
                at_k = slice(k, k + 1) if isinstance(k, int) else bass.ds(k, 1)
                alone(dve)
                dve.scalar_tensor_tensor(result[:, at_k, :].rearrange("p o s -> p (o s)"), x_rows_sb[:, par, :, D + 1],
                                         blk_expert[:, at_k], x_rows_sb[:, par, :, D], ALU.not_equal, ALU.add)\
                   .then_inc(s["result"], 1)
                if par:
                    dve.tensor_scalar(aside_rows[:, :], x_rows_sb[:, par, :, D + 1], 0.0, float(BLK), ALU.is_lt, ALU.mult)\
                       .then_inc(s["result"], 1)
                if par:
                    r = result[:, at_k, :].rearrange("p o s -> p (o s)")
                    dve.wait_ge(s["result"], 4 * half + 3)
                    dve.tensor_tensor(r, r, aside_rows[:, :], ALU.add).then_inc(s["result"], 1)

            def w1_low(k, par):
                dve.wait_ge(s["w1_hi"], k + 1)
                dve.tensor_tensor(w1_lo[:, par, :, :], w1_raw[:, par, :].rearrange("d (p c) -> d c p", c=FC),
                                  w1_hi[:, par, :, :].bitcast(F32), ALU.subtract).then_inc(s["w1_lo"], 1)

            def w2(k, par, half):
                dve.wait_ge(s["loaded"][par], 48 * (half + 1))
                wait(dve, s["h_used"], FC * (k - 1))
                dve.tensor_copy(w2_hi[:, par, :, :].rearrange("p c d -> p (c d)"), w2_raw[:, par, :])\
                   .then_inc(s["w2_hi"], 1)

            def x_lo(k, par):
                dve.wait_ge(s["x_hi"], k + 1)
                dve.tensor_tensor(xb_lo[:, par, :], bank[:, T_BANK, :], xb_hi[:, par, :].bitcast(F32), ALU.subtract)\
                   .then_inc(s["x_lo"], 1)

            def h_low(k, c):
                dve.wait_ge(s["h_hi"], FC * k + c + 1)
                dve.tensor_tensor(h_lo[:, c, :], bank[:, H_BANK + c, :], h_hi[:, c, :].bitcast(F32), ALU.subtract)\
                   .then_inc(s["h_lo"], 1)

            def rows(k, par, half):
                dve.wait_ge(s["rows_ps"], k + 1)
                if routed:
                    wait(dve, s["stored"][par], 16 * SUB * half)
                    dve.wait_ge(s["result"], 4 * half + (4 if par else 1))
                    at_k = slice(k, k + 1) if isinstance(k, int) else bass.ds(k, 1)
                    dve.tensor_copy(result_i[:, par, :], result[:, at_k, :].rearrange("p o s -> p (o s)"))\
                       .then_inc(s["rows"], 1)
                    dve.tensor_copy(y_rows[:, par, :, 0:D], bank[:, Y_BANK, :].rearrange("p (s d) -> p s d", d=D))\
                       .then_inc(s["rows"], 1)
                else:
                    xk = X[:, k * SUB:(k + 1) * SUB, :]
                    if lo:
                        dve.wait_ge(rt[1]["combined"], 2 * QT * sum(len(es) for es in COMBINED_AT[:k - lo + 2]))
                    dve.scalar_tensor_tensor(xk, bank[:, Y_BANK, :].rearrange("p (s d) -> p s d", d=D), 0.5, xk,
                                             ALU.mult, ALU.add).then_inc(s["rows"], 1)

            def body(k, par, half):
                if exists(k - lo, count - lo):
                    if routed:
                        w2(k, par, half)
                    for c in range(FC):
                        if beside:
                            beside(k, c)
                        h_low(k, c)
                        if c == 0 and routed and exists(k + 1, count):
                            w1(k + 1, 1 - par, half + par)
                            x_lo(k + 1, 1 - par)
                            w1_low(k + 1, 1 - par)
                        if c == 2 and routed and exists(k + 1, count):
                            results(k + 1, 1 - par, half + par)
                if exists(k - 2 - lo, count - lo):
                    rows(k - 2, par, half - 1)
                if beside:
                    beside(k, FC)
            if routed:
                w1(0, 0, 0)
                w1_low(0, 0)
                x_lo(0, 0)
                results(0, 0, 0)
            steps(dve, lo, count + 2, lo if beside else 4, lo if beside else count - 2, body)

        def dve_combine(dve, s, t, par, half, i):
            e, j = i // QT, i % QT
            if i == 0:
                dve.wait_ge(s["picked"][par], 16 * (half + 1))
            x = X[:, tile(t * QT, j), :].rearrange("p o d -> p (o d)")
            if e:
                dve.wait_ge(s["combined"], 2 * QT * t + j + 1)
            dve.scalar_tensor_tensor(x, picked[:, par, j, e, :], gate[:, e, tile(t * QT, j)], x,
                                     ALU.mult, ALU.add).then_inc(s["combined"], 1)
            if i == 2 * QT - 1:
                dve.wait_ge(s["combined"], 2 * QT * (t + 1))

        def pool_scatter(pool, f, b, rows):
            s = rt[f]
            if f == 0 and b == 0:
                pool.wait_ge(pads_in, 32)
            pool.wait_ge(s["rows"], b + 1)
            for t in range(QT):
                for j in range(2):
                    pool.indirect_dma_start(xs, bass.IndirectOffsetOnAxis(ap=row_i[:, QT * b + t, j:j + 1], axis=0),
                                            rows[:, t, :], None).then_inc(s["scattered"][b % 2], 16)

        def pool_route(pool):
            for b in range(2):
                pool_rstd(pool, rt[0], b, b)
            for b in range(NSH):
                if b + 2 < NSH:
                    pool_rstd(pool, rt[0], b + 2, b % 2)
                pool_scatter(pool, 0, b, xn[:, QT * b:QT * (b + 1), :])

        def pool_blocks(pool, s, count):
            def w2(k, par):
                pool.wait_ge(s["w2_hi"], k + 1)
                pool.tensor_tensor(w2_lo[:, par, :, :].rearrange("p c d -> p (c d)"), w2_raw[:, par, :],
                                   w2_hi[:, par, :, :].rearrange("p c d -> p (c d)").bitcast(F32), ALU.subtract)\
                    .then_inc(s["w2_lo"], 1)

            def send(k, par, half):
                pool.wait_ge(s["rows"], 2 * (k + 1))
                alone(pool)
                for j in range(SUB):
                    pool.indirect_dma_start(ys, bass.IndirectOffsetOnAxis(ap=result_i[:, par, j:j + 1], axis=0),
                                            y_rows[:, par, j, 0:D], None).then_inc(s["stored"][par], 16)

            def body(k, par, half):
                if exists(k, count):
                    w2(k, par)
                if exists(k - 3, count):
                    send(k - 3, 1 - par, half - 2 + par)
                if s is ex[0] and isinstance(k, int) and k < count:
                    if k == 0:
                        pool.wait_ge(sh[0]["h_ps"], FC * NSH)
                    if k in (2, 3):
                        return
                    g = k if k < 2 else k - count + 4
                    pool.memset(k_st[:, g, :, :].bitcast(F32), 0.0).then_inc(at["init"], 1)
                    if g == 1:
                        pool.memset(v_st[:, :, :, :, :], 0.0).then_inc(at["init"], 1)
                    if g == 3:
                        pool.wait_ge(at["init"], 4)
                        pool.memset(v_st[:, :, :, :, HD], 1.0).then_inc(at["init"], 1)

            steps(pool, 0, count + 3, 4, count - 2, body)

        def sp_blocks(sp, s, f, count):
            def load(k, par, half):
                at_k = slice(k, k + 1) if isinstance(k, int) else bass.ds(k, 1)
                e = sp.value_load(blk_e[0:1, at_k], min_val=0, max_val=E - 1)
                rows_k = bass.ds(sp.value_load(blk_at[0:1, at_k], min_val=0, max_val=ROWS // BLK - 1) * BLK, BLK)
                wait(sp, s["w1_lo"], k - 1)
                wait(sp, s["w2_lo"], k - 1)
                wait(sp, s["x_ps"], k - 1)
                wait(sp, s["result"], 4 * half - (0 if par else 3))
                alone(sp)
                sp.dma_start(w1_raw[:, par, :], W1[bass.ds(e, 1), :, :].rearrange("o d f -> (o d) f"))\
                  .then_inc(s["loaded"][par], 16)
                sp.dma_start(x_rows_sb[:, par, :, :], xs[rows_k, :].rearrange("(s p) d -> p s d", p=P))\
                  .then_inc(s["loaded"][par], 16)
                sp.dma_start(w2_raw[:, par, :], W2[bass.ds(e, 1), :, :].rearrange("o (p c) d -> (o p) (c d)", c=FC))\
                  .then_inc(s["loaded"][par], 16)

            def body(k, par, half):
                load(k, par, half)

            sp.wait_ge(rt[f]["maths"], MATHS_ALL + 2)
            for e in range(E):
                used = sp.value_load(size_i[0:1, e:e + 1], min_val=0, max_val=T)
                sp.dma_start(xs[bass.ds(used + e * REGION, BLK), :].rearrange("(p s) d -> p s d", p=P),
                             no_tokens[:, :, :]).then_inc(rt[f]["filled"], 16)
            sp.wait_ge(rt[f]["blk"], 1)
            sp.wait_ge(rt[f]["filled"], 16 * E)
            for p in range(2):
                sp.wait_ge(rt[f]["scattered"][p], 16 * 2 * NT // 2)
            steps(sp, 0, count, 2, count, body)

        def sp_pick(sp, f, b, par):
            if isinstance(b, int) and b < 2:
                for p in range(2):
                    sp.wait_ge(ex[f]["stored"][p], 16 * SUB * NEX // 2)
            else:
                sp.wait_ge(rt[f]["combined"], 2 * QT * (b - 1))
                alone(sp)
            per = 2 * QT * P
            rows = slice(b * per, (b + 1) * per) if isinstance(b, int) else bass.ds(b * per, per)
            sp.dma_start(picked[:, par, :, :, :].rearrange("p q j d -> p q (j d)"),
                         ys[rows, :].rearrange("(q p j) d -> p q (j d)", p=P, j=2)).then_inc(rt[f]["picked"][par], 16)

        FIRST_ROUND, ROUNDS = -2, BATCH + 2
        ST_BANK, S_BANK, CTX_BANK, MISC_BANK = 0, 2, 6, 7
        STEPS = G * QT * R
        MISC = {2: ("logit", -2, 0), 6: ("nmaxT", 0, 1), 10: ("turn", -1, G - 1), 14: ("ctxT", -1, 0),
                18: ("o", -1, 0), 22: ("nmaxT", 0, 2), 26: ("turn", 0, 0), 28: ("v", 1, 0), 31: ("xT", 2, 0),
                35: ("q", 2, 0), 39: ("nmaxT", 0, 3), 43: ("turn", 0, 1), 46: ("k", 2, 0), 50: ("count", -2, 0),
                54: ("nmaxT", 1, 0), 58: ("turn", 0, 2), 62: ("rT", -1, 0)}
        for name, (made, read) in dict(rT=("xT_ps", "xT_lo"), logit=("logit_ps", "logits"),
                                       count=("count_ps", "counted")).items():
            at[name + "_ps"], at[name] = rt[1][made], rt[1][read]
        READ = {"rT": "rT", "logit": "logit", "count": "count", "nmaxT": "nmaxT", "turn": "turned",
                "ctxT": "ctxT", "o": "added", "v": "v", "xT": "xT", "q": "q", "k": "k"}

        def number(what, b, g):
            return G * b + g + 1 if what in ("nmaxT", "turn") else b + 1

        def present(t, what, db, g):
            return exists(t + db, BATCH)

        def misc_before(t, step):
            keys = sorted(MISC)
            i, u = keys.index(step), t
            while True:
                i -= 1
                if i < 0:
                    i, u = len(keys) - 1, (u - 1 if isinstance(u, int) else t - 1)
                    if isinstance(u, int) and u < FIRST_ROUND:
                        return None
                what, db, g = MISC[keys[i]]
                if present(u, what, db, g):
                    return what, number(what, u + db, g)

        def entry_ahead(t, j):
            ahead = j + 2 * QT * R
            return t + ahead // STEPS, ahead % STEPS

        def heads(ap, r, rows):
            return ap[RP * r:RP * r + rows]

        def pe_attention(pe):
            def scores(b, j):
                g, qt, r = j // (QT * R), j // R % QT, j % R
                if j % (QT * R) == 0:
                    pe.wait_ge(stack_in[g % 2], 16 * (R + 2) * (G // 2 * b + g // 2 + 1))
                if j % 2 == 0:
                    wait(pe, at["s_read"], STEPS // 2 * b + j // 2 - 1)
                mm = pe.matmul(bank[:, S_BANK + j % 4, :], q_st[:, g, qt * P:(qt + 1) * P], k_st[:, g, r, :],
                               start=True, stop=True)
                if j % 2:
                    mm.then_inc(at["s_ps"], 1)

            def scores_t(b, s):
                g, kt, r = s // (QT * R), s // R % QT, s % R
                if s % (QT * R) == 0:
                    pe.wait_ge(nmax_in[g % 2], 16 * (G // 2 * b + g // 2 + 1))
                wait(pe, at["probs"], STEPS * b + s - 1)
                pe.matmul(bank[:, ST_BANK + s % 2, :], k_st[:, g, r, kt * P:(kt + 1) * P],
                          q_st[:, g, :], start=True, stop=True).then_inc(at["st_ps"], 1)

            def context(b, par, q):
                g, kt = q // QT, q % QT
                pe.wait_ge(at["probs"], STEPS * b + R * (q + 1))
                if q == 0:
                    pe.wait_ge(at["v"], b + 1)
                if kt == 0:
                    wait(pe, at["ctx_raw"], G * b + g)
                for r in range(R):
                    mm = pe.matmul(heads(bank, r, RP)[:, CTX_BANK, :], v_st[:, par, kt, g * R + r, :],
                                   probs[:, (R * q + r) % RING, :], start=kt == 0, stop=kt == QT - 1)
                mm.then_inc(at["pv_ps"], 1)

            def misc(t, par, step):
                what, db, g = MISC[step]
                b = t + db
                before = misc_before(t, step)
                if before:
                    pe.wait_ge(at[READ[before[0]]], before[1])
                o = bank[:, MISC_BANK, :]
                if what == "rT":
                    pe.wait_ge(rt[1]["xn"], QT * (b + 1))
                    return pe_turn(pe, rt[1], b, xr[:, 1 - par, :, :], o)
                if what == "logit":
                    pe.wait_ge(rt[1]["xT_lo"], b + 1)
                    return pe_logits(pe, rt[1], o, xrT_hi, xrT_lo)
                if what == "count":
                    pe.wait_ge(rt[1]["hot"], b + 1)
                    return pe_count(pe, rt[1], o)
                if what == "nmaxT":
                    pe.wait_ge(at["nmax_parts"], 2 * (G * b + g + 1))
                    mm = pe.transpose(o[0:2 * R * QT, 0:P],
                                      nmax_parts[:, g % 2].rearrange("p r h q -> p (r h q)"), ident[:, :])
                elif what == "turn":
                    pe.wait_ge(at["ctx_raw"], G * b + g + 1)
                    for j in range(QT):
                        mm = pe.transpose(o[:, j * P:(j + 1) * P], ctx_raw[:, j * P:(j + 1) * P], ident[:, :])
                elif what == "ctxT":
                    pe.wait_ge(at["turned"], G * (b + 1))
                    for j in range(QT):
                        mm = pe.transpose(o[:, j * P:(j + 1) * P], ctx_n[:, j, :], ident[:, :])
                elif what == "o":
                    pe.wait_ge(at["ctxT"], b + 1)
                    for j in range(QT):
                        mm = pe.matmul(o[:, j * P:(j + 1) * P], ctxT[:, j * P:(j + 1) * P], wo[:, :],
                                       start=True, stop=True)
                elif what == "v":
                    pe.wait_ge(at["xT"], b + 1)
                    for j in range(QT):
                        mm = pe.matmul(o[:, j * P:(j + 1) * P], xnT[:, j * P:(j + 1) * P], wv[:, :],
                                       start=True, stop=True)
                elif what == "xT":
                    pe.wait_ge(at["xn"], QT * (b + 1))
                    for j in range(QT):
                        mm = pe.transpose(o[:, j * P:(j + 1) * P], xa[:, par, j, 0:D], ident[:, :])
                elif what in ("q", "k"):
                    pe.wait_ge(at["xT"], b + 1)
                    mm = pe.matmul(o, (wq if what == "q" else wk)[:, :], xnT[:, :], start=True, stop=True)
                mm.then_inc(at[what + "_ps"], 1)

            def round_(t, par, half):
                for s in range(STEPS):
                    if exists(t, BATCH):
                        scores_t(t, s)
                    for j in {0: (s - 1,), 1: (), 2: (s - 2,), 3: (s - 2, s - 1)}[s % 4]:
                        ahead, of = entry_ahead(t, j)
                        if exists(ahead, BATCH):
                            scores(ahead, of)
                    if s == 1 and exists(t - 1, BATCH):
                        context(t - 1, 1 - par, G * QT - 1)
                    if s % R == 1 and s > R and exists(t, BATCH):
                        context(t, par, s // R - 1)
                    if s in MISC and present(t, *MISC[s]):
                        misc(t, par, s)

            pe.wait_ge(stack_const, 16 * STACK_CONSTS)
            pe.wait_ge(ex[0]["rows"], 2 * NEX)
            steps(pe, FIRST_ROUND, ROUNDS, LOOP[0], LOOP[1], round_)

        LOOP = (2, BATCH - 2)
        QK_PARTS = 2 * 3
        STACK_CONSTS = R

        def act_attention(act):
            def prob(b, s):
                act.wait_ge(at["st_ps"], STEPS * b + s + 1)
                wait(act, at["pv_ps"], G * QT * b + s // R - 1)
                act.activation(probs[:, s % RING, :], bank[:, ST_BANK + s % 2, :], ACT.Exp).then_inc(at["probs"], 1)

            def context_out(b, g):
                act.wait_ge(at["pv_ps"], QT * (G * b + g + 1))
                wait(act, at["turn_ps"], G * b + g)
                act.activation(ctx_raw[:, :], bank[:, CTX_BANK, :], ACT.Copy).then_inc(at["ctx_raw"], 1)

            def misc(t, par, half, step):
                what, db, g = MISC[step]
                b = t + db
                m = bank[:, MISC_BANK, :]
                act.wait_ge(at[what + "_ps"], number(what, b, g))
                if what == "ctxT":
                    act.activation(ctxT[:, :], m, ACT.Identity, bias=bv_col[:, 0:1]).then_inc(at["ctxT"], 1)
                elif what == "v":
                    v_par = 1 - par
                    act.activation(v_st[:, v_par, :, :, 0:HD].rearrange("p k h d -> p (k h) d"),
                                   m.rearrange("p (kh d) -> p kh d", d=HD), ACT.Copy).then_inc(at["v"], 1)
                elif what == "xT":
                    act.activation(xnT[:, :], m, ACT.Copy).then_inc(at["xT"], 1)
                elif what == "rT":
                    act.activation(xrT_hi, m, ACT.Copy).then_inc(rt[1]["xT_hi"], 1)
                elif what in ("q", "k"):
                    i = 0 if what == "q" else 1
                    act.activation(m, m, ACT.Identity, bias=(bqs_col if what == "q" else bk_col)[:, 0:1],
                                   scale=SCALE if what == "q" else 1.0).then_inc(at["qk_z"], 1)

            def qk_parts(t, step):
                what, db, g = MISC[step]
                b = t + db
                m = bank[:, MISC_BANK, :]
                if what in ("q", "k"):
                    i = 0 if what == "q" else 1
                    act.wait_ge(at["qk_z"], 2 * b + i + 1)
                    if not isinstance(b, int) or b > 0:
                        act.wait_ge(qk_out, 16 * QK_PARTS * (b + 1))
                    act.activation(qk_hi[:, i, :], m, ACT.Copy).then_inc(at["qk_hi"], 1)

            def round_(t, par, half):
                for s in range(STEPS):
                    if s == 4 and exists(t - 1, BATCH):
                        context_out(t - 1, G - 1)
                    if s % (QT * R) == 4 and s > QT * R and exists(t, BATCH):
                        context_out(t, s // (QT * R) - 1)
                    if exists(t, BATCH):
                        prob(t, s)
                    if s in MISC and MISC[s][0] in ("ctxT", "v", "xT", "q", "k", "rT") and present(t, *MISC[s]):
                        misc(t, par, half, s)
                    if s - 1 in MISC and present(t, *MISC[s - 1]):
                        qk_parts(t, s - 1)

            steps(act, FIRST_ROUND, ROUNDS, LOOP[0], LOOP[1], round_)

        TOP_AT, PLACE_AT = (5, 8, 12, 14, 17), (53, 55, 57)

        def dve_attention(dve):
            def maxima(b, j):
                g, qt, r = j // (QT * R), j // R % QT, j % R
                dve.wait_ge(at["s_ps"], STEPS // 2 * b + j // 2 + 1)
                slot2 = S_BANK + j % 4 - 1
                dve.tensor_reduce(nmax[:, g % 2, r - 1:r + 1, qt], bank[:, slot2:slot2 + 2, :],
                                  AX.X, ALU.max, negate=True).then_inc(at["s_read"], 1)

            def max_parts(b, g):
                n = G * b + g
                hi, lo = nmax_parts[:, g % 2, :, 0, :], nmax_parts[:, g % 2, :, 1, :]
                dve.wait_ge(at["s_read"], 2 * QT * (n + 1))
                wait(dve, at["nmaxT_ps"], n - 1)
                dve.tensor_copy(hi.bitcast(F32R), nmax[:, g % 2, :, :]).then_inc(at["nmax_parts"], 1)
                dve.wait_ge(at["nmax_parts"], 2 * n + 1)
                dve.tensor_tensor(lo.bitcast(F32R), nmax[:, g % 2, :, :], hi, ALU.subtract)\
                   .then_inc(at["nmax_parts"], 1)

            def misc(t, par, half, step):
                what, db, g = MISC[step]
                b = t + db
                m = bank[:, MISC_BANK, :]
                if what == "rT":
                    dve.wait_ge(rt[1]["xT_hi"], b + 1)
                    dve.tensor_tensor(xrT_lo, m, xrT_hi.bitcast(F32), ALU.subtract).then_inc(rt[1]["xT_lo"], 1)
                elif what == "logit":
                    dve_top(dve, rt[1], b, m, None, 0)
                elif what == "count":
                    dve_place(dve, rt[1], b, m, 0)
                elif what == "nmaxT":
                    n = G * b + g
                    dve.wait_ge(at["nmaxT_ps"], n + 1)
                    wait(dve, nmax_in[1 - g % 2], 16 * (G // 2 * b + (g + 1) // 2))
                    dve.tensor_copy(nmaxT[:, :], m[0:2 * R * QT, 0:P]).then_inc(at["nmaxT"], 1)
                elif what == "turn":
                    n = G * b + g
                    mv4 = m.rearrange("p (q r c) -> p q r c", r=R, c=RP)
                    dve.wait_ge(at["turn_ps"], n + 1)
                    if g == 0:
                        wait(dve, at["ctxT_ps"], b)
                    dve.reciprocal(rden[:, :, :], mv4[:, :, :, HD]).then_inc(at["rden"], 1)
                    dve.wait_ge(at["rden"], n + 1)
                    dve.tensor_tensor(ctx_n[:, :, g * R * HD:(g + 1) * R * HD].rearrange("p q (r d) -> p q r d", d=HD),
                                      mv4[:, :, :, 0:HD],
                                      rden[:, :, :].unsqueeze(3).to_broadcast([P, QT, R, HD]),
                                      ALU.mult).then_inc(at["turned"], 1)
                elif what == "o":
                    dve.wait_ge(at["biased"], b + 1)
                    dve.wait_ge(at["o_ps"], b + 1)
                    at_b = slice(b * QT, (b + 1) * QT) if isinstance(b, int) else bass.ds(b * QT, QT)
                    dve.tensor_tensor(X[:, at_b, :], m.rearrange("p (q d) -> p q d", d=D), X[:, at_b, :],
                                      ALU.add).then_inc(at["added"], 1)
                elif what in ("q", "k"):
                    i = 0 if what == "q" else 1
                    dve.wait_ge(at["qk_hi"], 2 * b + i + 1)
                    dve.tensor_tensor(qk_lo[:, i, :], m, qk_hi[:, i, :].bitcast(F32), ALU.subtract)\
                       .then_inc(at[what], 1)

            def round_(t, par, half):
                for s in range(STEPS):
                    if exists(t + 2, BATCH):
                        if s % 2 and s < 4 * QT:
                            dve_combine(dve, rt[0], t + 2, par, half + 1, s // 2)
                        if 4 * QT < s <= 5 * QT:
                            dve_stats(dve, at, t + 2, par, s - 4 * QT - 1)
                        if s == 5 * QT + 1:
                            dve_aggregate(dve, at, t + 2, par)
                        if 26 <= s < 26 + QT:
                            dve_norm(dve, at, t + 2, par, xa[:, par, :, :], s - 26)
                    if exists(t - 1, BATCH):
                        if s % 2 and 33 <= s < 33 + 2 * QT:
                            if s == 33:
                                dve.wait_ge(at["added"], t)
                            dve_stats(dve, rt[1], t - 1, 1 - par, (s - 33) // 2)
                        if s == 33 + 2 * QT:
                            dve_aggregate(dve, rt[1], t - 1, 1 - par)
                        if 45 <= s < 45 + QT:
                            if s == 45 and exists(t - 3, BATCH):
                                dve.wait_ge(kept, t - 1)
                            dve_norm(dve, rt[1], t - 1, 1 - par, xr[:, 1 - par, :, :], s - 45)
                    if exists(t - 2, BATCH):
                        if s in TOP_AT:
                            dve_top(dve, rt[1], t - 2, None, xr[:, par, :, :], TOP_AT.index(s) + 1)
                        if s in PLACE_AT:
                            dve_place(dve, rt[1], t - 2, None, PLACE_AT.index(s) + 1)
                    if s % 4 in (0, 3):
                        j = s - 1 if s % 4 == 0 else s - 2
                        ahead, of = entry_ahead(t, j)
                        if exists(ahead, BATCH):
                            maxima(ahead, of)
                            if of % (QT * R) == QT * R - 1:
                                max_parts(ahead, of // (QT * R))
                    if s in MISC and MISC[s][0] not in ("ctxT", "v", "xT") and present(t, *MISC[s]):
                        misc(t, par, half, s)

            steps(dve, FIRST_ROUND, ROUNDS, LOOP[0], LOOP[1], round_)

        def pool_attention(pool):
            pool.sem_inc(kept, 1)
            for t in range(FIRST_ROUND, ROUNDS):
                if t + 2 < BATCH:
                    pool_rstd(pool, at, t + 2, t % 2)
                    x = X[:, QT * (t + 2):QT * (t + 3), :]
                    pool.wait_ge(at["xn"], QT * (t + 3))
                    pool.tensor_tensor(x, x, bo_rows[:, :].unsqueeze(1).to_broadcast([P, QT, D]), ALU.add)\
                        .then_inc(at["biased"], 1)
                if 0 <= t - 1 < BATCH:
                    pool_rstd(pool, rt[1], t - 1, (t - 1) % 2)
                if 0 <= t - 2:
                    pool_scatter(pool, 1, t - 2, xr[:, t % 2, :, :])
                    pool.wait_ge(rt[1]["scattered"][t % 2], 16 * 2 * QT * (t // 2))
                    pool.tensor_copy(xn[:, QT * (t - 2):QT * (t - 1), :], xr[:, t % 2, :, :]).then_inc(kept, 1)

        def sp_attention(sp):
            def stack(b, par, g):
                if isinstance(b, int) and b == 0:
                    if g < 2:
                        sp.wait_ge(qk_out, 16 * QK_PARTS * (g + 1))
                elif g == 0:
                    sp.wait_ge(qk_out, 16 * QK_PARTS * (b + 2))
                    alone(sp)
                if not isinstance(b, int) or b > 0:
                    sp.wait_ge(at["st_ps"], STEPS * (b - 1) + QT * R * (g + 1))
                    alone(sp)
                elif g >= 2:
                    sp.wait_ge(at["s_ps"], QT * R // 2 * (g - 2) + 1)
                sp.dma_start(q_st[0:MAX_ROW, g, :].bitcast(F32),
                             q_dram[par][R * g:R * (g + 1)].rearrange("r x n -> (r x) n")).then_inc(stack_in[g % 2], 16)
                sp.dma_start(q_st[MAX_ROW:P, g, :].bitcast(F32),
                             zero_dram)\
                  .then_inc(stack_in[g % 2], 16)
                for r in range(R):
                    sp.dma_start(k_st[HK * r:HK * (r + 1), g, r, :].bitcast(F32), k_dram[par][R * g + r])\
                      .then_inc(stack_in[g % 2], 16)

            def maxima(b, g):
                n = G * b + g
                sp.wait_ge(at["nmaxT"], n + 1)
                alone(sp)
                sp.dma_start(q_st[MAX_ROW:MAX_ROW + 2 * R, g, :].bitcast(F32), nmaxT[:, :].bitcast(F32))\
                  .then_inc(nmax_in[g % 2], 16)

            def parts(b, par, first=0, last=G):
                rows, its = slice(first * R * HD, last * R * HD), slice(first * R, last * R)
                for i, (what, to, order) in enumerate((("q", q_dram[par], (qk_hi, qk_hi, qk_lo)),
                                                       ("k", k_dram[par], (qk_lo, qk_hi, qk_hi)))):
                    sp.wait_ge(at[what], b + 1)
                    alone(sp)
                    for x in range(3):
                        sp.dma_start(to[its, HD * x:HD * (x + 1), :], order[x][rows, i, :].bitcast(F32)).then_inc(qk_out, 16)

            def round_(t, par, half):
                if exists(t + 2, BATCH) and (not isinstance(t, int) or t >= 0):
                    sp_pick(sp, 0, t + 2, par)
                for g in range(G):
                    b, of = (t, g + 3) if g == 0 else (t + 1, g - 1)
                    if exists(b, BATCH):
                        stack(b, par if g == 0 else 1 - par, of)
                        if isinstance(t, int) and t == -1 and g == 1:
                            parts(0, 0, 1, G)
                    b, of = (t, g + 1) if g + 1 < G else (t + 1, 0)
                    if exists(b, BATCH):
                        maxima(b, of)
                if exists(t + 2, BATCH):
                    parts(t + 2, par, 0, 1 if isinstance(t, int) and t == -2 else G)

            for b in range(2):
                sp_pick(sp, 0, b, b)
            sp.wait_ge(at["init"], G + 2)
            for r in range(R):
                row = MAX_ROW + 2 * r
                sp.dma_start(k_st[row:row + 2, :, r, :].bitcast(F32), probs[0:2 * G, 4, :])\
                  .then_inc(stack_const, 16)
            steps(sp, FIRST_ROUND, ROUNDS, LOOP[0], LOOP[1], round_)

        @block.sync
        def _(sp):
            first = QT * P
            sp.dma_start(X[:, 0:QT, :], x_rows[0:first, :].rearrange("(t p) d -> p t d", p=P)).then_inc(x_first, 16)
            sp.dma_start(wg[:, :], Wg).then_inc(wg_in, 16)
            sp.dma_start(X[:, QT:NT, :], x_rows[first:T, :].rearrange("(t p) d -> p t d", p=P)).then_inc(x_loaded, 16)
            column = lambda v: v.rearrange("(p o) -> p o", o=1)
            loads = [(ws1_raw, Ws1), (ws2_raw, Ws2.rearrange("(p c) d -> p (c d)", c=FC)),
                     (bs1_col[:, :], bs1.rearrange("(p c) -> p c", c=FC)), (bs2_col[:, :], column(bs2)),
                     (b1_col[:, :].rearrange("p (e c) -> p e c", c=FC), b1.rearrange("e (p c) -> p e c", c=FC)),
                     (b2_col[:, :], b2.rearrange("e d -> d e")),
                     (wq[:, :], Wq), (wk[:, :], Wk), (wv[:, :], Wv), (wo[:, :], Wo),
                     (bq_col[:, :], column(bq)), (bk_col[:, :], column(bk)), (bv_col[:, :], column(bv)),
                     (bo_rows[:, :], bo.unsqueeze(0).to_broadcast([P, D]))]
            assert len(loads) == LOADS
            for to, of in loads:
                sp.dma_start(to, of, allow_slow_non_contiguous=True).then_inc(const_in, 16)
            sp.wait_ge(dve_const, 1)
            sp.dma_start(zero_dram, probs[MAX_ROW:P, 0, :]).then_inc(pads_in, 16)
            sp.wait_ge(pool_const, POOL_CONSTS)
            sp.dma_start(xs[PAD:ROWS, :].rearrange("(b p s) d -> p b (s d)", b=PAD_BLOCKS, p=P),
                         no_tokens[:, :, :].rearrange("p s d -> p (s d)").unsqueeze(1).to_broadcast([P, PAD_BLOCKS, SUB * W]))\
              .then_inc(pads_in, 16)
            sp.wait_ge(pads_in, 32)
            sp_blocks(sp, ex[0], 0, NEX)
            sp_attention(sp)
            sp_blocks(sp, ex[1], 1, NEX)
            for b in range(2):
                sp_pick(sp, 1, b, b)
            for b in range(BATCH):
                if 1 <= b < BATCH - 1:
                    sp_pick(sp, 1, b + 1, (b + 1) % 2)
                sp.wait_ge(rt[1]["combined"], 2 * QT * (b + 1))
                sp.wait_ge(sh[1]["rows"], b + 1)
                sp.dma_start(out_rows[b * SEQ:(b + 1) * SEQ, :].rearrange("(t p) d -> p t d", p=P),
                             X[:, b * QT:(b + 1) * QT, :]).then_inc(out_done, 16)
            sp.wait_ge(out_done, 16 * BATCH)

        @block.gpsimd
        def _(pool):
            pool.memset(ident[:, :], 0.0).then_inc(pool_const, 1)
            pool.memset(ones_bf[:, :], 1.0).then_inc(pool_const, 1)
            pool.memset(neg_half[:, :], -0.5).then_inc(pool_const, 1)
            pool.iota(iota_e[:, :], [[1, E]], 0, 0, allow_small_or_imprecise_dtypes=True).then_inc(pool_const, 1)
            pool.iota(iota_b[:, :], [[1, NEX]], 0, 0, allow_small_or_imprecise_dtypes=True).then_inc(pool_const, 1)
            pool.iota(token_row[:, :], [[2 * P, NT]], 0, 2, allow_small_or_imprecise_dtypes=True).then_inc(pool_const, 1)
            pool.memset(no_tokens[:, :, 0:D], 0.0).then_inc(pool_const, 1)
            pool.memset(no_tokens[:, :, D + 1], -1.0).then_inc(pool_const, 1)
            pool.iota(no_tokens[:, :, D], [[1, SUB]], TOP * T, SUB, allow_small_or_imprecise_dtypes=True)\
                .then_inc(pool_const, 1)
            pool.wait_ge(pool_const, 9)
            pool.affine_select(out=ident[:, :], in_=ident[:, :], compare_op=ALU.not_equal, fill=1.0,
                               base=0, pattern=[[-1, P]], channel_multiplier=1).then_inc(pool_const, 1)
            pool.affine_select(out=before_bf[:, :], in_=ones_bf[:, :], compare_op=ALU.is_gt, fill=0.0,
                               base=0, pattern=[[1, P]], channel_multiplier=-1).then_inc(pool_const, 1)
            pool_route(pool)
            pool_blocks(pool, ex[0], NEX)
            pool_attention(pool)
            pool_blocks(pool, ex[1], NEX)
        @block.vector
        def _(dve):
            dve.memset(probs[:, 0, :], 0.0).then_inc(dve_const, 1)
            dve.memset(probs[:, 4, :], 1.0).then_inc(dve_const, 1)
            dve.memset(scan_one[:, :], 1.0).then_inc(dve_const, 1)
            dve.wait_ge(wg_in, 16)
            dve.tensor_copy(wg_hi[:, :], wg[:, :]).then_inc(wg_parts, 1)
            dve.wait_ge(pool_const, POOL_CONSTS)
            dve.tensor_scalar(region_start[:, :], iota_e[:, :], float(REGION), None, ALU.mult).then_inc(dve_const, 1)
            dve.wait_ge(wg_parts, 1)
            dve.tensor_tensor(wg_lo[:, :], wg[:, :], wg_hi[:, :].bitcast(F32), ALU.subtract).then_inc(wg_parts, 1)
            dve.wait_ge(dve_const, 4)
            dve.tensor_copy(next_row[:, :], region_start[:, :]).then_inc(dve_const, 1)
            dve.wait_ge(dve_const, 5)
            dve_blocks(dve, sh[0], NSH, False, dve_route(dve))
            dve_blocks(dve, ex[0], NEX, True)
            dve.tensor_copy(next_row[:, :], region_start[:, :]).then_inc(dve_const, 1)
            dve.wait_ge(dve_const, DVE_CONSTS + 1)
            dve_attention(dve)
            dve_blocks_of(dve, rt[1])
            dve_blocks(dve, sh[1], EARLY, False, dve_turned_again(dve, 0))
            dve_gates(dve, rt[1])
            dve.wait_ge(kept, NSH + 1)
            dve_blocks(dve, ex[1], NEX, True)
            dve_blocks(dve, sh[1], NSH, False, dve_turned_again(dve, EARLY), EARLY)

        @block.scalar
        def _(act):
            act.wait_ge(const_in, 16 * LOADS)
            act_blocks(act, sh[0], 0, NSH, False, act_route(act))
            act_gates(act, rt[0])
            act_blocks(act, ex[0], 0, NEX, True)
            act.wait_ge(dve_const, DVE_CONSTS)
            act.wait_ge(at["init"], G + 2)
            act_attention(act)
            act_blocks(act, sh[1], 1, EARLY, False, act_turned_again(act, 0))
            act_gates(act, rt[1])
            act_blocks(act, ex[1], 1, NEX, True)
            act_blocks(act, sh[1], 1, NSH, False, act_turned_again(act, EARLY), EARLY)

        @block.tensor
        def _(pe):
            pe.wait_ge(pool_const, POOL_CONSTS)
            pe.wait_ge(wg_parts, 2)
            pe_blocks(pe, sh[0], NSH, False, pe_route(pe))
            pe.wait_ge(rt[0]["counted"], NSH)
            pe_blocks(pe, ex[0], NEX, True)
            pe_attention(pe)
            pe.wait_ge(rt[1]["counted"], NSH)
            pe_blocks(pe, sh[1], EARLY, False, pe_turned(pe, 0))
            pe_blocks(pe, ex[1], NEX, True)
            pe_blocks(pe, sh[1], NSH, False, pe_turned(pe, EARLY), EARLY, ex[1])


LOADS = 14
POOL_CONSTS = 11
DVE_CONSTS = 10

_INS = ["L0_attn_x", "L0_attn_Wq", "L0_attn_bq", "L0_attn_Wk", "L0_attn_bk", "L0_attn_Wv", "L0_attn_bv",
        "L0_attn_Wo", "L0_attn_bo", "L0_ffn_Wg", "L0_ffn_W1", "L0_ffn_b1", "L0_ffn_W2", "L0_ffn_b2",
        "L0_ffn_Ws1", "L0_ffn_bs1", "L0_ffn_Ws2", "L0_ffn_bs2"]


def kernel(**inputs):
    import numpy as _np
    import concourse.bacc as _bacc
    from concourse import mybir as _mybir
    from concourse.bass_utils import run_bass_kernel_spmd as _run

    nc = _bacc.Bacc("TRN2", target_bir_lowering=False, num_devices=1)
    arrays, args = {}, []
    for name in _INS:
        a = _np.ascontiguousarray(inputs[name])
        arrays[f"in_{name}_dram"] = a
        args.append(nc.dram_tensor(f"in_{name}_dram", a.shape, _mybir.dt.from_np(a.dtype), kind="ExternalInput").ap())
    shape = inputs["L0_attn_x"].shape
    args.append(nc.dram_tensor("out_0_dram", shape, _mybir.dt.float32, kind="ExternalOutput").ap())
    macaron(nc, *args)
    r = _run(nc, [arrays], core_ids=[0])
    return r.results[0]["out_0_dram"]
```
